# Optimizing a Trainium2 kernel written in Bass

```python
import numpy as np
import jax
import jax.numpy as jnp

def _softmax(x, axis=-1):
    return jax.nn.softmax(x, axis=axis)

def _gelu(x):
    return jax.nn.gelu(x, approximate=True)

def _silu(x):
    return jax.nn.silu(x)

def _sigmoid(x):
    return jax.nn.sigmoid(x)

def _layernorm(x, axis=-1, eps=1e-05):
    m = jnp.mean(x, axis=axis, keepdims=True)
    v = jnp.var(x, axis=axis, keepdims=True)
    return (x - m) / jnp.sqrt(v + eps)

def _scatter_add(tgt, idx, src, axis=0):
    return tgt.at[idx].add(src)

def _segment_sum(src, seg, n):
    return jax.ops.segment_sum(src, seg, n)
kernel_name = 'mk_decoder_preln_d2_seqx_r8_8c312d'

def setup_inputs(seed: int=0):
    np.random.seed(seed)
    _w = jnp.asarray

    def _rec_inputs():
        import jax
        import jax.numpy as jnp
        _rk = jax.random.key(seed)
        x = -7.109e-05 + 0.9999 * jax.random.normal(jax.random.fold_in(_rk, 1), (4, 256, 256), jnp.float32)
        _lenS = 256 - jax.random.randint(jax.random.fold_in(_rk, 7), (4,), 0, max(1, 256 // 4) + 1, jnp.int32)
        _lenS2 = 256 - jax.random.randint(jax.random.fold_in(_rk, 8), (4,), 0, max(1, 256 // 4) + 1, jnp.int32)
        _ctx_512P = jax.random.normal(jax.random.fold_in(_rk, 11), (4, 16, 64), jnp.float32)
        _ctx_512c = jax.random.dirichlet(jax.random.fold_in(_rk, 511), 0.3 * jnp.ones((16,), jnp.float32), (4, 256))
        _ctx_512t = jnp.einsum('bsk,bkd->bsd', _ctx_512c, _ctx_512P)
        _ctx_512t = _ctx_512t * jax.lax.rsqrt(jnp.mean(jnp.square(_ctx_512t)) + 1e-12) * 0.953939
        ctx_512 = 2.81802e-05 + 1.00001 * (_ctx_512t + 0.3 * jax.random.normal(jax.random.fold_in(_rk, 611), (4, 256, 64), jnp.float32))
        return (x, ctx_512)
    x, ctx_512 = _rec_inputs()

    def _L0_attn_setup():
        import jax, jax.numpy as jnp
        import numpy as np
        SCALE_BASE = 64
        EPS = 1e-05

        def _xpos_terms(seq_len, d):
            half = d // 2
            xscale = (jnp.arange(0, d, 2, dtype=jnp.float32) + 0.4 * d) / (1.4 * d)
            pos = jnp.arange(seq_len, dtype=jnp.float32)
            scale = xscale[None, :] ** (pos[:, None] / SCALE_BASE)
            inv_freq = 1.0 / 10000.0 ** (jnp.arange(half, dtype=jnp.float32) / half)
            sinu = pos[:, None] * inv_freq[None, :]
            return (jnp.sin(sinu), jnp.cos(sinu), scale)

        def _dup(t):
            return jnp.repeat(t, 2, axis=-1)

        def _rot(x):
            x1 = x[..., ::2]
            x2 = x[..., 1::2]
            return jnp.stack((-x2, x1), axis=-1).reshape(x.shape)

        def _apply_xpos(x, sin, cos, scale):
            c = _dup(cos * scale)
            s = _dup(sin * scale)
            return x * c + _rot(x) * s
        key = jax.random.key(seed)
        ks = jax.random.split(key, 6)
        B, S, H, nheads = (2, 128, 256, 16)
        d = H // nheads
        X = jax.random.normal(ks[0], (B, S, H), dtype=jnp.float32)
        W_Q = jax.random.normal(ks[1], (nheads, H, d), dtype=jnp.float32) / H
        W_K = jax.random.normal(ks[2], (nheads, H, d), dtype=jnp.float32) / H
        W_V = jax.random.normal(ks[3], (nheads, H, d), dtype=jnp.float32) / H
        W_G = jax.random.normal(ks[4], (H, H), dtype=jnp.float32) / H
        W_O = jax.random.normal(ks[5], (H, H), dtype=jnp.float32) / H
        gn_weight = jnp.ones((H,), dtype=jnp.float32)
        gn_bias = jnp.zeros((H,), dtype=jnp.float32)
        return {'X': X, 'W_Q': W_Q, 'W_K': W_K, 'W_V': W_V, 'W_G': W_G, 'W_O': W_O, 'gn_weight': gn_weight, 'gn_bias': gn_bias}
    _L0_attn_all = _L0_attn_setup()
    _L0_attn_in = {k: v for k, v in _L0_attn_all.items() if k in ('W_Q', 'W_K', 'W_V', 'W_G', 'W_O', 'gn_weight', 'gn_bias')}
    del _L0_attn_all

    def _L0_xattn_setup():
        import jax, jax.numpy as jnp
        import numpy as np
        EPS = 1e-06
        IMAGE_DIMS = 256
        key = jax.random.key(seed)
        k1, k2, k3 = jax.random.split(key, 3)
        B, I, J, D = (16, 256, 256, 64)
        p = jax.random.normal(k1, (B, I, J), dtype=jnp.float32)
        k_v = jax.random.normal(k2, (B, J, D), dtype=jnp.float32)
        W_k = jax.random.normal(k3, (D, D), dtype=jnp.float32) * (1.0 / np.sqrt(D))
        b_k = jnp.zeros((D,), dtype=jnp.float32)
        ln_gamma = jnp.ones((J,), dtype=jnp.float32)
        ln_beta = jnp.zeros((J,), dtype=jnp.float32)
        return {'p': p, 'k_v': k_v, 'W_k': W_k, 'b_k': b_k, 'ln_gamma': ln_gamma, 'ln_beta': ln_beta}
    _L0_xattn_all = _L0_xattn_setup()
    _L0_xattn_in = {k: v for k, v in _L0_xattn_all.items() if k in ('W_k', 'b_k', 'ln_gamma', 'ln_beta')}
    del _L0_xattn_all

    def _L0_ffn_setup():
        import jax, jax.numpy as jnp
        import numpy as np
        GOLDEN_CENTER = 1.0 / np.e
        GOLDEN_LOWER = 0.5 - np.log(4.0 / 3.0)
        GOLDEN_UPPER = 0.5

        def _golden_weights(x, Wr, temperature):
            inh = jax.nn.sigmoid(x @ Wr / temperature)
            in_zone = (inh >= GOLDEN_LOWER) & (inh <= GOLDEN_UPPER)
            distance = jnp.abs(inh - GOLDEN_CENTER)
            weights = jnp.exp(-distance / 0.1) * in_zone.astype(x.dtype)
            wsum = jnp.sum(weights, axis=-1, keepdims=True)
            no_expert = wsum < 1e-08
            fb = jnp.exp(-distance / 0.3)
            _, top2 = jax.lax.top_k(fb, 2)
            fb_mask = jnp.sum(jax.nn.one_hot(top2, weights.shape[-1], dtype=x.dtype), axis=-2)
            fb_w = fb * fb_mask
            fb_w = fb_w / jnp.maximum(jnp.sum(fb_w, axis=-1, keepdims=True), 1e-08)
            weights = jnp.where(no_expert, fb_w, weights)
            weights = weights / jnp.maximum(jnp.sum(weights, axis=-1, keepdims=True), 1e-08)
            return weights
        key = jax.random.key(seed)
        ks = jax.random.split(key, 5)
        B, T, D, E, F = (2, 256, 256, 8, 256)
        s_in = 1.0 / np.sqrt(D)
        s_f = 1.0 / np.sqrt(F)
        return {'x': jax.random.normal(ks[0], (B, T, D), dtype=jnp.float32), 'Wg': jax.random.normal(ks[1], (E, D, F), dtype=jnp.float32) * s_in, 'Wu': jax.random.normal(ks[2], (E, D, F), dtype=jnp.float32) * s_in, 'Wd': jax.random.normal(ks[3], (E, F, D), dtype=jnp.float32) * s_f, 'Wr': jax.random.normal(ks[4], (D, E), dtype=jnp.float32) * s_in, 'temperature': jnp.ones((1,), dtype=jnp.float32)}
    _L0_ffn_all = _L0_ffn_setup()
    _L0_ffn_in = {k: v for k, v in _L0_ffn_all.items() if k in ('Wg', 'Wu', 'Wd', 'Wr', 'temperature')}
    del _L0_ffn_all

    def _L1_attn_setup():
        import jax, jax.numpy as jnp
        import numpy as np
        NH = 16
        D = 128
        C = 64
        EPS = 1e-12

        def _l2norm(x):
            n = jnp.linalg.norm(x, axis=-1, keepdims=True)
            return x / jnp.maximum(n, EPS)
        key = jax.random.key(seed)
        ks = jax.random.split(key, 12)
        B, L, H = (4, 512, 256)
        std = 0.02
        f32 = jnp.float32
        inp = {'hidden_states': jax.random.normal(ks[0], (B, L, H), f32), 'q_w': jax.random.normal(ks[1], (NH * D, H), f32) * std, 'q_b': jnp.zeros((NH * D,), f32), 'k_w': jax.random.normal(ks[2], (NH * D, H), f32) * std, 'k_b': jnp.zeros((NH * D,), f32), 'v_w': jax.random.normal(ks[3], (NH * D, H), f32) * std, 'v_b': jnp.zeros((NH * D,), f32), 'a_w': jax.random.normal(ks[4], (NH, H), f32) * std, 'a_b': jnp.zeros((NH,), f32), 'b_w': jax.random.normal(ks[5], (NH, H), f32) * std, 'b_b': jnp.zeros((NH,), f32), 'og_w': jax.random.normal(ks[6], (NH * D, H), f32) * std, 'o_w': jax.random.normal(ks[7], (H, NH * D), f32) * std, 'o_b': jnp.zeros((H,), f32)}
        return inp
    _L1_attn_all = _L1_attn_setup()
    _L1_attn_in = {k: v for k, v in _L1_attn_all.items() if k in ('q_w', 'q_b', 'k_w', 'k_b', 'v_w', 'v_b', 'a_w', 'a_b', 'b_w', 'b_b', 'og_w', 'o_w', 'o_b')}
    del _L1_attn_all

    def _L1_xattn_setup():
        import jax, jax.numpy as jnp
        import numpy as np
        import math
        NUM_Q_HEADS = 32
        NUM_KV_HEADS = 8
        key = jax.random.key(seed)
        k1, k2, k3 = jax.random.split(key, 3)
        B, S, E = (2, 256, 256)
        kv_E = NUM_KV_HEADS * (E // NUM_Q_HEADS)
        q = jax.random.normal(k1, (B, S, E), dtype=jnp.float32)
        k = jax.random.normal(k2, (B, S, kv_E), dtype=jnp.float32)
        v = jax.random.normal(k3, (B, S, kv_E), dtype=jnp.float32)
        return {'q': q, 'k': k, 'v': v}
    _L1_xattn_all = _L1_xattn_setup()
    _L1_xattn_in = {k: v for k, v in _L1_xattn_all.items() if k in ()}
    del _L1_xattn_all

    def _L1_ffn_setup():
        import jax, jax.numpy as jnp
        import numpy as np
        BLOCK_SIZE = 32
        HIDDEN_SIZE = 256
        MLP_DIM = 2048
        NVFP4_LUT = jnp.array([0.0, 0.5, 1.0, 1.5, 2.0, 3.0, 4.0, 6.0, 0.0, -0.5, -1.0, -1.5, -2.0, -3.0, -4.0, -6.0], dtype=jnp.float32)

        def dequant_nvfp4(W_packed, scales, block=BLOCK_SIZE):
            N = W_packed.shape[0]
            low = W_packed & 15
            high = W_packed >> 4 & 15
            idx = jnp.stack([low, high], axis=-1).reshape(N, -1)
            vals = NVFP4_LUT[idx]
            K = vals.shape[1]
            vals = vals.reshape(N, K // block, block) * scales[:, :, None]
            return vals.reshape(N, K)
        key = jax.random.key(seed)
        ks = jax.random.split(key, 7)
        x = jax.random.normal(ks[0], (4, 32, HIDDEN_SIZE), dtype=jnp.float32)
        gate_W_packed = jax.random.randint(ks[1], (MLP_DIM, HIDDEN_SIZE // 2), 0, 32, dtype=jnp.int32)
        gate_scales = jax.random.uniform(ks[2], (MLP_DIM, HIDDEN_SIZE // BLOCK_SIZE), dtype=jnp.float32) * 0.1 + 0.001
        up_W_packed = jax.random.randint(ks[3], (MLP_DIM, HIDDEN_SIZE // 2), 0, 32, dtype=jnp.int32)
        up_scales = jax.random.uniform(ks[4], (MLP_DIM, HIDDEN_SIZE // BLOCK_SIZE), dtype=jnp.float32) * 0.1 + 0.001
        down_W_packed = jax.random.randint(ks[5], (HIDDEN_SIZE, MLP_DIM // 2), 0, 32, dtype=jnp.int32)
        down_scales = jax.random.uniform(ks[6], (HIDDEN_SIZE, MLP_DIM // BLOCK_SIZE), dtype=jnp.float32) * 0.1 + 0.001
        return {'x': x, 'gate_W_packed': gate_W_packed, 'gate_scales': gate_scales, 'up_W_packed': up_W_packed, 'up_scales': up_scales, 'down_W_packed': down_W_packed, 'down_scales': down_scales}
    _L1_ffn_all = _L1_ffn_setup()
    _L1_ffn_in = {k: v for k, v in _L1_ffn_all.items() if k in ('gate_W_packed', 'gate_scales', 'up_W_packed', 'up_scales', 'down_W_packed', 'down_scales')}
    del _L1_ffn_all
    return {'x': x, 'ctx_512': ctx_512, 'L0_attn_W_Q': _L0_attn_in['W_Q'], 'L0_attn_W_K': _L0_attn_in['W_K'], 'L0_attn_W_V': _L0_attn_in['W_V'], 'L0_attn_W_G': _L0_attn_in['W_G'], 'L0_attn_W_O': _L0_attn_in['W_O'], 'L0_attn_gn_weight': _L0_attn_in['gn_weight'], 'L0_attn_gn_bias': _L0_attn_in['gn_bias'], 'L0_xattn_W_k': _L0_xattn_in['W_k'], 'L0_xattn_b_k': _L0_xattn_in['b_k'], 'L0_xattn_ln_gamma': _L0_xattn_in['ln_gamma'], 'L0_xattn_ln_beta': _L0_xattn_in['ln_beta'], 'L0_ffn_Wg': _L0_ffn_in['Wg'], 'L0_ffn_Wu': _L0_ffn_in['Wu'], 'L0_ffn_Wd': _L0_ffn_in['Wd'], 'L0_ffn_Wr': _L0_ffn_in['Wr'], 'L0_ffn_temperature': _L0_ffn_in['temperature'], 'L1_attn_q_w': _L1_attn_in['q_w'], 'L1_attn_q_b': _L1_attn_in['q_b'], 'L1_attn_k_w': _L1_attn_in['k_w'], 'L1_attn_k_b': _L1_attn_in['k_b'], 'L1_attn_v_w': _L1_attn_in['v_w'], 'L1_attn_v_b': _L1_attn_in['v_b'], 'L1_attn_a_w': _L1_attn_in['a_w'], 'L1_attn_a_b': _L1_attn_in['a_b'], 'L1_attn_b_w': _L1_attn_in['b_w'], 'L1_attn_b_b': _L1_attn_in['b_b'], 'L1_attn_og_w': _L1_attn_in['og_w'], 'L1_attn_o_w': _L1_attn_in['o_w'], 'L1_attn_o_b': _L1_attn_in['o_b'], 'L1_ffn_gate_W_packed': _L1_ffn_in['gate_W_packed'], 'L1_ffn_gate_scales': _L1_ffn_in['gate_scales'], 'L1_ffn_up_W_packed': _L1_ffn_in['up_W_packed'], 'L1_ffn_up_scales': _L1_ffn_in['up_scales'], 'L1_ffn_down_W_packed': _L1_ffn_in['down_W_packed'], 'L1_ffn_down_scales': _L1_ffn_in['down_scales']}

def reference(x, ctx_512, L0_attn_W_Q, L0_attn_W_K, L0_attn_W_V, L0_attn_W_G, L0_attn_W_O, L0_attn_gn_weight, L0_attn_gn_bias, L0_xattn_W_k, L0_xattn_b_k, L0_xattn_ln_gamma, L0_xattn_ln_beta, L0_ffn_Wg, L0_ffn_Wu, L0_ffn_Wd, L0_ffn_Wr, L0_ffn_temperature, L1_attn_q_w, L1_attn_q_b, L1_attn_k_w, L1_attn_k_b, L1_attn_v_w, L1_attn_v_b, L1_attn_a_w, L1_attn_a_b, L1_attn_b_w, L1_attn_b_b, L1_attn_og_w, L1_attn_o_w, L1_attn_o_b, L1_ffn_gate_W_packed, L1_ffn_gate_scales, L1_ffn_up_W_packed, L1_ffn_up_scales, L1_ffn_down_W_packed, L1_ffn_down_scales):
    import jax
    import jax.numpy as jnp

    def _L0_attn_ref(X, W_Q, W_K, W_V, W_G, W_O, gn_weight, gn_bias):
        import jax, jax.numpy as jnp
        import numpy as np
        SCALE_BASE = 64
        EPS = 1e-05

        def _xpos_terms(seq_len, d):
            half = d // 2
            xscale = (jnp.arange(0, d, 2, dtype=jnp.float32) + 0.4 * d) / (1.4 * d)
            pos = jnp.arange(seq_len, dtype=jnp.float32)
            scale = xscale[None, :] ** (pos[:, None] / SCALE_BASE)
            inv_freq = 1.0 / 10000.0 ** (jnp.arange(half, dtype=jnp.float32) / half)
            sinu = pos[:, None] * inv_freq[None, :]
            return (jnp.sin(sinu), jnp.cos(sinu), scale)

        def _dup(t):
            return jnp.repeat(t, 2, axis=-1)

        def _rot(x):
            x1 = x[..., ::2]
            x2 = x[..., 1::2]
            return jnp.stack((-x2, x1), axis=-1).reshape(x.shape)

        def _apply_xpos(x, sin, cos, scale):
            c = _dup(cos * scale)
            s = _dup(sin * scale)
            return x * c + _rot(x) * s
        B, S, H = X.shape
        nheads, _, d = W_Q.shape
        gammas = 1.0 - jnp.exp(jnp.linspace(np.log(1.0 / 32), np.log(1.0 / 64), nheads)).astype(jnp.float32)
        sin, cos, scale = _xpos_terms(S, d)
        Q = jnp.einsum('bsh,nhd->bnsd', X, W_Q)
        K = jnp.einsum('bsh,nhd->bnsd', X, W_K)
        V = jnp.einsum('bsh,nhd->bnsd', X, W_V)
        Q = _apply_xpos(Q, sin, cos, scale)
        K = _apply_xpos(K, sin, cos, 1.0 / scale)
        n = jnp.arange(S)[:, None]
        m = jnp.arange(S)[None, :]
        D = jnp.where(n >= m, gammas[:, None, None] ** (n - m).astype(jnp.float32), 0.0)
        ret = jnp.einsum('bnsd,bntd->bnst', Q, K) * D[None]
        Y = jnp.einsum('bnst,bntv->bnsv', ret, V)
        Y = jnp.transpose(Y, (0, 2, 1, 3)).reshape(B, S, nheads * d)
        Yg = Y.reshape(B, S, nheads, d)
        mu = Yg.mean(-1, keepdims=True)
        var = Yg.var(-1, keepdims=True)
        Yn = ((Yg - mu) / jnp.sqrt(var + EPS)).reshape(B, S, nheads * d)
        Yn = Yn * gn_weight + gn_bias
        G = X @ W_G
        gate = G * jax.nn.sigmoid(G)
        return gate * Yn @ W_O

    def _L0_xattn_ref(p, k_v, W_k, b_k, ln_gamma, ln_beta):
        import jax, jax.numpy as jnp
        import numpy as np
        EPS = 1e-06
        IMAGE_DIMS = 256
        kv = k_v @ W_k.T + b_k
        out = jnp.einsum('bij,bjd->bid', p, kv)
        scale = IMAGE_DIMS ** (-0.5)
        sim = jnp.einsum('bid,bjd->bij', out, kv) * scale
        mu = jnp.mean(sim, axis=-1, keepdims=True)
        var = jnp.var(sim, axis=-1, keepdims=True)
        sim = (sim - mu) * jax.lax.rsqrt(var + EPS) * ln_gamma + ln_beta
        attn = jax.nn.softmax(sim, axis=-1)
        return attn

    def _L0_ffn_ref(x, Wg, Wu, Wd, Wr, temperature):
        import jax, jax.numpy as jnp
        import numpy as np
        GOLDEN_CENTER = 1.0 / np.e
        GOLDEN_LOWER = 0.5 - np.log(4.0 / 3.0)
        GOLDEN_UPPER = 0.5

        def _golden_weights(x, Wr, temperature):
            inh = jax.nn.sigmoid(x @ Wr / temperature)
            in_zone = (inh >= GOLDEN_LOWER) & (inh <= GOLDEN_UPPER)
            distance = jnp.abs(inh - GOLDEN_CENTER)
            weights = jnp.exp(-distance / 0.1) * in_zone.astype(x.dtype)
            wsum = jnp.sum(weights, axis=-1, keepdims=True)
            no_expert = wsum < 1e-08
            fb = jnp.exp(-distance / 0.3)
            _, top2 = jax.lax.top_k(fb, 2)
            fb_mask = jnp.sum(jax.nn.one_hot(top2, weights.shape[-1], dtype=x.dtype), axis=-2)
            fb_w = fb * fb_mask
            fb_w = fb_w / jnp.maximum(jnp.sum(fb_w, axis=-1, keepdims=True), 1e-08)
            weights = jnp.where(no_expert, fb_w, weights)
            weights = weights / jnp.maximum(jnp.sum(weights, axis=-1, keepdims=True), 1e-08)
            return weights
        weights = _golden_weights(x, Wr, temperature)
        gate = jnp.einsum('btd,edf->betf', x, Wg)
        up = jnp.einsum('btd,edf->betf', x, Wu)
        h = jax.nn.silu(gate) * up
        e_out = jnp.einsum('betf,efd->betd', h, Wd)
        out = jnp.einsum('bte,betd->btd', weights, e_out)
        return out

    def _L1_attn_ref(hidden_states, q_w, q_b, k_w, k_b, v_w, v_b, a_w, a_b, b_w, b_b, og_w, o_w, o_b):
        import jax, jax.numpy as jnp
        import numpy as np
        NH = 16
        D = 128
        C = 64
        EPS = 1e-12

        def _l2norm(x):
            n = jnp.linalg.norm(x, axis=-1, keepdims=True)
            return x / jnp.maximum(n, EPS)
        B, L, H = hidden_states.shape
        nh, d, c = (NH, D, C)
        hs = hidden_states
        q = (hs @ q_w.T + q_b).reshape(B, L, nh, d)
        k = (hs @ k_w.T + k_b).reshape(B, L, nh, d)
        v = (hs @ v_w.T + v_b).reshape(B, L, nh, d)
        beta = jax.nn.softplus(hs @ b_w.T + b_b)
        scale = float(d) ** 0.5
        qn = _l2norm(q / scale)
        kn = _l2norm(k / scale)
        gv = beta[..., None] * v
        nchunks = L // c

        def to_chunks(x):
            return x.reshape(B, nchunks, c, nh, d).transpose(0, 1, 3, 2, 4)
        qc, kc, gvc = (to_chunks(qn), to_chunks(kn), to_chunks(gv))
        attn = jnp.einsum('bnhid,bnhjd->bnhij', qc, kc)
        pos = jnp.arange(c, dtype=jnp.float32)
        dist = jnp.clip(pos[None, :] - pos[:, None], 0.0, None)
        decay = jnp.exp(-0.1 * dist)
        causal = pos[None, :] <= pos[:, None]
        mask = jnp.where(causal, decay, 0.0)
        out = jnp.einsum('bnhij,bnhjd->bnhid', attn * mask, gvc)
        out = out.transpose(0, 1, 3, 2, 4).reshape(B, L, nh * d)
        gate = jax.nn.silu(hs @ og_w.T)
        out = out * gate
        return out @ o_w.T + o_b

    def _L1_xattn_ref(q, k, v):
        import jax, jax.numpy as jnp
        import numpy as np
        import math
        NUM_Q_HEADS = 32
        NUM_KV_HEADS = 8
        B, S, E = q.shape
        H, KV = (NUM_Q_HEADS, NUM_KV_HEADS)
        D = E // H
        G = H // KV
        scale = math.sqrt(D)
        qh = q.reshape(B, S, KV, G, D).transpose(0, 2, 3, 1, 4)
        kh = k.reshape(B, S, KV, D).transpose(0, 2, 1, 3)
        vh = v.reshape(B, S, KV, D).transpose(0, 2, 1, 3)
        scores = jnp.einsum('bkgsd,bktd->bkgst', qh, kh) / scale
        weights = jax.nn.softmax(scores, axis=-1)
        out = jnp.einsum('bkgst,bktd->bkgsd', weights, vh)
        return out.transpose(0, 3, 1, 2, 4).reshape(B, S, E)

    def _L1_ffn_ref(x, gate_W_packed, gate_scales, up_W_packed, up_scales, down_W_packed, down_scales):
        import jax, jax.numpy as jnp
        import numpy as np
        BLOCK_SIZE = 32
        HIDDEN_SIZE = 256
        MLP_DIM = 2048
        NVFP4_LUT = jnp.array([0.0, 0.5, 1.0, 1.5, 2.0, 3.0, 4.0, 6.0, 0.0, -0.5, -1.0, -1.5, -2.0, -3.0, -4.0, -6.0], dtype=jnp.float32)

        def dequant_nvfp4(W_packed, scales, block=BLOCK_SIZE):
            N = W_packed.shape[0]
            low = W_packed & 15
            high = W_packed >> 4 & 15
            idx = jnp.stack([low, high], axis=-1).reshape(N, -1)
            vals = NVFP4_LUT[idx]
            K = vals.shape[1]
            vals = vals.reshape(N, K // block, block) * scales[:, :, None]
            return vals.reshape(N, K)
        B, S, H = x.shape
        xt = x.reshape(B * S, H)
        Wg = dequant_nvfp4(gate_W_packed, gate_scales)
        Wu = dequant_nvfp4(up_W_packed, up_scales)
        Wd = dequant_nvfp4(down_W_packed, down_scales)
        gate = jnp.einsum('th,nh->tn', xt, Wg)
        up = jnp.einsum('th,nh->tn', xt, Wu)
        gelu = jnp.tanh(0.7978845608028654 * (gate + 0.044715 * gate ** 3)) * gate * 0.5 + gate * 0.5
        inter = gelu * up
        out = jnp.einsum('tn,hn->th', inter, Wd)
        return out.reshape(B, S, H)
    x = x + _L0_attn_ref(_layernorm(x, axis=-1), L0_attn_W_Q, L0_attn_W_K, L0_attn_W_V, L0_attn_W_G, L0_attn_W_O, L0_attn_gn_weight, L0_attn_gn_bias)
    x = x + _L0_xattn_ref(_layernorm(x, axis=-1), ctx_512, L0_xattn_W_k, L0_xattn_b_k, L0_xattn_ln_gamma, L0_xattn_ln_beta)
    x = x + _L0_ffn_ref(_layernorm(x, axis=-1), L0_ffn_Wg, L0_ffn_Wu, L0_ffn_Wd, L0_ffn_Wr, L0_ffn_temperature)
    x = x + _L1_attn_ref(_layernorm(x, axis=-1), L1_attn_q_w, L1_attn_q_b, L1_attn_k_w, L1_attn_k_b, L1_attn_v_w, L1_attn_v_b, L1_attn_a_w, L1_attn_a_b, L1_attn_b_w, L1_attn_b_b, L1_attn_og_w, L1_attn_o_w, L1_attn_o_b)
    x = x + _L1_xattn_ref(_layernorm(x, axis=-1), ctx_512, ctx_512)
    x = x + _L1_ffn_ref(_layernorm(x, axis=-1), L1_ffn_gate_W_packed, L1_ffn_gate_scales, L1_ffn_up_W_packed, L1_ffn_up_scales, L1_ffn_down_W_packed, L1_ffn_down_scales)
    return x

_drawn_inputs = setup_inputs


def setup_inputs(seed=0):
    import zlib

    import numpy as np

    out = dict(_drawn_inputs(seed))
    spreads = {'L0_attn_gn_weight': (1.0, 0.6),
     'L0_attn_gn_bias': (0.0, 0.8),
     'L0_xattn_b_k': (0.0, 0.8),
     'L0_xattn_ln_gamma': (1.0, 0.6),
     'L0_xattn_ln_beta': (0.0, 0.8),
     'L1_attn_q_b': (0.0, 0.8),
     'L1_attn_k_b': (0.0, 0.538),
     'L1_attn_v_b': (0.0, 0.545),
     'L1_attn_a_b': (0.0, 0.1),
     'L1_attn_b_b': (0.0, 0.8),
     'L1_attn_o_b': (0.0, 0.1)}
    factors = {'L0_attn_W_Q': 6.68,
     'L0_attn_W_K': 7.067,
     'L0_attn_W_V': 6.901,
     'L0_attn_W_G': 5.424,
     'L0_attn_W_O': 5.35,
     'L0_xattn_W_k': 3.123,
     'L1_attn_b_w': 8.0}
    for name, (base, spread) in spreads.items():
        noise = np.random.default_rng([zlib.crc32(name.encode()), seed]).standard_normal(out[name].shape)
        drawn = base * np.exp(spread * noise) if base else spread * noise
        out[name] = jnp.asarray(drawn.astype(out[name].dtype))
    for name, factor in factors.items():
        out[name] = (out[name] * factor).astype(out[name].dtype)
    return out
```

```python
from contextlib import ExitStack

import numpy as np

import concourse.bass as bass
from concourse import mybir

ALU = mybir.AluOpType
ACT = mybir.ActivationFunctionType
AX = mybir.AxisListType
F32 = mybir.dt.float32
BF16 = mybir.dt.bfloat16
I16 = mybir.dt.int16
I32 = mybir.dt.int32

P = 128
B, S, H = 4, 256, 256
T = B * S
NT = T // P
KT = H // P
HALF = T // 2
NH0, HD0 = 16, 16
E0 = 8
NH1, HD1 = 16, 128
CHUNK = 64
KVH, GRP, HD2 = 8, 4, 8
CD = 64
MLP = 2048
NB = MLP // P
LN_EPS = 1e-5

KB = 256


def build_decoder(nc, ins, out):
    with ExitStack() as ctx:
        def sb(name, shape, dt=F32):
            return ctx.enter_context(nc.sbuf_tensor(name, shape, dt))

        sem_names = set()

        def sem(name):
            assert name not in sem_names
            sem_names.add(name)
            return ctx.enter_context(nc.semaphore(name))

        PS = ctx.enter_context(nc.psum_tensor("PS", [P, 8, 512], F32))
        x = sb("x", [P, NT, H])
        hT = sb("hT", [P, KT, T])
        consts = sb("consts", [P, 1152])
        ident = consts[:, 0:128]
        ones = consts[:, 128:256]
        mask_ret = consts[:, 256:640]
        mask_chunk = consts[:, 640:1152]
        eps_t = sb("eps_t", [P, 2])
        small = sb("small", [P, 1024])
        R0 = sb("R0", [P, 32 * KB])
        R1 = sb("R1", [P, 48 * KB])
        R2 = sb("R2", [P, 88 * KB])
        SC = sb("SC", [P, 8 * KB])

        def v3(ap, a, b):
            return ap.rearrange("p (a b) -> p a b", a=a, b=b)

        def v4(ap, a, b, c):
            return ap.rearrange("p (a b c) -> p a b c", a=a, b=b, c=c)

        wq32 = v4(R0[:, 0:1024], KT, 4, 128)
        wk32 = v4(R0[:, 1024:2048], KT, 4, 128)
        wkr32 = v4(R0[:, 2048:3072], KT, 4, 128)
        wvg = v3(R0[:, 3072:4096], KT, 512)
        wo0 = v3(R0[:, 4096:4608], KT, 256)
        rot_tab = v4(R0[:, 4608:7680], 3, 4, 256)
        gn_w = R0[:, 7680:7936]
        gn_b = R0[:, 7936:8192]
        wge = R1[:, 0:4096].rearrange("p (e k f) -> p e k f", e=E0, k=KT)
        wue = R1[:, 4096:8192].rearrange("p (e k f) -> p e k f", e=E0, k=KT)
        wde = R1[:, 8192:12288].rearrange("p (e k f) -> p e k f", e=E0, k=KT)
        qw1 = v3(R2[:, 0:4096], KT, 2048)
        kw1 = v3(R2[:, 4096:8192], KT, 2048)
        vw1 = v3(R2[:, 8192:12288], KT, 2048)
        gw1 = v3(R2[:, 12288:16384], KT, 2048)
        ow1 = v3(R2[:, 16384:20480], NB, 256)
        vb1 = R2[:, 20480:22528]
        pg = R1[:, 0:2048].bitcast(I16)
        pu = R1[:, 2048:4096].bitcast(I16)
        pd = R1[:, 4096:6144].bitcast(I16)
        sg1 = R1[:, 6144:8192]
        su1 = R1[:, 8192:10240]
        sd1 = R1[:, 10240:12288]
        wgm = v3(R2[:, 0:4096], 2, 2048)
        wum = v3(R2[:, 4096:8192], 2, 2048)
        wdm = R2[:, 8192:12288].rearrange("p (y j h) -> p y j h", y=2, j=8)

        s_vec = sem("s_vec")
        s_act = sem("s_act")
        s_pool = sem("s_pool")
        chain = {"v": 0, "a": 0, "p": 0}

        def link(eng, key, s, inst):
            chain[key] += 1
            inst.then_inc(s, 1)
            eng.wait_ge(s, chain[key])

        ld_x, ld_c, ld_a = sem("ld_x"), sem("ld_c"), sem("ld_a")
        ld_b, ld_moe = sem("ld_b"), sem("ld_moe")
        ld_d, ld_z, ld_f, eps_set = sem("ld_d"), sem("ld_z"), sem("ld_f"), sem("eps_set")
        z_clear = sem("z_clear")
        ctxT = SC[0:64, 0:1024]
        wkT = small[0:64, 0:64]
        bk_col = small[0:64, 64:65]
        bk_row = small[:, 128:192]
        xg_row = sb("xg_row", [P, 512])
        wr = small[:, 192:208].rearrange("p (k e) -> p k e", k=KT)
        temp = small[:, 208:209]
        qb1 = small[:, 224:240]
        kb1 = small[:, 240:256]
        bw1 = small[:, 256:288].rearrange("p (k e) -> p k e", k=KT)
        bb1 = small[:, 288:304]
        ob1 = small[:, 304:560]
        ctx_s = sb("ctx_s", [P, NT, CD])
        mv = sb("mv", [P, NT, 2])
        stats = sb("stats", [P, NT, 6])
        rstd = sb("rstd", [P, NT])
        rin = sb("rin", [P, NT])
        xn = sb("xn", [P, 2, 256])

        def bcast_row(a, n):
            return a.rearrange("(o n) -> o n", o=1).to_broadcast([P, n])

        N_A, N_B, N_MOE, N_D = 9, 7, 5, 11

        with nc.Block() as block:
            @block.sync
            def _(sp):
                sp.dma_start(x[:], ins["x"]).then_inc(ld_x, 16)
                sp.dma_start(consts[:], ins["consts"]).then_inc(ld_c, 16)
                sp.dma_start(wq32, ins["wq32"]).then_inc(ld_a, 16)
                sp.dma_start(wk32, ins["wk32"]).then_inc(ld_a, 16)
                sp.dma_start(wkr32, ins["wkr32"]).then_inc(ld_a, 16)
                sp.dma_start(rot_tab, ins["rot_tab"]).then_inc(ld_a, 16)
                sp.dma_start(wvg[:, :, 0:256], ins["wv0"]).then_inc(ld_a, 16)
                sp.dma_start(wvg[:, :, 256:512], ins["wg0"]).then_inc(ld_a, 16)
                sp.dma_start(wo0, ins["wo0"]).then_inc(ld_a, 16)
                sp.dma_start(gn_w, bcast_row(ins["gn_w"], 256)).then_inc(ld_a, 16)
                sp.dma_start(gn_b, bcast_row(ins["gn_b"], 256)).then_inc(ld_a, 16)
                sp.dma_start(ctxT, ins["ctxT"]).then_inc(ld_b, 16)
                sp.dma_start(wkT, ins["wkT"]).then_inc(ld_b, 16)
                sp.dma_start(bk_col, ins["bk"].rearrange("(n o) -> n o", o=1)).then_inc(ld_b, 16)
                sp.dma_start(bk_row, bcast_row(ins["bk"], 64)).then_inc(ld_b, 16)
                sp.dma_start(xg_row[:, 0:256], bcast_row(ins["xg"], 256)).then_inc(ld_b, 16)
                sp.dma_start(xg_row[:, 256:512], bcast_row(ins["xb"], 256)).then_inc(ld_b, 16)
                sp.dma_start(ctx_s[:], ins["ctx_s"]).then_inc(ld_b, 16)
                sp.dma_start(wr, ins["wr"]).then_inc(ld_moe, 16)
                sp.dma_start(temp, bcast_row(ins["temp"], 1)).then_inc(ld_moe, 16)
                sp.dma_start(wge, ins["wge"]).then_inc(ld_moe, 16)
                sp.dma_start(wue, ins["wue"]).then_inc(ld_moe, 16)
                sp.dma_start(wde, ins["wde"]).then_inc(ld_moe, 16)

            @block.vector
            def _(dve):
                nc.vector.memset(eps_t[:, 0:1], LN_EPS)
                nc.vector.memset(eps_t[:, 1:2], 1e-6).then_inc(eps_set, 1)

        def layer_norm(ph, parity=False):
            sd, xn_ready, tr_done, evac = (sem(f"{ph}_ln_{n}") for n in ("sd", "xn", "tr", "ev"))
            var_ready = sem(f"{ph}_ln_var")
            with nc.Block() as block:
                @block.vector
                def _(dve):
                    if ph == "A":
                        dve.wait_ge(ld_x, 16)
                    for i in range(NT):
                        nc.vector.bn_stats(stats[:, i, :], x[:, i, :]).then_inc(s_vec, 1)
                        chain["v"] += 1
                    dve.wait_ge(s_vec, chain["v"])
                    for i in range(NT):
                        last = nc.vector.bn_aggr(mv[:, i, :], stats[:, i, :])
                    last.then_inc(var_ready, 1)
                    dve.wait_ge(sd, 1)
                    link(dve, "v", s_vec, nc.vector.reciprocal(rstd[:], rin[:]))
                    for i in range(NT):
                        if i >= 2:
                            dve.wait_ge(tr_done, i - 1)
                        nc.vector.tensor_scalar(xn[:, i % 2, :], x[:, i, :], mv[:, i, 0:1], rstd[:, i:i + 1],
                                                ALU.subtract, ALU.mult).then_inc(xn_ready, 1)

                @block.scalar
                def _(act):
                    if ph == "A":
                        act.wait_ge(eps_set, 1)
                    act.wait_ge(var_ready, 1)
                    nc.scalar.activation(rin[:], mv[:, :, 1], ACT.Sqrt, bias=eps_t[:, 0:1]).then_inc(sd, 1)
                    for j in range(NT // 2):
                        act.wait_ge(tr_done, 2 * j + 2)
                        nc.scalar.copy(hT[:, :, j * 256:(j + 1) * 256], v3(PS[:, j, :], KT, 256)).then_inc(evac, 1)
                    act.wait_ge(evac, NT // 2)

                @block.tensor
                def _(pe):
                    if ph == "A":
                        pe.wait_ge(ld_c, 16)
                    for i in range(NT):
                        pe.wait_ge(xn_ready, i + 1)
                        for k in range(KT):
                            src = xn[:, i % 2, k::2] if parity else xn[:, i % 2, k * 128:(k + 1) * 128]
                            o = k * 256 + (i % 2) * 128
                            last = nc.tensor.transpose(PS[:, i // 2, o:o + 128], src, ident)
                        last.then_inc(tr_done, 1)

        layer_norm("A")
        q32 = v3(R2[:, 0:4096], 4, T)
        k32 = v3(R2[:, 4096:8192], 4, T)
        v0 = v3(R2[:, 8192:10240], NT, 256)
        sgate = v3(R2[:, 10240:12288], NT, 256)
        krt = v3(R2[:, 12288:13312], 2, 512)
        sT = v3(R2[:, 13312:13312 + 4 * 384], 4, 384)
        yc = R2[:, 15360:15872]
        ysq = R2[:, 15872:16384]
        z0 = v3(R2[:, 16384:16896], 2, 256)
        zT0 = v3(R2[:, 16896:17408], KT, 256)
        ysum = R2[:, 17408:17440]
        ymean = R2[:, 17440:17472]
        yvar = R2[:, 17472:17504]
        ysd = R2[:, 17504:17536]
        yrs = R2[:, 17536:17568]
        a_q, a_k, a_vg = sem("a_q"), sem("a_k"), sem("a_vg")
        a_qev, a_kev, a_vgev = sem("a_qev"), sem("a_kev"), sem("a_vgev")
        a_kpart = sem("a_kpart")
        a_s, a_sev, a_pv, a_yread = sem("a_s"), sem("a_sev"), sem("a_pv"), sem("a_yread")
        a_var, a_sd, a_z, a_zt, a_ztev, a_o, a_xadd = (sem(f"a_{n}") for n in ("var", "sd", "z", "zt", "ztev", "o", "xadd"))
        with nc.Block() as block:
            units = [(g, c) for g in range(4) for c in range(2)]

            @block.tensor
            def _(pe):
                pe.wait_ge(ld_a, 16 * N_A)
                for u, (g, c) in enumerate(units):
                    tok = slice(c * 512, (c + 1) * 512)
                    if u >= 2:
                        pe.wait_ge(a_qev, u - 1)
                    for k in range(KT):
                        last = nc.tensor.matmul(PS[:, u % 2, :], wq32[:, k, g, :], hT[:, k, tok], start=k == 0, stop=k == 1)
                    last.then_inc(a_q, 1)
                    if u >= 2:
                        pe.wait_ge(a_kpart, 2 * (u - 1))
                    for j, w in enumerate((wk32, wkr32)):
                        for k in range(KT):
                            last = nc.tensor.matmul(PS[:, 2 + 2 * j + u % 2, :], w[:, k, g, :], hT[:, k, tok],
                                                    start=k == 0, stop=k == 1)
                    last.then_inc(a_k, 1)
                    if u >= 2:
                        pe.wait_ge(a_vgev, 2 * (u - 1))
                    for k in range(KT):
                        last = nc.tensor.matmul(PS[:, 6 + u % 2, :], hT[:, k, u * 128:(u + 1) * 128], wvg[:, k, :],
                                                start=k == 0, stop=k == 1)
                    last.then_inc(a_vg, 1)
                pe.wait_ge(a_qev, 8)
                pe.wait_ge(a_kev, 8)
                pe.wait_ge(a_vgev, 16)

                def scores(b, n):
                    g, r = n // 4, n % 4
                    row = slice(32 * r, 32 * r + 32)
                    m = b * NH0 + n
                    if m >= 4:
                        pe.wait_ge(a_sev, m - 3)
                    nc.tensor.matmul(PS[:, r, 0:256], k32[row, g, b * 256:b * 256 + 128], q32[row, g, b * 256:b * 256 + 256],
                                     start=True, stop=True)
                    nc.tensor.matmul(PS[:, r, 256:384], k32[row, g, b * 256 + 128:b * 256 + 256],
                                     q32[row, g, b * 256 + 128:b * 256 + 256], start=True, stop=True).then_inc(a_s, 1)

                def mix(b, n):
                    m = b * NH0 + n
                    pe.wait_ge(a_sev, m + 1)
                    if n == 0 and b >= 2:
                        pe.wait_ge(a_yread, b - 1)
                    y = v3(PS[:, 4 + b % 2, :], 2, 256)
                    col = slice(16 * n, 16 * n + 16)
                    nc.tensor.matmul(y[:, 0, col], sT[:, n % 4, 0:128], v0[:, 2 * b, col], start=True, stop=True)
                    nc.tensor.matmul(y[:, 1, col], sT[:, n % 4, 128:256], v0[:, 2 * b, col], start=True, stop=False)
                    nc.tensor.matmul(y[:, 1, col], sT[:, n % 4, 256:384], v0[:, 2 * b + 1, col],
                                     start=False, stop=True).then_inc(a_pv, 1)

                def project(b):
                    pe.wait_ge(a_z, b + 1)
                    if b >= 1:
                        pe.wait_ge(a_ztev, b)
                    for i in range(2):
                        for k in range(KT):
                            last = nc.tensor.transpose(PS[:, 6, k * 256 + i * 128:k * 256 + i * 128 + 128],
                                                       z0[:, i, k * 128:(k + 1) * 128], ident)
                    last.then_inc(a_zt, 1)
                    pe.wait_ge(a_ztev, b + 1)
                    if b >= 1:
                        pe.wait_ge(a_xadd, b)
                    for i in range(2):
                        for k in range(KT):
                            last = nc.tensor.matmul(PS[:, 7, i * 256:(i + 1) * 256], zT0[:, k, i * 128:(i + 1) * 128],
                                                    wo0[:, k, :], start=k == 0, stop=k == 1)
                    last.then_inc(a_o, 1)

                LAG = 3
                total = B * NH0
                for m in range(total + LAG):
                    if m < total:
                        scores(m // NH0, m % NH0)
                    if m >= LAG:
                        mix((m - LAG) // NH0, (m - LAG) % NH0)
                    if m % NH0 == 12 and m > NH0:
                        project(m // NH0 - 1)
                project(B - 1)

            @block.scalar
            def _(act):
                for i in range(NT):
                    act.wait_ge(a_vg, i + 1)
                    nc.scalar.copy(v0[:, i, :], PS[:, 6 + i % 2, 0:256]).then_inc(a_vgev, 1)
                    nc.scalar.activation(sgate[:, i, :], PS[:, 6 + i % 2, 256:512], ACT.Silu).then_inc(a_vgev, 1)
                for b in range(B):
                    act.wait_ge(a_var, b + 1)
                    nc.scalar.activation(ysd, yvar, ACT.Sqrt, bias=eps_t[:, 0:1], scale=1.0 / HD0).then_inc(a_sd, 1)
                    act.wait_ge(a_zt, b + 1)
                    if b >= 1:
                        act.wait_ge(a_o, b)
                    nc.scalar.copy(zT0, v3(PS[:, 6, :], KT, 256)).then_inc(a_ztev, 1)

            @block.vector
            def _(dve):
                for u, (g, c) in enumerate(units):
                    tok = slice(c * 512, (c + 1) * 512)

                    def table(j):
                        return rot_tab[:, j, g:g + 1, :].to_broadcast([P, 2, 256])
                    dve.wait_ge(a_q, u + 1)
                    nc.vector.tensor_tensor(v3(q32[:, g, tok], 2, 256), v3(PS[:, u % 2, :], 2, 256), table(0),
                                            ALU.mult).then_inc(a_qev, 1)
                    dve.wait_ge(a_k, u + 1)
                    nc.vector.tensor_tensor(v3(k32[:, g, tok], 2, 256), v3(PS[:, 2 + u % 2, :], 2, 256), table(1),
                                            ALU.mult).then_inc(a_kpart, 1)
                    nc.vector.tensor_tensor(v3(krt[:, u % 2, :], 2, 256), v3(PS[:, 4 + u % 2, :], 2, 256), table(2),
                                            ALU.mult).then_inc(a_kpart, 1)
                    dve.wait_ge(a_kpart, 2 * (u + 1))
                    nc.vector.tensor_tensor(k32[:, g, tok], k32[:, g, tok], krt[:, u % 2, :], ALU.add).then_inc(a_kev, 1)

                def mask(m):
                    dve.wait_ge(a_s, m + 1)
                    if m >= 4:
                        dve.wait_ge(a_pv, m - 3)
                    nc.vector.tensor_tensor(sT[:, m % 4, :], PS[:, m % 4, 0:384], mask_ret, ALU.mult).then_inc(a_sev, 1)

                def norm(b):
                    y = PS[:, 4 + b % 2, :].rearrange("p (n d) -> p n d", d=HD0)
                    n3 = lambda ap: ap.rearrange("p (n d) -> p n d", d=HD0)
                    wide = lambda ap: ap.rearrange("p (n o) -> p n o", o=1).to_broadcast([P, 32, HD0])
                    both = lambda ap: ap.rearrange("p (o f) -> p o f", o=1).to_broadcast([P, 2, 256])
                    dve.wait_ge(a_pv, (b + 1) * NH0)
                    link(dve, "v", s_vec, nc.vector.tensor_reduce(ysum, y, AX.X, ALU.add))
                    link(dve, "v", s_vec, nc.vector.tensor_scalar(ymean, ysum, 1.0 / HD0, None, ALU.mult))
                    nc.vector.tensor_tensor(n3(yc), y, wide(ymean), ALU.subtract).then_inc(a_yread, 1)
                    dve.wait_ge(a_yread, b + 1)
                    link(dve, "v", s_vec, nc.vector.tensor_tensor(ysq, yc, yc, ALU.mult))
                    nc.vector.tensor_reduce(yvar, n3(ysq), AX.X, ALU.add).then_inc(a_var, 1)
                    dve.wait_ge(a_sd, b + 1)
                    link(dve, "v", s_vec, nc.vector.reciprocal(yrs, ysd))
                    link(dve, "v", s_vec, nc.vector.tensor_tensor(n3(yc), n3(yc), wide(yrs), ALU.mult))
                    link(dve, "v", s_vec, nc.vector.tensor_tensor(v3(yc, 2, 256), v3(yc, 2, 256), both(gn_w), ALU.mult))
                    link(dve, "v", s_vec, nc.vector.tensor_tensor(v3(yc, 2, 256), v3(yc, 2, 256), both(gn_b), ALU.add))
                    if b >= 1:
                        dve.wait_ge(a_zt, b)
                    nc.vector.tensor_tensor(z0, v3(yc, 2, 256), sgate[:, 2 * b:2 * b + 2, :], ALU.mult).then_inc(a_z, 1)

                def add(b):
                    dve.wait_ge(a_o, b + 1)
                    nc.vector.tensor_tensor(x[:, 2 * b:2 * b + 2, :], x[:, 2 * b:2 * b + 2, :], v3(PS[:, 7, :], 2, 256),
                                            ALU.add).then_inc(a_xadd, 1)

                for m in range(B * NH0):
                    mask(m)
                    if m % NH0 == 5 and m > NH0:
                        norm(m // NH0 - 1)
                    if m % NH0 == 15 and m > NH0:
                        add(m // NH0 - 1)
                norm(B - 1)
                add(B - 1)
                dve.wait_ge(a_xadd, B)

        layer_norm("B")
        kvT = SC[0:64, 1024:2048]
        kvs = R2[:, 0:512].rearrange("p (i d) -> p i d", d=CD)
        oT = R2[0:64, 512:1024].rearrange("p (a t) -> p a t", a=2)
        sim = v3(R2[:, 1024:2048], 4, 256)
        att = v3(R2[:, 2048:3072], 4, 256)
        bstat = v3(R2[:, 3072:3072 + 48], NT, 6)
        bmv = v3(R2[:, 3120:3136], NT, 2)
        bsd, brs, bmx, bsum, bri = (R2[:, 3136 + 8 * j:3144 + 8 * j] for j in range(5))
        b_kv, b_kvev, b_o, b_oev, b_sim, b_var, b_sd, b_norm, b_max, b_exp, b_read = (
            sem(f"b_{n}") for n in ("kv", "kvev", "o", "oev", "sim", "var", "sd", "norm", "max", "exp", "read"))
        with nc.Block() as block:
            @block.tensor
            def _(pe):
                pe.wait_ge(ld_b, 16 * N_B)
                for c in range(2):
                    nc.tensor.matmul(PS[0:64, c, :], wkT, ctxT[:, c * 512:(c + 1) * 512], start=True, stop=True).then_inc(b_kv, 1)
                for i in range(NT):
                    last = nc.tensor.matmul(PS[:, 2, i * 64:(i + 1) * 64], ctxT[:, i * 128:(i + 1) * 128], wkT, start=True, stop=True)
                last.then_inc(b_kv, 1)
                pe.wait_ge(b_kvev, 3)
                for b in range(B):
                    if b >= 2:
                        pe.wait_ge(b_oev, b - 1)
                    for k in range(KT):
                        last = nc.tensor.matmul(PS[0:64, b % 2, 0:256], kvs[:, 2 * b + k, :], hT[:, k, b * 256:(b + 1) * 256],
                                                start=k == 0, stop=k == 1)
                    last.then_inc(b_o, 1)
                    pe.wait_ge(b_oev, b + 1)
                    for i in range(2):
                        nc.tensor.matmul(PS[:, 4 + b, i * 256:(i + 1) * 256], oT[:, b % 2, i * 128:(i + 1) * 128],
                                         kvT[:, b * 256:(b + 1) * 256], start=True, stop=True).then_inc(b_sim, 1)

            @block.scalar
            def _(act):
                for c in range(2):
                    act.wait_ge(b_kv, c + 1)
                    nc.scalar.activation(kvT[:, c * 512:(c + 1) * 512], PS[0:64, c, :], ACT.Identity, bias=bk_col).then_inc(b_kvev, 1)
                for b in range(B):
                    act.wait_ge(b_o, b + 1)
                    if b >= 2:
                        act.wait_ge(b_sim, 2 * (b - 1))
                    nc.scalar.activation(oT[:, b % 2, :], PS[0:64, b % 2, 0:256], ACT.Copy, scale=1.0 / 16.0).then_inc(b_oev, 1)
                act.wait_ge(b_var, 1)
                nc.scalar.activation(bsd, bmv[:, :, 1], ACT.Sqrt, bias=eps_t[:, 1:2]).then_inc(b_sd, 1)
                for i in range(NT):
                    act.wait_ge(b_max, i + 1)
                    if i >= 4:
                        act.wait_ge(b_read, i - 3)
                    nc.scalar.activation(att[:, i % 4, :], sim[:, i % 4, :], ACT.Exp, bias=bmx[:, i:i + 1],
                                         accum_out=bsum[:, i:i + 1]).then_inc(b_exp, 1)

            @block.vector
            def _(dve):
                dve.wait_ge(b_kv, 3)
                nc.vector.tensor_tensor(kvs, PS[:, 2, :].rearrange("p (i d) -> p i d", d=CD),
                                        bk_row.rearrange("p (o d) -> p o d", o=1).to_broadcast([P, NT, CD]), ALU.add).then_inc(b_kvev, 1)
                for i in range(NT):
                    dve.wait_ge(b_sim, 2 * (i // 2) + 2)
                    link(dve, "v", s_vec, nc.vector.bn_stats(bstat[:, i, :], PS[:, 4 + i // 2, (i % 2) * 256:(i % 2) * 256 + 256]))
                    last = nc.vector.bn_aggr(bmv[:, i, :], bstat[:, i, :])
                last.then_inc(b_var, 1)
                dve.wait_ge(b_sd, 1)
                link(dve, "v", s_vec, nc.vector.reciprocal(brs, bsd))

                def finish(i):
                    dve.wait_ge(b_exp, i + 1)
                    link(dve, "v", s_vec, nc.vector.reciprocal(bri[:, i:i + 1], bsum[:, i:i + 1]))
                    nc.vector.scalar_tensor_tensor(x[:, i, :], att[:, i % 4, :], bri[:, i:i + 1], x[:, i, :],
                                                   ALU.mult, ALU.add).then_inc(b_read, 1)

                for i in range(NT):
                    s = sim[:, i % 4, :]
                    if i >= 4:
                        dve.wait_ge(b_exp, i - 3)
                    link(dve, "v", s_vec, nc.vector.tensor_scalar(s, PS[:, 4 + i // 2, (i % 2) * 256:(i % 2) * 256 + 256],
                                                                  bmv[:, i, 0:1], brs[:, i:i + 1], ALU.subtract, ALU.mult))
                    link(dve, "v", s_vec, nc.vector.tensor_tensor(s, s, xg_row[:, 0:256], ALU.mult))
                    link(dve, "v", s_vec, nc.vector.tensor_tensor(s, s, xg_row[:, 256:512], ALU.add))
                    link(dve, "v", s_vec, nc.vector.tensor_reduce(rin[:, i:i + 1], s, AX.X, ALU.max))
                    nc.vector.tensor_scalar(bmx[:, i:i + 1], rin[:, i:i + 1], -1.0, None, ALU.mult).then_inc(b_max, 1)
                    if i >= 2:
                        finish(i - 2)
                finish(NT - 2)
                finish(NT - 1)
                dve.wait_ge(b_read, NT)

        layer_norm("C")
        hid = SC[:, 0:2048].rearrange("p (a m t) -> p a m t", a=2, m=KT)
        RT = v3(R0[:, 2048:2048 + 12 * 64], 12, 64)
        cmp8 = R0[:, 0:512]
        cmp8b = R0[:, 512:1024]
        sgc = v3(R0[:, 1024:2048], 2, 512)
        inv_t = small[:, 209:210]
        c_z, c_e, c_inh, c_dist, c_w, c_route = (sem(f"c_{n}") for n in ("z", "e", "inh", "dist", "w", "route"))
        c_g, c_silu, c_hid, c_hidt, c_dn, c_add, c_temp = (sem(f"c_{n}") for n in ("g", "silu", "hid", "hidt", "dn", "add", "temp"))
        c_zread = sem("c_zread")
        CENTER = float(np.float32(1.0 / np.e))
        LOWER = float(np.float32(0.5 - np.log(4.0 / 3.0)))
        with nc.Block() as block:
            cunits = [(e, c) for e in range(E0) for c in range(2)]

            @block.sync
            def _(sp):
                for dst, name in ((qw1, "qw1"), (kw1, "kw1"), (vw1, "vw1"), (gw1, "gw1"), (ow1, "ow1")):
                    sp.dma_start(dst, ins[name]).then_inc(ld_d, 16)
                sp.dma_start(vb1, bcast_row(ins["vb1"], 2048)).then_inc(ld_d, 16)
                sp.dma_start(qb1, ins["qb1"]).then_inc(ld_d, 16)
                sp.dma_start(kb1, ins["kb1"]).then_inc(ld_d, 16)
                sp.dma_start(bw1, ins["bw1"]).then_inc(ld_d, 16)
                sp.dma_start(bb1, bcast_row(ins["bb1"], 16)).then_inc(ld_d, 16)
                sp.dma_start(ob1, bcast_row(ins["ob1"], 256)).then_inc(ld_d, 16)

            @block.tensor
            def _(pe):
                pe.wait_ge(ld_moe, 16 * N_MOE)
                for i in range(NT):
                    for k in range(KT):
                        last = nc.tensor.matmul(PS[:, 7, i * 8:(i + 1) * 8], hT[:, k, i * 128:(i + 1) * 128], wr[:, k, :],
                                                start=k == 0, stop=k == 1)
                last.then_inc(c_z, 1)

                def up(u):
                    e, c = cunits[u]
                    for m in range(KT):
                        v = 2 * u + m
                        if v >= 2:
                            pe.wait_ge(c_hid, v - 1)
                        for j, w in enumerate((wge, wue)):
                            for k in range(KT):
                                last = nc.tensor.matmul(PS[:, 2 * (v % 2) + j, :], w[:, e, k, m * 128:(m + 1) * 128],
                                                        hT[:, k, c * 512:(c + 1) * 512], start=k == 0, stop=k == 1)
                            last.then_inc(c_g, 1)

                def down(u):
                    e, c = cunits[u]
                    pe.wait_ge(c_hid, 2 * u + 2)
                    if u == 1:
                        pe.wait_ge(c_zread, 1)
                    if u >= 2:
                        pe.wait_ge(c_add, 4 * (u - 1))
                    for i in range(4):
                        for k in range(KT):
                            last = nc.tensor.matmul(PS[:, 4 + 2 * (u % 2) + i // 2, (i % 2) * 256:(i % 2) * 256 + 256],
                                                    hid[:, u % 2, k, i * 128:(i + 1) * 128], wde[:, e, k, :],
                                                    start=k == 0, stop=k == 1)
                        last.then_inc(c_dn, 1)

                up(0)
                for u in range(1, len(cunits)):
                    up(u)
                    down(u - 1)
                down(len(cunits) - 1)

            @block.scalar
            def _(act):
                act.wait_ge(c_temp, 1)
                act.wait_ge(c_z, 1)
                nc.scalar.activation(RT[:, 0, :], PS[:, 7, 0:64], ACT.Exp, scale=small[:, 210:211]).then_inc(c_zread, 1)
                act.wait_ge(c_dist, 1)
                nc.scalar.activation(RT[:, 2, :], RT[:, 1, :], ACT.Exp, scale=-10.0)
                nc.scalar.activation(RT[:, 3, :], RT[:, 1, :], ACT.Exp, scale=-1.0 / 0.3).then_inc(c_w, 1)
                for u in range(len(cunits)):
                    for m in range(KT):
                        v = 2 * u + m
                        act.wait_ge(c_g, 2 * v + 1)
                        if v >= 2:
                            act.wait_ge(c_hid, v - 1)
                        nc.scalar.activation(sgc[:, v % 2, :], PS[:, 2 * (v % 2), :], ACT.Silu).then_inc(c_silu, 1)

            @block.vector
            def _(dve):
                L = lambda inst: link(dve, "v", s_vec, inst)
                r = lambda j: RT[:, j, :]
                r3 = lambda j: RT[:, j, :].rearrange("p (i e) -> p i e", e=E0)
                dve.wait_ge(ld_moe, 16 * N_MOE)
                L(nc.vector.reciprocal(inv_t, temp))
                nc.vector.tensor_scalar(small[:, 210:211], inv_t, -1.0, None, ALU.mult).then_inc(c_temp, 1)
                dve.wait_ge(c_zread, 1)
                L(nc.vector.tensor_scalar(r(4), r(0), 1.0, None, ALU.add))
                L(nc.vector.reciprocal(r(5), r(4)))
                L(nc.vector.tensor_scalar(r(6), r(5), CENTER, None, ALU.subtract))
                nc.vector.scalar_tensor_tensor(r(1), r(6), -1.0, r(6), ALU.mult, ALU.max).then_inc(c_dist, 1)
                L(nc.vector.tensor_scalar(r(7), r(5), LOWER, None, ALU.is_ge))
                L(nc.vector.scalar_tensor_tensor(r(8), r(5), 0.5, r(7), ALU.is_le, ALU.mult))
                dve.wait_ge(c_w, 1)
                L(nc.vector.tensor_tensor(r(9), r(2), r(8), ALU.mult))
                w8 = small[:, 576:584]
                L(nc.vector.tensor_reduce(w8, r3(9), AX.X, ALU.add))
                no = small[:, 584:592]
                L(nc.vector.tensor_scalar(no, w8, 1e-8, None, ALU.is_lt))
                a4 = RT[:, 3, :].rearrange("p (i e o) -> p i e o", e=E0, o=1).to_broadcast([P, NT, E0, E0])
                b4 = RT[:, 3, :].rearrange("p (i o e) -> p i o e", e=E0, o=1).to_broadcast([P, NT, E0, E0])
                c4 = cmp8.rearrange("p (i e f) -> p i e f", e=E0, f=E0)
                d4 = cmp8b.rearrange("p (i e f) -> p i e f", e=E0, f=E0)
                L(nc.vector.tensor_tensor(c4, b4, a4, ALU.is_gt))
                L(nc.vector.tensor_tensor(d4, b4, a4, ALU.is_equal))
                for e in range(E0):
                    if e:
                        L(nc.vector.tensor_tensor(c4[:, :, e, 0:e], c4[:, :, e, 0:e], d4[:, :, e, 0:e], ALU.add))
                L(nc.vector.tensor_reduce(r(4), cmp8.rearrange("p (i f) -> p i f", f=E0), AX.X, ALU.add))
                L(nc.vector.scalar_tensor_tensor(r(6), r(4), 1.5, r(3), ALU.is_lt, ALU.mult))
                f8, fi = small[:, 592:600], small[:, 600:608]
                L(nc.vector.tensor_reduce(f8, r3(6), AX.X, ALU.add))
                L(nc.vector.tensor_scalar(f8, f8, 1e-8, None, ALU.max))
                L(nc.vector.reciprocal(fi, f8))
                wide = lambda a: a.rearrange("p (i o) -> p i o", o=1).to_broadcast([P, NT, E0])
                L(nc.vector.tensor_tensor(r3(6), r3(6), wide(fi), ALU.mult))
                L(nc.vector.tensor_tensor(r3(6), r3(6), wide(no), ALU.mult))
                L(nc.vector.tensor_scalar(no, no, -1.0, 1.0, ALU.mult, ALU.add))
                L(nc.vector.tensor_tensor(r3(9), r3(9), wide(no), ALU.mult))
                L(nc.vector.tensor_tensor(r(9), r(9), r(6), ALU.add))
                L(nc.vector.tensor_reduce(w8, r3(9), AX.X, ALU.add))
                L(nc.vector.tensor_scalar(w8, w8, 1e-8, None, ALU.max))
                L(nc.vector.reciprocal(fi, w8))
                L(nc.vector.tensor_tensor(r3(10), r3(9), wide(fi), ALU.mult))

                def gated(u):
                    for m in range(KT):
                        v = 2 * u + m
                        dve.wait_ge(c_silu, v + 1)
                        dve.wait_ge(c_g, 2 * v + 2)
                        if u >= 2:
                            dve.wait_ge(c_dn, 4 * (u - 1))
                        nc.vector.tensor_tensor(hid[:, u % 2, m, :], PS[:, 2 * (v % 2) + 1, :], sgc[:, v % 2, :],
                                                ALU.mult).then_inc(c_hid, 1)

                def add(u):
                    e, c = cunits[u]
                    for i in range(4):
                        dve.wait_ge(c_dn, 4 * u + 2 * (i // 2) + 2)
                        ti = 4 * c + i
                        if u >= 2:
                            dve.wait_ge(c_add, 4 * (u - 2) + i + 1)
                        nc.vector.scalar_tensor_tensor(
                            x[:, ti, :], PS[:, 4 + 2 * (u % 2) + i // 2, (i % 2) * 256:(i % 2) * 256 + 256],
                            RT[:, 10, 8 * ti + e:8 * ti + e + 1], x[:, ti, :], ALU.mult, ALU.add).then_inc(c_add, 1)

                gated(0)
                for u in range(1, len(cunits)):
                    gated(u)
                    add(u - 1)
                add(len(cunits) - 1)
                dve.wait_ge(c_add, 4 * len(cunits))

        layer_norm("D")
        def r1(n, a):
            o = r1.at
            r1.at += n * a
            return v3(R1[:, o:o + n * a], a, n)
        r1.at = 0
        qraw, qn, kT1, sqq, sqk, gate1, v1, st1, zT1, rq1 = (r1(512, 2) for _ in range(10))
        DS = r1(64, 8)
        betas = DS[:, 0:2, :]
        kn4 = DS[:, 3, :]
        kr4 = DS[:, 4, :]
        beta_v = DS[:, 0:2, :].rearrange("p a b -> p (a b)")
        d_z, d_zp, d_q, d_k, d_g, d_v = (sem(f"d_{n}") for n in ("z", "zp", "q", "k", "g", "v"))
        d_qev, d_kev, d_gev, d_vev, d_nq, d_nk, d_nqs, d_nks, d_qn, d_rb = (
            sem(f"d_{n}") for n in ("qev", "kev", "gev", "vev", "nq", "nk", "nqs", "nks", "qn", "rb"))
        d_s, d_sev, d_o, d_zev, d_acc, d_xadd, d_b1, d_b2 = (sem(f"d_{n}") for n in ("s", "sev", "o", "zev", "acc", "xadd", "b1", "b2"))
        d_x0 = sem("d_x0")
        ctxZ = R0[:, :].rearrange("p (k g t) -> p k g t", k=2, g=GRP)
        with nc.Block() as block:
            dunits = [(c, n) for c in range(2) for n in range(NH1)]
            ND = len(dunits)

            @block.gpsimd
            def _(pool):
                nc.gpsimd.memset(R0[:, :], 0.0).then_inc(z_clear, 1)

            @block.sync
            def _(sp):
                sp.wait_ge(z_clear, 1)
                for kv in range(KVH):
                    for g in range(GRP):
                        r0 = 32 * (kv % 4) + 8 * g
                        sp.dma_start(ctxZ[r0:r0 + 8, kv // 4, g, :], ins["ctxT"][kv * 8:kv * 8 + 8, :]).then_inc(ld_z, 16)

            @block.tensor
            def _(pe):
                pe.wait_ge(ld_d, 16 * N_D)
                for i in range(NT):
                    for k in range(KT):
                        last = nc.tensor.matmul(PS[:, 7, i * 16:(i + 1) * 16], hT[:, k, i * 128:(i + 1) * 128], bw1[:, k, :],
                                                start=k == 0, stop=k == 1)
                last.then_inc(d_z, 1)

                def proj(w, bank, u, done):
                    c, n = dunits[u]
                    for k in range(KT):
                        last = nc.tensor.matmul(PS[:, bank, :], w[:, k, n * 128:(n + 1) * 128], hT[:, k, c * 512:(c + 1) * 512],
                                                start=k == 0, stop=k == 1)
                    last.then_inc(done, 1)

                def qk(u):
                    if u >= 1:
                        pe.wait_ge(d_qev, 2 * u)
                    proj(qw1, 0, u, d_q)
                    if u >= 1:
                        pe.wait_ge(d_kev, 2 * u)
                    proj(kw1, 1, u, d_k)

                def gate(u):
                    if u >= 1:
                        pe.wait_ge(d_gev, u)
                    proj(gw1, 2, u, d_g)

                def val(u):
                    c, n = dunits[u]
                    if u >= 1:
                        pe.wait_ge(d_nks, u)
                    for i in range(4):
                        for k in range(KT):
                            last = nc.tensor.matmul(PS[:, 3, i * 128:(i + 1) * 128],
                                                    hT[:, k, (4 * c + i) * 128:(4 * c + i + 1) * 128], vw1[:, k, n * 128:(n + 1) * 128],
                                                    start=k == 0, stop=k == 1)
                    last.then_inc(d_v, 1)

                def norms(u):
                    pe.wait_ge(d_qev, 2 * u + 2)
                    if u >= 1:
                        pe.wait_ge(d_zev, u)
                    nc.tensor.matmul(PS[:, 4, :], ones, sqq[:, u % 2, :], start=True, stop=True).then_inc(d_nq, 1)
                    pe.wait_ge(d_kev, 2 * u + 2)
                    pe.wait_ge(d_vev, u + 1)
                    for i in range(4):
                        last = nc.tensor.matmul(PS[:, 3, i:i + 1], sqk[:, u % 2, i * 128:(i + 1) * 128], ones[:, 0:1],
                                                start=True, stop=True)
                    last.then_inc(d_nk, 1)

                def scores(u):
                    pe.wait_ge(d_qn, u + 1)
                    if u >= 1:
                        pe.wait_ge(d_sev, 4 * u)
                    for i in range(4):
                        t = slice(i * 128, (i + 1) * 128)
                        nc.tensor.matmul(PS[:, 5, t], kT1[:, u % 2, t], qn[:, u % 2, t], start=True, stop=True).then_inc(d_s, 1)

                def mix(u):
                    for i in range(4):
                        t = slice(i * 128, (i + 1) * 128)
                        pe.wait_ge(d_sev, 4 * u + i + 1)
                        last = nc.tensor.matmul(PS[:, 4, t], v1[:, u % 2, t], st1[:, u % 2, t], start=True, stop=True)
                    last.then_inc(d_o, 1)

                def out_proj(u):
                    c, n = dunits[u]
                    pe.wait_ge(d_zev, u + 1)
                    if n == 0:
                        if c:
                            pe.wait_ge(d_xadd, 2 * c)
                        else:
                            pe.wait_ge(d_zp, 1)
                    for i in range(4):
                        last = nc.tensor.matmul(PS[:, 6 + i // 2, (i % 2) * 256:(i % 2) * 256 + 256],
                                                zT1[:, u % 2, i * 128:(i + 1) * 128], ow1[:, n, :],
                                                start=(n == 0 and i % 2 == 0), stop=n == NH1 - 1, skip_group_check=True)
                    last.then_inc(d_acc, 1)

                for u in range(ND + 2):
                    if u < ND:
                        qk(u)
                    if u >= 2:
                        out_proj(u - 2)
                    if 1 <= u <= ND:
                        scores(u - 1)
                    if u < ND:
                        gate(u)
                    if 1 <= u <= ND:
                        mix(u - 1)
                    if u < ND:
                        val(u)
                        norms(u)

            @block.scalar
            def _(act):
                act.wait_ge(d_b1, 1)
                nc.scalar.activation(DS[:, 5:7, :], DS[:, 5:7, :], ACT.Exp, scale=-1.0).then_inc(s_act, 1)
                chain["a"] += 1
                act.wait_ge(s_act, chain["a"])
                nc.scalar.activation(DS[:, 5:7, :], DS[:, 5:7, :], ACT.Ln, bias=1.0).then_inc(d_b2, 1)
                for u in range(ND):
                    c, n = dunits[u]
                    act.wait_ge(d_q, u + 1)
                    if u >= 2:
                        act.wait_ge(d_qn, u - 1)
                    nc.scalar.activation(qraw[:, u % 2, :], PS[:, 0, :], ACT.Identity, bias=qb1[:, n:n + 1]).then_inc(d_qev, 1)
                    if u >= 2:
                        act.wait_ge(d_nq, u - 1)
                    nc.scalar.activation(sqq[:, u % 2, :], PS[:, 0, :], ACT.Square, bias=qb1[:, n:n + 1]).then_inc(d_qev, 1)
                    act.wait_ge(d_k, u + 1)
                    if u >= 2:
                        act.wait_ge(d_s, 4 * (u - 1))
                    nc.scalar.activation(kT1[:, u % 2, :], PS[:, 1, :], ACT.Identity, bias=kb1[:, n:n + 1]).then_inc(d_kev, 1)
                    if u >= 2:
                        act.wait_ge(d_nk, u - 1)
                    nc.scalar.activation(sqk[:, u % 2, :], PS[:, 1, :], ACT.Square, bias=kb1[:, n:n + 1]).then_inc(d_kev, 1)
                    act.wait_ge(d_g, u + 1)
                    if u >= 2:
                        act.wait_ge(d_zev, u - 1)
                    nc.scalar.activation(gate1[:, u % 2, :], PS[:, 2, :], ACT.Silu).then_inc(d_gev, 1)
                    act.wait_ge(d_nq, u + 1)
                    if u >= 2:
                        act.wait_ge(d_qn, u - 1)
                    nc.scalar.activation(rq1[:, u % 2, :], PS[:, 4, :], ACT.Sqrt).then_inc(d_nqs, 1)
                    act.wait_ge(d_nk, u + 1)
                    if u >= 1:
                        act.wait_ge(d_sev, 4 * u)
                    nc.scalar.activation(kn4[:, 0:4], PS[:, 3, 0:4], ACT.Sqrt).then_inc(d_nks, 1)

            @block.vector
            def _(dve):
                L = lambda inst: link(dve, "v", s_vec, inst)
                zb = beta_v.rearrange("p (i n) -> p i n", n=NH1)
                tmp = DS[:, 5:7, :].rearrange("p a b -> p (a b)").rearrange("p (i n) -> p i n", n=NH1)
                dve.wait_ge(d_z, 1)
                nc.vector.tensor_tensor(zb, PS[:, 7, 0:128].rearrange("p (i n) -> p i n", n=NH1),
                                        bb1.rearrange("p (o n) -> p o n", o=1).to_broadcast([P, NT, NH1]), ALU.add).then_inc(d_zp, 1)
                dve.wait_ge(d_zp, 1)
                nc.vector.scalar_tensor_tensor(tmp, zb, -1.0, zb, ALU.mult, ALU.max).then_inc(d_b1, 1)
                L(nc.vector.tensor_scalar(zb, zb, 0.0, None, ALU.max))
                dve.wait_ge(d_b2, 1)
                L(nc.vector.tensor_tensor(zb, zb, tmp, ALU.add))
                nc.vector.tensor_tensor(x[:], x[:], ob1.rearrange("p (o f) -> p o f", o=1).to_broadcast([P, NT, H]), ALU.add).then_inc(d_x0, 1)

                def values(u):
                    c, n = dunits[u]
                    dve.wait_ge(d_v, u + 1)
                    if u >= 2:
                        dve.wait_ge(d_o, u - 1)
                    nc.vector.tensor_tensor(v3(v1[:, u % 2, :], 4, 128), v3(PS[:, 3, :], 4, 128),
                                            vb1[:, n * 128:(n + 1) * 128].rearrange("p (o d) -> p o d", o=1).to_broadcast([P, 4, 128]),
                                            ALU.add).then_inc(d_vev, 1)

                def qnorm(u):
                    c, n = dunits[u]
                    dve.wait_ge(d_nqs, u + 1)
                    r = rq1[:, u % 2, :]
                    L(nc.vector.tensor_scalar(r, r, 1e-12 * float(HD1) ** 0.5, None, ALU.max))
                    L(nc.vector.reciprocal(r, r))
                    if u >= 2:
                        dve.wait_ge(d_s, 4 * (u - 1))
                    nc.vector.tensor_tensor(qn[:, u % 2, :], qraw[:, u % 2, :], r, ALU.mult).then_inc(d_qn, 1)
                    dve.wait_ge(d_nks, u + 1)
                    L(nc.vector.tensor_scalar(kr4[:, 4:8], kn4[:, 0:4], 1e-12 * float(HD1) ** 0.5, None, ALU.max))
                    L(nc.vector.reciprocal(kr4[:, 8:12], kr4[:, 4:8]))
                    L(nc.vector.tensor_tensor(kr4[:, 0:4], kr4[:, 8:12], zb[:, 4 * c:4 * c + 4, n], ALU.mult))

                def masked(u):
                    for i in range(4):
                        t = slice(i * 128, (i + 1) * 128)
                        dve.wait_ge(d_s, 4 * u + 4)
                        if u >= 2:
                            dve.wait_ge(d_o, u - 1)
                        nc.vector.scalar_tensor_tensor(st1[:, u % 2, t], PS[:, 5, t], kr4[:, i:i + 1], mask_chunk[:, t],
                                                       ALU.mult, ALU.mult).then_inc(d_sev, 1)

                def gated(u):
                    dve.wait_ge(d_o, u + 1)
                    dve.wait_ge(d_gev, u + 1)
                    if u >= 2:
                        dve.wait_ge(d_acc, u - 1)
                    nc.vector.tensor_tensor(zT1[:, u % 2, :], PS[:, 4, :], gate1[:, u % 2, :], ALU.mult).then_inc(d_zev, 1)

                def add(c):
                    dve.wait_ge(d_acc, (c + 1) * NH1)
                    if c == 0:
                        dve.wait_ge(d_x0, 1)
                    for j in range(2):
                        t = slice(4 * c + 2 * j, 4 * c + 2 * j + 2)
                        nc.vector.tensor_tensor(x[:, t, :], x[:, t, :], v3(PS[:, 6 + j, :], 2, 256), ALU.add).then_inc(d_xadd, 1)

                for u in range(ND + 1):
                    if u >= 1:
                        masked(u - 1)
                        gated(u - 1)
                    if u < ND:
                        values(u)
                        qnorm(u)
                    if u == NH1 + 1:
                        add(0)
                add(1)
                dve.wait_ge(d_xadd, 4)

        layer_norm("E")
        nh8 = 8
        Pp = R2[:, 12288:12288 + 4096].rearrange("p (a j s) -> p a j s", a=2, j=nh8)
        PT = R2[:, 16384:16384 + 4096].rearrange("p (a m t) -> p a m t", a=2, m=16)
        mx = R2[:, 20480:20992].rearrange("p (a b) -> p a b", b=nh8)
        nmx = R2[:, 20992:21504].rearrange("p (a b) -> p a b", b=nh8)
        rs = R2[:, 21504:21504 + 256].rearrange("p (b v j) -> p b v j", b=B, v=KVH)
        rri = R2[:, 21760:21760 + 256].rearrange("p (b v j) -> p b v j", b=B, v=KVH)
        on = v3(R2[:, 22016:22528], 2, 256)
        SCALE2 = 1.0 / float(np.sqrt(HD2))
        e_s, e_mx, e_nm, e_ex, e_t, e_tev, e_pv, e_ri, e_fin, e_oread = (
            sem(f"e_{n}") for n in ("s", "mx", "nm", "ex", "t", "tev", "pv", "ri", "fin", "oread"))
        with nc.Block() as block:
            eunits = [(b, kv) for b in range(B) for kv in range(KVH)]
            NE = len(eunits)

            @block.sync
            def _(sp):
                sp.dma_start(R1[:, 0:2048].bitcast(I32), ins["pg"]).then_inc(ld_f, 16)
                sp.dma_start(R1[:, 2048:4096].bitcast(I32), ins["pu"]).then_inc(ld_f, 16)
                sp.dma_start(R1[:, 4096:6144].bitcast(I32), ins["pd"]).then_inc(ld_f, 16)
                for blk in range(8):
                    rows = slice(16 * blk, 16 * blk + 16)
                    sp.dma_start(sg1[rows, :], ins["gs"][blk:blk + 1, :].to_broadcast([16, MLP])).then_inc(ld_f, 16)
                    sp.dma_start(su1[rows, :], ins["us"][blk:blk + 1, :].to_broadcast([16, MLP])).then_inc(ld_f, 16)
                    sp.dma_start(sd1[rows, :], ins["ds"][blk:blk + 1, :].to_broadcast([16, MLP])).then_inc(ld_f, 16)

            @block.tensor
            def _(pe):
                pe.wait_ge(ld_z, 16 * 32)

                def scores(u):
                    b, kv = eunits[u]
                    row = slice(32 * (kv % 4), 32 * (kv % 4) + 32)
                    for j in range(nh8):
                        tt, g = j // 4, j % 4
                        if u >= 1 and j % 2 == 0:
                            pe.wait_ge(e_ex, 8 * (u - 1) + j + 2)
                        tok = b * 256 + tt * 128
                        nc.tensor.matmul(PS[:, j // 2, (j % 2) * 256:(j % 2) * 256 + 256], hT[row, kv // 4, tok:tok + 128],
                                         ctxZ[row, kv // 4, g, b * 256:(b + 1) * 256], start=True, stop=True).then_inc(e_s, 1)

                def turn(u):
                    for q in range(4):
                        w = 4 * u + q
                        pe.wait_ge(e_ex, 8 * u + 2 * q + 2)
                        if w >= 3:
                            pe.wait_ge(e_tev, w - 2)
                        for m in range(4):
                            last = nc.tensor.transpose(PS[:, 4 + w % 3, m * 128:(m + 1) * 128],
                                                       Pp[:, u % 2, 2 * q + m // 2, (m % 2) * 128:(m % 2) * 128 + 128], ident)
                        last.then_inc(e_t, 1)

                def mix(u):
                    b, kv = eunits[u]
                    pe.wait_ge(e_tev, 4 * u + 4)
                    if kv == 0 and b:
                        pe.wait_ge(e_oread, b)
                    for j in range(nh8):
                        tt, g = j // 4, j % 4
                        o = tt * 256 + kv * 32 + g * 8
                        for st in range(2):
                            last = nc.tensor.matmul(PS[:, 7, o:o + 8], PT[:, u % 2, 2 * j + st, :],
                                                    ctx_s[:, 2 * b + st, kv * 8:kv * 8 + 8], start=st == 0, stop=st == 1)
                    last.then_inc(e_pv, 1)

                for u in range(NE + 2):
                    if u < NE:
                        scores(u)
                    if 1 <= u <= NE:
                        turn(u - 1)
                    if u >= 2:
                        mix(u - 2)

            @block.scalar
            def _(act):
                for u in range(NE):
                    b, kv = eunits[u]
                    act.wait_ge(e_nm, u + 1)
                    if u >= 2:
                        act.wait_ge(e_t, 4 * (u - 1))
                    for j in range(nh8):
                        nc.scalar.activation(Pp[:, u % 2, j, :], PS[:, j // 2, (j % 2) * 256:(j % 2) * 256 + 256], ACT.Exp,
                                             bias=nmx[:, u, j:j + 1], scale=SCALE2,
                                             accum_out=rs[:, b, kv, j:j + 1]).then_inc(e_ex, 1)

            @block.vector
            def _(dve):
                L = lambda inst: link(dve, "v", s_vec, inst)

                def maxima(u):
                    for q in range(4):
                        dve.wait_ge(e_s, 8 * u + 2 * q + 2)
                        nc.vector.tensor_reduce(mx[:, u, 2 * q:2 * q + 2], v3(PS[:, q, :], 2, 256), AX.X, ALU.max).then_inc(e_mx, 1)
                    dve.wait_ge(e_mx, 4 * u + 4)
                    nc.vector.tensor_scalar(nmx[:, u, :], mx[:, u, :], -SCALE2, None, ALU.mult).then_inc(e_nm, 1)

                def evac(u):
                    for q in range(4):
                        w = 4 * u + q
                        dve.wait_ge(e_t, w + 1)
                        if u >= 2:
                            dve.wait_ge(e_pv, u - 1)
                        nc.vector.tensor_copy(PT[:, u % 2, 4 * q:4 * q + 4, :], v3(PS[:, 4 + w % 3, :], 4, 128)).then_inc(e_tev, 1)

                def finish(b):
                    dve.wait_ge(e_pv, KVH * (b + 1))
                    L(nc.vector.reciprocal(rri[:, b, :, :], rs[:, b, :, :]))
                    for tt in range(2):
                        o4 = PS[:, 7, tt * 256:(tt + 1) * 256].rearrange("p (h d) -> p h d", d=HD2)
                        n4 = on[:, tt, :].rearrange("p (h d) -> p h d", d=HD2)
                        for kv in range(KVH):
                            last = nc.vector.tensor_tensor(
                                n4[:, 4 * kv:4 * kv + 4, :], o4[:, 4 * kv:4 * kv + 4, :],
                                rri[:, b, kv, 4 * tt:4 * tt + 4].rearrange("p (h o) -> p h o", o=1).to_broadcast([P, 4, HD2]), ALU.mult)
                    last.then_inc(e_oread, 1)
                    dve.wait_ge(e_oread, b + 1)
                    L(nc.vector.tensor_tensor(x[:, 2 * b:2 * b + 2, :], x[:, 2 * b:2 * b + 2, :], on, ALU.add))

                for u in range(NE + 1):
                    if u < NE:
                        maxima(u)
                    if u >= 1:
                        evac(u - 1)
                    if u >= 2 and (u - 2) % KVH == KVH - 1:
                        finish((u - 2) // KVH)
                finish(B - 1)

        layer_norm("F", parity=True)
        code, sign = R0[:, 0:1024].bitcast(I16), R0[:, 1024:2048].bitcast(I16)
        lin = R0[:, 2048:3072].bitcast(BF16)
        val = R0[:, 3072:4096].bitcast(BF16)
        gel = v3(SC[:, 0:1024], 2, 512)
        hidm = v3(SC[:, 1024:2048], 2, 512)
        f_w = sem("f_w")
        f_g, f_gel, f_hid, f_dn, f_add, f_out = (sem(f"f_{n}") for n in ("g", "gel", "hid", "dn", "add", "out"))
        with nc.Block() as block:
            funits = [(c, n) for c in range(2) for n in range(NB)]
            NF = len(funits)

            @block.tensor
            def _(pe):
                pe.wait_ge(f_w, 4)

                def up(u):
                    c, n = funits[u]
                    if u >= 2:
                        pe.wait_ge(f_hid, u - 1)
                    for j, w in enumerate((wgm, wum)):
                        for k in range(KT):
                            last = nc.tensor.matmul(PS[:, 2 * (u % 2) + j, :], w[:, k, n * 128:(n + 1) * 128],
                                                    hT[:, k, c * 512:(c + 1) * 512], start=k == 0, stop=k == 1)
                        last.then_inc(f_g, 1)

                def down(u):
                    c, n = funits[u]
                    pe.wait_ge(f_hid, u + 1)
                    if u == 0:
                        pe.wait_ge(f_w, 6)
                    for i in range(4):
                        last = nc.tensor.matmul(PS[:, 4 + 2 * c + i // 2, (i % 2) * 256:(i % 2) * 256 + 256],
                                                hidm[:, u % 2, i * 128:(i + 1) * 128], wdm[:, n % 2, n // 2, :],
                                                start=(n == 0 and i % 2 == 0), stop=n == NB - 1, skip_group_check=True)
                    last.then_inc(f_dn, 1)

                up(0)
                for u in range(1, NF):
                    up(u)
                    down(u - 1)
                down(NF - 1)

            @block.scalar
            def _(act):
                for u in range(NF):
                    act.wait_ge(f_g, 2 * u + 1)
                    if u >= 2:
                        act.wait_ge(f_hid, u - 1)
                    nc.scalar.activation(gel[:, u % 2, :], PS[:, 2 * (u % 2), :], ACT.Gelu_apprx_tanh).then_inc(f_gel, 1)

            @block.vector
            def _(dve):
                L = lambda inst: link(dve, "v", s_vec, inst)
                dve.wait_ge(ld_f, 16 * 27)

                def dequant(packed, scales, dst, parity):
                    src = packed[:, 0::2]
                    if parity == 0:
                        L(nc.vector.tensor_scalar(code, src, 6, 0x1C0, ALU.logical_shift_left, ALU.bitwise_and))
                        L(nc.vector.tensor_scalar(sign, src, 12, -32768, ALU.logical_shift_left, ALU.bitwise_and))
                    else:
                        L(nc.vector.tensor_scalar(code, src, 2, 0x1C0, ALU.logical_shift_left, ALU.bitwise_and))
                        L(nc.vector.tensor_scalar(sign, src, 8, -32768, ALU.logical_shift_left, ALU.bitwise_and))
                    L(nc.vector.tensor_scalar(code, code, 0x3E00, None, ALU.bitwise_or))
                    L(nc.vector.tensor_scalar(lin, code.bitcast(BF16), 8.0, -1.0, ALU.mult, ALU.add))
                    L(nc.vector.tensor_scalar(val, code.bitcast(BF16), 4.0, None, ALU.mult))
                    L(nc.vector.tensor_tensor(val, lin, val, ALU.min))
                    L(nc.vector.tensor_tensor(val.bitcast(I16), val.bitcast(I16), sign, ALU.bitwise_or))
                    L(nc.vector.tensor_tensor(dst, val, scales, ALU.mult))
                    nc.vector.memset(small[:, 610:611], 0.0).then_inc(f_w, 1)

                dequant(pg, sg1, wgm[:, 0, :], 0)
                dequant(pg, sg1, wgm[:, 1, :], 1)
                dequant(pu, su1, wum[:, 0, :], 0)
                dequant(pu, su1, wum[:, 1, :], 1)
                dequant(pd, sd1, wdm[:, 0, :, :].rearrange("p j h -> p (j h)"), 0)
                dequant(pd, sd1, wdm[:, 1, :, :].rearrange("p j h -> p (j h)"), 1)

                def add(c):
                    dve.wait_ge(f_dn, (c + 1) * NB)
                    for j in range(2):
                        t = slice(4 * c + 2 * j, 4 * c + 2 * j + 2)
                        nc.vector.tensor_tensor(x[:, t, :], x[:, t, :], v3(PS[:, 4 + 2 * c + j, :], 2, 256), ALU.add).then_inc(f_add, 1)

                for u in range(NF):
                    dve.wait_ge(f_gel, u + 1)
                    dve.wait_ge(f_g, 2 * u + 2)
                    if u >= 2:
                        dve.wait_ge(f_dn, u - 1)
                    nc.vector.tensor_tensor(hidm[:, u % 2, :], PS[:, 2 * (u % 2) + 1, :], gel[:, u % 2, :], ALU.mult).then_inc(f_hid, 1)
                    if u == NB + 1:
                        add(0)
                add(1)

            @block.sync
            def _(sp):
                for c in range(2):
                    sp.wait_ge(f_add, 2 * c + 2)
                    sp.dma_start(out[:, 4 * c:4 * c + 4, :], x[:, 4 * c:4 * c + 4, :]).then_inc(f_out, 16)
                sp.wait_ge(f_out, 32)


def shape_constants():
    i = np.arange(P)
    causal = (i[:, None] <= i[None, :]).astype(np.float32)
    same = (i[:, None] // CHUNK == i[None, :] // CHUNK).astype(np.float32)
    mask_ret = np.concatenate([causal, np.ones((P, P), np.float32), causal], 1)
    consts = np.concatenate([np.eye(P, dtype=np.float32), np.ones((P, P), np.float32), mask_ret] + [causal * same] * 4, 1)
    half = HD0 // 2
    xscale = (np.arange(0, HD0, 2, dtype=np.float32) + np.float32(0.4 * HD0)) / np.float32(1.4 * HD0)
    pos = np.arange(S, dtype=np.float32)
    scale = xscale[None, :].astype(np.float64) ** (pos[:, None] / 64).astype(np.float64)
    inv_freq = (1.0 / 10000.0 ** (np.arange(half) / half)).astype(np.float32)
    angle = (pos[:, None] * inv_freq[None, :]).astype(np.float64)
    gammas = (1.0 - np.exp(np.linspace(np.log(1.0 / 32), np.log(1.0 / 64), NH0))).astype(np.float32).astype(np.float64)
    tab = np.zeros((3, NH0, 2, HD0, S))
    for n in range(NH0):
        grow = gammas[n] ** pos.astype(np.float64)
        for d in range(HD0):
            sgn = -1.0 if d % 2 == 0 else 1.0
            c, s, sc = np.cos(angle[:, d // 2]), sgn * np.sin(angle[:, d // 2]), scale[:, d // 2]
            tab[0, n, 0, d] = c * sc * grow
            tab[0, n, 1, d] = s * sc * grow
            tab[1, n, :, d] = c / sc / grow
            tab[2, n, :, d] = s / sc / grow
    tab = tab.reshape(3, 4, P, S).transpose(2, 0, 1, 3)
    return consts, tab.astype(np.float32)


def kernel(**inputs):
    import concourse.bacc as _bacc
    from concourse.bass_utils import run_bass_kernel_spmd as _run

    a = {k: np.asarray(v) for k, v in inputs.items()}
    kp = lambda w: w.reshape(KT, P, -1).transpose(1, 0, 2)
    swap = np.arange(HD0) ^ 1
    heads = lambda w: w.transpose(1, 0, 2)
    pair = lambda u, v: kp(np.stack([heads(u), heads(v)], 2).reshape(H, 512)).reshape(P, KT, 4, P)
    wq, wk = a["L0_attn_W_Q"], a["L0_attn_W_K"]
    consts, rot_tab = shape_constants()
    ctx = a["ctx_512"]
    codes = lambda p: p.T.reshape(P, 8, P, 2).transpose(0, 1, 3, 2).reshape(P, MLP)
    scl = lambda s: s.T.reshape(8, 8, P, 2).transpose(0, 1, 3, 2).reshape(8, MLP)
    arrays = {
        "x": a["x"].reshape(NT, P, H).transpose(1, 0, 2),
        "consts": consts, "rot_tab": rot_tab,
        "wq32": pair(wq, wq[:, :, swap]), "wk32": pair(wk, wk), "wkr32": pair(wk[:, :, swap], wk[:, :, swap]),
        "wv0": kp(heads(a["L0_attn_W_V"]).reshape(H, 256)), "wg0": kp(a["L0_attn_W_G"]), "wo0": kp(a["L0_attn_W_O"]),
        "gn_w": a["L0_attn_gn_weight"], "gn_b": a["L0_attn_gn_bias"],
        "ctxT": ctx.reshape(T, CD).T, "ctx_s": ctx.reshape(NT, P, CD).transpose(1, 0, 2),
        "wkT": a["L0_xattn_W_k"].T, "bk": a["L0_xattn_b_k"], "xg": a["L0_xattn_ln_gamma"], "xb": a["L0_xattn_ln_beta"],
        "wr": kp(a["L0_ffn_Wr"]), "temp": a["L0_ffn_temperature"],
        "wge": a["L0_ffn_Wg"].reshape(E0, KT, P, 256).transpose(2, 0, 1, 3),
        "wue": a["L0_ffn_Wu"].reshape(E0, KT, P, 256).transpose(2, 0, 1, 3),
        "wde": a["L0_ffn_Wd"].reshape(E0, KT, P, 256).transpose(2, 0, 1, 3),
        "qw1": kp(a["L1_attn_q_w"].T), "kw1": kp(a["L1_attn_k_w"].T), "vw1": kp(a["L1_attn_v_w"].T), "gw1": kp(a["L1_attn_og_w"].T),
        "ow1": a["L1_attn_o_w"].T.reshape(NB, P, H).transpose(1, 0, 2),
        "vb1": a["L1_attn_v_b"], "qb1": a["L1_attn_q_b"].reshape(NH1, P).T, "kb1": a["L1_attn_k_b"].reshape(NH1, P).T,
        "bw1": kp(a["L1_attn_b_w"].T), "bb1": a["L1_attn_b_b"], "ob1": a["L1_attn_o_b"],
        "pg": codes(a["L1_ffn_gate_W_packed"]), "pu": codes(a["L1_ffn_up_W_packed"]),
        "pd": a["L1_ffn_down_W_packed"].T.reshape(8, P, H).transpose(1, 0, 2).reshape(P, MLP),
        "gs": scl(a["L1_ffn_gate_scales"]), "us": scl(a["L1_ffn_up_scales"]),
        "ds": a["L1_ffn_down_scales"].T.reshape(8, 8, H).transpose(1, 0, 2).reshape(8, MLP),
    }
    nc = _bacc.Bacc("TRN2", target_bir_lowering=False, num_devices=1)
    args, feed = {}, {}
    for name, arr in arrays.items():
        arr = np.ascontiguousarray(arr)
        feed[f"in_{name}"] = arr
        args[name] = nc.dram_tensor(f"in_{name}", arr.shape, mybir.dt.from_np(arr.dtype), kind="ExternalInput").ap()
    out = nc.dram_tensor("out_x", (P, NT, H), F32, kind="ExternalOutput").ap()
    build_decoder(nc, args, out)
    r = _run(nc, [feed], core_ids=[0])
    return r.results[0]["out_x"].transpose(1, 0, 2).reshape(B, S, H)
```

```python
from contextlib import ExitStack

import numpy as np

import concourse.bass as bass
from concourse import mybir

ALU = mybir.AluOpType
ACT = mybir.ActivationFunctionType
AX = mybir.AxisListType
F32 = mybir.dt.float32
F32R = mybir.dt.float32r
BF16 = mybir.dt.bfloat16
I16 = mybir.dt.int16
I32 = mybir.dt.int32

P = 128
B, S, H = 4, 256, 256
T = B * S
NT = T // P
KT = H // P
HALF = T // 2
NH0, HD0 = 16, 16
E0 = 8
NH1, HD1 = 16, 128
CHUNK = 64
KVH, GRP, HD2 = 8, 4, 8
CD = 64
MLP = 2048
NB = MLP // P
LN_EPS = 1e-5

KB = 256


def build_decoder(nc, ins, out):
    with ExitStack() as ctx:
        def sb(name, shape, dt=F32):
            return ctx.enter_context(nc.sbuf_tensor(name, shape, dt))

        sem_names = set()

        def sem(name):
            assert name not in sem_names
            sem_names.add(name)
            return ctx.enter_context(nc.semaphore(name))

        PS = ctx.enter_context(nc.psum_tensor("PS", [P, 8, 512], F32))
        x = sb("x", [P, NT, H])
        hTh = sb("hTh", [P, KT, T], F32R)
        hTl = sb("hTl", [P, KT, T], F32R)
        consts = sb("consts", [P, 1152])
        ident = consts[:, 0:128]
        ones = consts[:, 128:256]
        mask_ret = consts[:, 256:640]
        mask_chunk = consts[:, 640:1152]
        eps_t = sb("eps_t", [P, 2])
        small = sb("small", [P, 640])

        SLAB_KB = 167
        slab = sb("slab", [P, SLAB_KB * KB])
        slab_at = nc.lookup_mloc("slab").addr

        def at(kb, name, words, dt=F32):
            assert kb * KB + words <= SLAB_KB * KB
            n = words * 4 // (2 if dt in (I16, BF16) else 4)
            return nc.alloc_sbuf_tensor_at(name, [P, n], dt, offset=slab_at + kb * 1024)[:, :]

        def v3(ap, a, b):
            return ap.rearrange("p (a b) -> p a b", a=a, b=b)

        def v4(ap, a, b, c):
            return ap.rearrange("p (a b c) -> p a b c", a=a, b=b, c=c)

        PASSES = ((0, 0), (0, 1), (1, 0))

        def mm3(out, stat, mov, start, stop, **kw):
            for j, (a, b) in enumerate(PASSES):
                last = nc.tensor.matmul(out, stat[a], mov[b], start=start and j == 0, stop=stop and j == 2, **kw)
            return last

        R2 = at(32, "R2", 88 * KB)
        hT = v3(at(120, "hT", 2048), KT, T)
        SC = at(128, "SC", 2048)
        a_w = v3(at(0, "a_w", 2048), KT, 1024)
        a_wh_t = v3(at(8, "a_wh_t", 2048, F32R), KT, 1024)
        a_wl_t = v3(at(16, "a_wl_t", 2048, F32R), KT, 1024)
        rot_tab = v3(at(24, "rot_tab", 2048), 2, 1024)
        gn_w, gn_b = at(112, "gn_w", 256), at(113, "gn_b", 256)
        wo0 = v3(at(114, "a_wo", 512), KT, 256)
        woh = v3(at(116, "a_woh", 512, F32R), KT, 256)
        wol = v3(at(118, "a_wol", 512, F32R), KT, 256)

        s_vec = sem("s_vec")
        s_act = sem("s_act")
        s_pool = sem("s_pool")
        chain = {"v": 0, "a": 0, "p": 0}

        def link(eng, key, s, inst):
            chain[key] += 1
            inst.then_inc(s, 1)
            eng.wait_ge(s, chain[key])

        ld_x, ld_c, ld_a, ld_w = sem("ld_x"), sem("ld_c"), sem("ld_a"), sem("ld_w")
        a_whi, a_wl, a_wo = sem("a_whi"), sem("a_wl"), sem("a_wo")
        ld_b, ld_moe = sem("ld_b"), sem("ld_moe")
        ld_d, ld_f, eps_set = sem("ld_d"), sem("ld_f"), sem("eps_set")
        ld_keys = [sem("ld_keys0"), sem("ld_keys1")]
        e_ld, e_sel, e_vs = sem("e_ld"), sem("e_sel"), sem("e_vs")
        z_clear = sem("z_clear")
        ctx_h = at(154, "ctx_h", 1024, F32R)[0:64, :]
        ctx_l = at(158, "ctx_l", 1024, F32R)[0:64, :]
        ctx_parts = nc.dram_tensor("ctx_parts", (2, CD, T), F32, kind="Internal").ap()
        ctx_split, ctx_stored = sem("ctx_split"), sem("ctx_stored")
        ctxT = SC[0:64, 0:1024]
        wkT = small[0:64, 0:64]
        bk_col = small[0:64, 64:65]
        bk_row = small[:, 128:192]
        xg_row = sb("xg_row", [P, 512])
        wr = small[:, 192:208].rearrange("p (k e) -> p k e", k=KT)
        temp = small[:, 208:209]
        bw1 = small[:, 256:288].rearrange("p (k e) -> p k e", k=KT)
        bb1 = small[:, 288:304]
        ob1 = small[:, 304:560]
        ctx_s = sb("ctx_s", [P, NT, CD])
        mv = sb("mv", [P, NT, 2])
        stats = sb("stats", [P, NT, 6])
        rstd = sb("rstd", [P, NT])
        rin = sb("rin", [P, NT])
        xn = sb("xn", [P, 2, 256])

        c_raw = v3(at(136, "c_raw", 3 * 1536), 3, 1536)
        ld_exp = [sem(f"ld_exp{j}") for j in range(3)]

        def bcast_row(a, n):
            return a.rearrange("(o n) -> o n", o=1).to_broadcast([P, n])

        N_A, N_B, N_MOE, N_D = 4, 7, 2, 4

        with nc.Block() as block:
            @block.sync
            def _(sp):
                sp.dma_start(x[:], ins["x"]).then_inc(ld_x, 16)
                sp.dma_start(consts[:], ins["consts"]).then_inc(ld_c, 16)
                for k in range(KT):
                    sp.dma_start(a_w[:, k, :], ins["wqkvg"][:, k, :]).then_inc(ld_w, 16)
                sp.dma_start(rot_tab, ins["rot_tab"]).then_inc(ld_a, 16)
                sp.dma_start(wo0, ins["wo0"]).then_inc(ld_a, 16)
                sp.dma_start(gn_w, bcast_row(ins["gn_w"], 256)).then_inc(ld_a, 16)
                sp.dma_start(gn_b, bcast_row(ins["gn_b"], 256)).then_inc(ld_a, 16)
                sp.dma_start(ctxT, ins["ctxT"]).then_inc(ld_b, 16)
                sp.dma_start(wkT, ins["wkT"]).then_inc(ld_b, 16)
                sp.dma_start(bk_col, ins["bk"].rearrange("(n o) -> n o", o=1)).then_inc(ld_b, 16)
                sp.dma_start(bk_row, bcast_row(ins["bk"], 64)).then_inc(ld_b, 16)
                sp.dma_start(xg_row[:, 0:256], bcast_row(ins["xg"], 256)).then_inc(ld_b, 16)
                sp.dma_start(xg_row[:, 256:512], bcast_row(ins["xb"], 256)).then_inc(ld_b, 16)
                sp.dma_start(ctx_s[:], ins["ctx_s"]).then_inc(ld_b, 16)
                sp.dma_start(wr, ins["wr"]).then_inc(ld_moe, 16)
                sp.dma_start(temp, bcast_row(ins["temp"], 1)).then_inc(ld_moe, 16)

            @block.vector
            def _(dve):
                nc.vector.memset(eps_t[:, 0:1], LN_EPS)
                nc.vector.memset(eps_t[:, 1:2], 1e-6).then_inc(eps_set, 1)

        ln_var, ln_sd, ln_xn, ln_turned, ln_out, ln_low = (sem(f"ln_{n}") for n in ("var", "sd", "xn", "turned", "out", "low"))
        ln_round = [0, 0]

        def layer_norm(ph, parity=False, split=False, beside=None):
            n0 = ln_round[0]
            n0_low = ln_round[1]
            ln_round[0] += 1
            ln_round[1] += split
            tr0, ev0, low0 = n0 * NT, n0 * NT // 2, n0_low * NT // 2
            dst = hTh if split else hT
            with nc.Block() as block:
                @block.vector
                def _(dve):
                    if ph == "A":
                        dve.wait_ge(ld_x, 16)
                    for i in range(NT):
                        nc.vector.bn_stats(stats[:, i, :], x[:, i, :]).then_inc(s_vec, 1)
                        chain["v"] += 1
                    dve.wait_ge(s_vec, chain["v"])
                    for i in range(NT):
                        last = nc.vector.bn_aggr(mv[:, i, :], stats[:, i, :])
                    last.then_inc(ln_var, 1)
                    dve.wait_ge(ln_sd, n0 + 1)
                    link(dve, "v", s_vec, nc.vector.reciprocal(rstd[:], rin[:]))
                    for i in range(NT):
                        if i >= 2:
                            dve.wait_ge(ln_turned, tr0 + i - 1)
                        nc.vector.tensor_scalar(xn[:, i % 2, :], x[:, i, :], mv[:, i, 0:1], rstd[:, i:i + 1],
                                                ALU.subtract, ALU.mult).then_inc(ln_xn, 1)
                    if split:
                        for j in range(NT // 2):
                            t = slice(j * 256, (j + 1) * 256)
                            dve.wait_ge(ln_out, ev0 + j + 1)
                            nc.vector.tensor_tensor(hTl[:, :, t], v3(PS[:, j, :], KT, 256), hTh[:, :, t].bitcast(F32),
                                                    ALU.subtract).then_inc(ln_low, 1)
                        dve.wait_ge(ln_low, low0 + NT // 2)

                if beside:
                    beside(block)
                if ph == "A":
                    @block.gpsimd
                    def _(pool):
                        for k in range(KT):
                            pool.wait_ge(a_whi, k + 1)
                            nc.gpsimd.tensor_tensor(a_wl_t[:, k, :], a_w[:, k, :], a_wh_t[:, k, :].bitcast(F32),
                                                    ALU.subtract).then_inc(a_wl, 1)

                @block.scalar
                def _(act):
                    if ph == "A":
                        act.wait_ge(eps_set, 1)
                    act.wait_ge(ln_var, n0 + 1)
                    nc.scalar.activation(rin[:], mv[:, :, 1], ACT.Sqrt, bias=eps_t[:, 0:1]).then_inc(ln_sd, 1)
                    if ph == "A":
                        act.wait_ge(ld_w, 16 * KT)
                        for k in range(KT):
                            nc.scalar.copy(a_wh_t[:, k, :], a_w[:, k, :]).then_inc(a_whi, 1)
                    for j in range(NT // 2):
                        act.wait_ge(ln_turned, tr0 + 2 * j + 2)
                        nc.scalar.copy(dst[:, :, j * 256:(j + 1) * 256], v3(PS[:, j, :], KT, 256)).then_inc(ln_out, 1)
                    act.wait_ge(ln_out, ev0 + NT // 2)

                @block.tensor
                def _(pe):
                    if ph == "A":
                        pe.wait_ge(ld_c, 16)
                    for i in range(NT):
                        pe.wait_ge(ln_xn, tr0 + i + 1)
                        for k in range(KT):
                            src = xn[:, i % 2, k::2] if parity else xn[:, i % 2, k * 128:(k + 1) * 128]
                            o = k * 256 + (i % 2) * 128
                            last = nc.tensor.transpose(PS[:, i // 2, o:o + 128], src, ident)
                        last.then_inc(ln_turned, 1)

        layer_norm("A", split=True)
        QT = v3(at(32, "a_QT", 8192, F32R), 8, T)
        KTs = v3(at(64, "a_KT", 8192, F32R), 8, T)
        v0 = v3(at(96, "a_v", 2048), NT, 256)
        sgate = v3(at(104, "a_gate", 2048), NT, 256)
        Qs = v3(at(120, "a_Qs", 2048, F32R), 2, 1024)
        Ks = v3(at(136, "a_Ks", 2048, F32R), 2, 1024)
        rot = v3(at(144, "a_rotated", 1024), 2, 512)
        by_cos = at(148, "a_cos", 512)
        by_sin = at(150, "a_sin", 512)
        identr = at(152, "a_identr", 128, F32R)
        a_qk, a_vg, a_vgev, a_prod, a_rot, a_hi, a_low, a_pad, a_tn, a_qtev, a_ktev = (
            sem(f"a_{n}") for n in ("qk", "vg", "vgev", "prod", "rot", "hi", "low", "pad", "tn", "qtev", "ktev"))
        a_s, a_sev, a_pv, a_yread, a_yn = sem("a_s"), sem("a_sev"), sem("a_pv"), sem("a_yread"), sem("a_yn")
        a_var, a_sd, a_z, a_zt, a_zth, a_ztl, a_o, a_xadd = (sem(f"a_{n}") for n in ("var", "sd", "z", "zt", "zth", "ztl", "o", "xadd"))
        with nc.Block() as block:
            @block.gpsimd
            def _(pool):
                for stack in (Qs, Ks):
                    pad = stack.bitcast(F32).rearrange("p s (n c) -> p (s n) c", c=64)[:, :, 48:64]
                    nc.gpsimd.memset(pad, 0.0).then_inc(a_pad, 1)
                pool.wait_ge(ld_a, 16 * N_A)
                nc.gpsimd.tensor_copy(woh.rearrange("p k n -> p (k n)"), wo0.rearrange("p k n -> p (k n)")).then_inc(a_wo, 1)
                pool.wait_ge(a_wo, 1)
                nc.gpsimd.tensor_tensor(wol.rearrange("p k n -> p (k n)"), wo0.rearrange("p k n -> p (k n)"),
                                        woh.bitcast(F32).rearrange("p k n -> p (k n)"), ALU.subtract).then_inc(a_wo, 1)

            @block.tensor
            def _(pe):
                pe.wait_ge(a_wl, KT)

                def project(i):
                    tok = slice(i * 128, (i + 1) * 128)
                    for j, done in enumerate((a_qk, a_vg)):
                        if i >= 2:
                            if j == 0:
                                pe.wait_ge(a_prod, 3 * (i - 1))
                            else:
                                pe.wait_ge(a_vgev, 2 * (i - 1))
                        col = slice(j * 512, (j + 1) * 512)
                        for k in range(KT):
                            last = mm3(PS[:, 2 * j + i % 2, :], (hTh[:, k, tok], hTl[:, k, tok]),
                                       (a_wh_t[:, k, col], a_wl_t[:, k, col]), k == 0, k == 1)
                        last.then_inc(done, 1)

                def turn(i):
                    for j, (stack, ev) in enumerate(((Qs, a_qtev), (Ks, a_ktev))):
                        pe.wait_ge(a_low, 2 * i + j + 1)
                        for half in range(2):
                            if i >= 1:
                                pe.wait_ge(ev, 2 * (i - 1) + half + 1)
                            for g in range(4):
                                o = (4 * half + g) * 128
                                last = nc.tensor.matmul(PS[:, 4 + 2 * j + half, g * 128:(g + 1) * 128], stack[:, i % 2, o:o + 128],
                                                        identr, start=True, stop=True)
                            last.then_inc(a_tn, 1)

                for i in range(NT + 1):
                    if i < NT:
                        project(i)
                    if i == 1:
                        pe.wait_ge(a_pad, 3)
                    if i >= 1:
                        turn(i - 1)

            @block.scalar
            def _(act):
                for i in range(NT + 1):
                    if i < NT:
                        r = lambda j: rot[:, i % 2, j * 256:(j + 1) * 256].rearrange("p (n o d) -> p n o d", o=1, d=HD0).to_broadcast([P, NH0, 2, HD0])
                        st = lambda stack: stack[:, i % 2, :].rearrange("p (n c d) -> p n c d", c=4, d=HD0)
                        for j, dst in enumerate((st(Qs)[:, :, 0:3:2, :], st(Ks)[:, :, 0:2, :])):
                            act.wait_ge(a_rot, 2 * i + j + 1)
                            if i >= 2:
                                act.wait_ge(a_tn, 4 * (i - 1))
                            nc.scalar.copy(dst, r(j)).then_inc(a_hi, 1)
                    if i >= 1:
                        for half in range(2):
                            act.wait_ge(a_tn, 4 * (i - 1) + half + 1)
                            nc.scalar.copy(QT[:, 4 * half:4 * half + 4, (i - 1) * 128:i * 128], v3(PS[:, 4 + half, :], 4, 128)).then_inc(a_qtev, 1)
                    if i < NT:
                        act.wait_ge(a_vg, i + 1)
                        nc.scalar.copy(v0[:, i, :], PS[:, 2 + i % 2, 0:256]).then_inc(a_vgev, 1)
                        nc.scalar.activation(sgate[:, i, :], PS[:, 2 + i % 2, 256:512], ACT.Silu).then_inc(a_vgev, 1)
                act.wait_ge(a_vgev, 2 * NT)
                act.wait_ge(a_qtev, 2 * NT)

            @block.vector
            def _(dve):
                nc.vector.tensor_copy(identr, ident).then_inc(a_pad, 1)
                dve.wait_ge(ld_a, 16 * N_A)
                for i in range(NT + 1):
                    if i < NT:
                        qk = v4(PS[:, i % 2, :], 2, 2, 128)
                        sins = v4(rot_tab[:, i % 2, 512:1024], 2, 2, 128)
                        prod = v4(by_sin, 2, 2, 128)
                        dve.wait_ge(a_qk, i + 1)
                        dve.wait_ge(a_rot, 2 * i) if i else None
                        nc.vector.tensor_tensor(by_cos, PS[:, i % 2, :], rot_tab[:, i % 2, 0:512], ALU.mult).then_inc(a_prod, 1)
                        for eo in range(2):
                            nc.vector.tensor_tensor(prod[:, :, eo, :], qk[:, :, 1 - eo, :], sins[:, :, eo, :], ALU.mult).then_inc(a_prod, 1)
                        dve.wait_ge(a_prod, 3 * (i + 1))
                        for j in range(2):
                            c = slice(j * 256, (j + 1) * 256)
                            src = lambda ap: ap[:, c].rearrange("p (e n f) -> p e n f", e=2, n=NH0)
                            nc.vector.tensor_tensor(rot[:, i % 2, c].rearrange("p (n e f) -> p e n f", e=2, n=NH0), src(by_cos), src(by_sin),
                                                    ALU.add).then_inc(a_rot, 1)
                    if i >= 1:
                        for half in range(2):
                            dve.wait_ge(a_tn, 4 * (i - 1) + half + 3)
                            nc.vector.tensor_copy(KTs[:, 4 * half:4 * half + 4, (i - 1) * 128:i * 128], v3(PS[:, 6 + half, :], 4, 128)).then_inc(a_ktev, 1)
                    if i < NT:
                        for j, (stack, low) in enumerate(((Qs, 1), (Ks, 2))):
                            st = stack[:, i % 2, :].rearrange("p (n c d) -> p n c d", c=4, d=HD0)
                            dve.wait_ge(a_hi, 2 * i + j + 1)
                            nc.vector.tensor_tensor(st[:, :, low, :], rot[:, i % 2, j * 256:(j + 1) * 256].rearrange("p (n d) -> p n d", d=HD0),
                                                    st[:, :, 0, :].bitcast(F32), ALU.subtract).then_inc(a_low, 1)
                dve.wait_ge(a_ktev, 2 * NT)

        sT = v3(at(0, "a_sT", 4 * 384), 4, 384)
        yc, ysq = at(6, "a_yc", 512), at(8, "a_ysq", 512)
        z0 = v3(at(10, "a_z0", 512), 2, 256)
        zTh = v3(at(12, "a_zTh", 512, F32R), KT, 256)
        zTl = v3(at(14, "a_zTl", 512, F32R), KT, 256)
        ysmall = at(16, "a_ysmall", 160)
        ysum, ymean, yvar, ysd, yrs = (ysmall[:, 32 * j:32 * j + 32] for j in range(5))
        with nc.Block() as block:
            n3 = lambda ap: ap.rearrange("p (n d) -> p n d", d=HD0)

            @block.gpsimd
            def _(pool):
                both = lambda ap: ap.rearrange("p (o f) -> p o f", o=1).to_broadcast([P, 2, 256])
                for b in range(B):
                    """Affine and gate of the normed heads."""
                    pool.wait_ge(a_yn, b + 1)
                    link(pool, "p", s_pool, nc.gpsimd.tensor_tensor(v3(yc, 2, 256), v3(yc, 2, 256), both(gn_w), ALU.mult))
                    link(pool, "p", s_pool, nc.gpsimd.tensor_tensor(v3(yc, 2, 256), v3(yc, 2, 256), both(gn_b), ALU.add))
                    if b >= 1:
                        pool.wait_ge(a_zt, b)
                    nc.gpsimd.tensor_tensor(z0, v3(yc, 2, 256), sgate[:, 2 * b:2 * b + 2, :], ALU.mult).then_inc(a_z, 1)

            @block.tensor
            def _(pe):
                def scores(b, n):
                    g, r = n // 2, n % 4
                    row = slice(64 * (n % 2), 64 * (n % 2) + 48)
                    m = b * NH0 + n
                    if m >= 4:
                        pe.wait_ge(a_sev, m - 3)
                    nc.tensor.matmul(PS[:, r, 0:256], KTs[row, g, b * 256:b * 256 + 128], QT[row, g, b * 256:b * 256 + 256],
                                     start=True, stop=True)
                    nc.tensor.matmul(PS[:, r, 256:384], KTs[row, g, b * 256 + 128:b * 256 + 256],
                                     QT[row, g, b * 256 + 128:b * 256 + 256], start=True, stop=True).then_inc(a_s, 1)

                def mix(b, n):
                    m = b * NH0 + n
                    pe.wait_ge(a_sev, m + 1)
                    if n == 0 and b >= 2:
                        pe.wait_ge(a_yread, b - 1)
                    y = v3(PS[:, 4 + b % 2, :], 2, 256)
                    col = slice(16 * n, 16 * n + 16)
                    nc.tensor.matmul(y[:, 0, col], sT[:, n % 4, 0:128], v0[:, 2 * b, col], start=True, stop=True)
                    nc.tensor.matmul(y[:, 1, col], sT[:, n % 4, 128:256], v0[:, 2 * b, col], start=True, stop=False)
                    nc.tensor.matmul(y[:, 1, col], sT[:, n % 4, 256:384], v0[:, 2 * b + 1, col],
                                     start=False, stop=True).then_inc(a_pv, 1)

                def turn(b):
                    pe.wait_ge(a_z, b + 1)
                    if b >= 1:
                        pe.wait_ge(a_ztl, b)
                    for i in range(2):
                        for k in range(KT):
                            last = nc.tensor.transpose(PS[:, 6, k * 256 + i * 128:k * 256 + i * 128 + 128],
                                                       z0[:, i, k * 128:(k + 1) * 128], ident)
                    last.then_inc(a_zt, 1)

                def project(b):
                    pe.wait_ge(a_ztl, b + 1)
                    if b == 0:
                        pe.wait_ge(a_wo, 2)
                    else:
                        pe.wait_ge(a_xadd, b)
                    for i in range(2):
                        t = slice(i * 128, (i + 1) * 128)
                        for k in range(KT):
                            last = mm3(PS[:, 7, i * 256:(i + 1) * 256], (zTh[:, k, t], zTl[:, k, t]), (woh[:, k, :], wol[:, k, :]),
                                       k == 0, k == 1)
                    last.then_inc(a_o, 1)

                LAG = 3
                total = B * NH0
                for m in range(total + LAG):
                    if m < total:
                        scores(m // NH0, m % NH0)
                    if m >= LAG:
                        mix((m - LAG) // NH0, (m - LAG) % NH0)
                    if m > NH0 and m % NH0 == 12:
                        turn(m // NH0 - 1)
                    if m > NH0 and m % NH0 == 14:
                        project(m // NH0 - 1)
                turn(B - 1)
                project(B - 1)

            @block.scalar
            def _(act):
                for b in range(B):
                    act.wait_ge(a_var, b + 1)
                    nc.scalar.activation(ysd, yvar, ACT.Sqrt, bias=eps_t[:, 0:1], scale=1.0 / HD0).then_inc(a_sd, 1)
                    act.wait_ge(a_zt, b + 1)
                    if b >= 1:
                        act.wait_ge(a_o, b)
                    nc.scalar.copy(zTh, v3(PS[:, 6, :], KT, 256)).then_inc(a_zth, 1)

            @block.vector
            def _(dve):
                wide = lambda ap: ap.rearrange("p (n o) -> p n o", o=1).to_broadcast([P, 32, HD0])

                def mask(m):
                    dve.wait_ge(a_s, m + 1)
                    if m >= 4:
                        dve.wait_ge(a_pv, m - 3)
                    nc.vector.tensor_tensor(sT[:, m % 4, :], PS[:, m % 4, 0:384], mask_ret, ALU.mult).then_inc(a_sev, 1)

                def means(b):
                    dve.wait_ge(a_pv, (b + 1) * NH0)
                    link(dve, "v", s_vec, nc.vector.tensor_reduce(ysum, n3(PS[:, 4 + b % 2, :]), AX.X, ALU.add))
                    link(dve, "v", s_vec, nc.vector.tensor_scalar(ymean, ysum, 1.0 / HD0, None, ALU.mult))

                def centre(b):
                    if b >= 1:
                        dve.wait_ge(a_z, b)
                    nc.vector.tensor_tensor(n3(yc), n3(PS[:, 4 + b % 2, :]), wide(ymean), ALU.subtract).then_inc(a_yread, 1)

                def variances(b):
                    dve.wait_ge(a_yread, b + 1)
                    link(dve, "v", s_vec, nc.vector.tensor_tensor(ysq, yc, yc, ALU.mult))
                    nc.vector.tensor_reduce(yvar, n3(ysq), AX.X, ALU.add).then_inc(a_var, 1)

                def normed(b):
                    dve.wait_ge(a_sd, b + 1)
                    link(dve, "v", s_vec, nc.vector.reciprocal(yrs, ysd))
                    nc.vector.tensor_tensor(n3(yc), n3(yc), wide(yrs), ALU.mult).then_inc(a_yn, 1)

                def low(b):
                    dve.wait_ge(a_zth, b + 1)
                    nc.vector.tensor_tensor(zTl, v3(PS[:, 6, :], KT, 256), zTh.bitcast(F32), ALU.subtract).then_inc(a_ztl, 1)

                def add(b):
                    dve.wait_ge(a_o, b + 1)
                    nc.vector.tensor_tensor(x[:, 2 * b:2 * b + 2, :], x[:, 2 * b:2 * b + 2, :], v3(PS[:, 7, :], 2, 256),
                                            ALU.add).then_inc(a_xadd, 1)

                for m in range(B * NH0):
                    mask(m)
                    b, n = m // NH0 - 1, m % NH0
                    if b >= 0:
                        if n == 3:
                            means(b)
                        if n == 4:
                            centre(b)
                        if n == 5:
                            variances(b)
                        if n == 7:
                            normed(b)
                        if n == 13:
                            low(b)
                    if b >= 1 and n == 0:
                        add(b - 1)
                add(B - 2)
                means(B - 1)
                centre(B - 1)
                variances(B - 1)
                normed(B - 1)
                low(B - 1)
                add(B - 1)
                dve.wait_ge(a_xadd, B)

        layer_norm("B")
        kvT = SC[0:64, 1024:2048]
        kvs = R2[:, 0:512].rearrange("p (i d) -> p i d", d=CD)
        oT = R2[0:64, 512:1024].rearrange("p (a t) -> p a t", a=2)
        sim = v3(R2[:, 1024:2048], 4, 256)
        att = v3(R2[:, 2048:3072], 4, 256)
        bstat = v3(R2[:, 3072:3072 + 48], NT, 6)
        bmv = v3(R2[:, 3120:3136], NT, 2)
        bsd, brs, bmx, bsum, bri = (R2[:, 3136 + 8 * j:3144 + 8 * j] for j in range(5))
        b_kv, b_kvev, b_o, b_oev, b_sim, b_var, b_sd, b_norm, b_max, b_exp, b_read = (
            sem(f"b_{n}") for n in ("kv", "kvev", "o", "oev", "sim", "var", "sd", "norm", "max", "exp", "read"))
        with nc.Block() as block:
            @block.gpsimd
            def _(pool):
                pool.wait_ge(ld_b, 16 * N_B)
                nc.gpsimd.tensor_copy(ctx_h, ctxT).then_inc(ctx_split, 1)
                pool.wait_ge(ctx_split, 1)
                nc.gpsimd.tensor_tensor(ctx_l, ctxT, ctx_h.bitcast(F32), ALU.subtract).then_inc(ctx_split, 1)

            @block.sync
            def _(sp):
                for e in range(3):
                    sp.dma_start(c_raw[:, e, :], ins["wexp"][:, e, :]).then_inc(ld_exp[e], 16)
                sp.wait_ge(ctx_split, 2)
                sp.dma_start(ctx_parts[0], ctx_h.bitcast(F32)).then_inc(ctx_stored, 16)
                sp.dma_start(ctx_parts[1], ctx_l.bitcast(F32)).then_inc(ctx_stored, 16)

            @block.tensor
            def _(pe):
                pe.wait_ge(ld_b, 16 * N_B)
                for c in range(2):
                    nc.tensor.matmul(PS[0:64, c, :], wkT, ctxT[:, c * 512:(c + 1) * 512], start=True, stop=True).then_inc(b_kv, 1)
                for i in range(NT):
                    last = nc.tensor.matmul(PS[:, 2, i * 64:(i + 1) * 64], ctxT[:, i * 128:(i + 1) * 128], wkT, start=True, stop=True)
                last.then_inc(b_kv, 1)
                pe.wait_ge(b_kvev, 3)
                for b in range(B):
                    if b >= 2:
                        pe.wait_ge(b_oev, b - 1)
                    for k in range(KT):
                        last = nc.tensor.matmul(PS[0:64, b % 2, 0:256], kvs[:, 2 * b + k, :], hT[:, k, b * 256:(b + 1) * 256],
                                                start=k == 0, stop=k == 1)
                    last.then_inc(b_o, 1)
                    pe.wait_ge(b_oev, b + 1)
                    for i in range(2):
                        nc.tensor.matmul(PS[:, 4 + b, i * 256:(i + 1) * 256], oT[:, b % 2, i * 128:(i + 1) * 128],
                                         kvT[:, b * 256:(b + 1) * 256], start=True, stop=True).then_inc(b_sim, 1)

            @block.scalar
            def _(act):
                for c in range(2):
                    act.wait_ge(b_kv, c + 1)
                    nc.scalar.activation(kvT[:, c * 512:(c + 1) * 512], PS[0:64, c, :], ACT.Identity, bias=bk_col).then_inc(b_kvev, 1)
                for b in range(B):
                    act.wait_ge(b_o, b + 1)
                    if b >= 2:
                        act.wait_ge(b_sim, 2 * (b - 1))
                    nc.scalar.activation(oT[:, b % 2, :], PS[0:64, b % 2, 0:256], ACT.Copy, scale=1.0 / 16.0).then_inc(b_oev, 1)
                act.wait_ge(b_var, 1)
                nc.scalar.activation(bsd, bmv[:, :, 1], ACT.Sqrt, bias=eps_t[:, 1:2]).then_inc(b_sd, 1)
                for i in range(NT):
                    act.wait_ge(b_max, i + 1)
                    if i >= 4:
                        act.wait_ge(b_read, i - 3)
                    nc.scalar.activation(att[:, i % 4, :], sim[:, i % 4, :], ACT.Exp, bias=bmx[:, i:i + 1],
                                         accum_out=bsum[:, i:i + 1]).then_inc(b_exp, 1)

            @block.vector
            def _(dve):
                dve.wait_ge(b_kv, 3)
                nc.vector.tensor_tensor(kvs, PS[:, 2, :].rearrange("p (i d) -> p i d", d=CD),
                                        bk_row.rearrange("p (o d) -> p o d", o=1).to_broadcast([P, NT, CD]), ALU.add).then_inc(b_kvev, 1)
                for i in range(NT):
                    dve.wait_ge(b_sim, 2 * (i // 2) + 2)
                    link(dve, "v", s_vec, nc.vector.bn_stats(bstat[:, i, :], PS[:, 4 + i // 2, (i % 2) * 256:(i % 2) * 256 + 256]))
                    last = nc.vector.bn_aggr(bmv[:, i, :], bstat[:, i, :])
                last.then_inc(b_var, 1)
                dve.wait_ge(b_sd, 1)
                link(dve, "v", s_vec, nc.vector.reciprocal(brs, bsd))

                def finish(i):
                    dve.wait_ge(b_exp, i + 1)
                    link(dve, "v", s_vec, nc.vector.reciprocal(bri[:, i:i + 1], bsum[:, i:i + 1]))
                    nc.vector.scalar_tensor_tensor(x[:, i, :], att[:, i % 4, :], bri[:, i:i + 1], x[:, i, :],
                                                   ALU.mult, ALU.add).then_inc(b_read, 1)

                for i in range(NT):
                    s = sim[:, i % 4, :]
                    if i >= 4:
                        dve.wait_ge(b_exp, i - 3)
                    link(dve, "v", s_vec, nc.vector.tensor_scalar(s, PS[:, 4 + i // 2, (i % 2) * 256:(i % 2) * 256 + 256],
                                                                  bmv[:, i, 0:1], brs[:, i:i + 1], ALU.subtract, ALU.mult))
                    link(dve, "v", s_vec, nc.vector.tensor_tensor(s, s, xg_row[:, 0:256], ALU.mult))
                    link(dve, "v", s_vec, nc.vector.tensor_tensor(s, s, xg_row[:, 256:512], ALU.add))
                    link(dve, "v", s_vec, nc.vector.tensor_reduce(rin[:, i:i + 1], s, AX.X, ALU.max))
                    nc.vector.tensor_scalar(bmx[:, i:i + 1], rin[:, i:i + 1], -1.0, None, ALU.mult).then_inc(b_max, 1)
                    if i >= 2:
                        finish(i - 2)
                finish(NT - 2)
                finish(NT - 1)
                dve.wait_ge(b_read, NT)

        layer_norm("C", split=True)
        c_wh = v3(at(0, "c_wh", 2 * 1536, F32R), 2, 1536)
        c_wl = v3(at(12, "c_wl", 2 * 1536, F32R), 2, 1536)
        CR = at(24, "CR", 2048)
        RT = v3(CR[:, 0:768], 12, 64)
        cmp8 = CR[:, 768:1280]
        cmp8b = CR[:, 1280:1792]
        hidf = v3(at(32, "c_hidf", 1024), 2, 512)
        hidh = v4(at(36, "c_hidh", 2048, F32R), 2, KT, 512)
        hidl = v4(at(44, "c_hidl", 2048, F32R), 2, KT, 512)
        sgc = v3(at(52, "c_sg", 1024), 2, 512)
        inv_t = small[:, 209:210]
        c_z, c_dist, c_w = (sem(f"c_{n}") for n in ("z", "dist", "w"))
        c_g, c_silu, c_hid, c_high, c_low, c_dn, c_add, c_temp = (
            sem(f"c_{n}") for n in ("g", "silu", "hid", "high", "low", "dn", "add", "temp"))
        c_zread, c_whi, c_wlo = sem("c_zread"), sem("c_whi"), sem("c_wlo")

        def cw(part, e):
            return [v3(part[:, e % 2, j * 512:(j + 1) * 512], KT, 256) for j in range(3)]

        c_wr = sem("c_wr")
        wrh = sb("wrh", [P, KT, E0], F32R)[:, :, :]
        wrl = sb("wrl", [P, KT, E0], F32R)[:, :, :]
        d_raw = v3(at(60, "d_raw", 3 * 1280), 3, 1280)
        qkvb = at(75, "qkvb", 6144).rearrange("p (n w) -> p n w", n=NH1)
        ld_head = [sem(f"ld_head{j}") for j in range(3)]
        CENTER = float(np.float32(1.0 / np.e))
        LOWER = float(np.float32(0.5 - np.log(4.0 / 3.0)))
        with nc.Block() as block:
            cunits = [(e, c) for e in range(E0) for c in range(2)]
            NC = len(cunits)

            @block.gpsimd
            def _(pool):
                for e in range(E0):
                    pool.wait_ge(c_whi, e + 1)
                    nc.gpsimd.tensor_tensor(c_wl[:, e % 2, :], c_raw[:, e % 3, :], c_wh[:, e % 2, :].bitcast(F32),
                                            ALU.subtract).then_inc(c_wlo, 1)

            @block.sync
            def _(sp):
                for e in range(3, E0):
                    sp.wait_ge(c_whi, e - 2)
                    sp.wait_ge(c_wlo, e - 2)
                    sp.dma_start(c_raw[:, e % 3, :], ins["wexp"][:, e, :]).then_inc(ld_exp[e % 3], 16)
                for n in range(3):
                    sp.dma_start(d_raw[:, n, :], ins["w1"][:, n, :]).then_inc(ld_head[n], 16)
                sp.dma_start(qkvb.rearrange("p n w -> p (n w)"), bcast_row(ins["qkvb"], 6144)).then_inc(ld_d, 16)
                sp.dma_start(bw1, ins["bw1"]).then_inc(ld_d, 16)
                sp.dma_start(bb1, bcast_row(ins["bb1"], 16)).then_inc(ld_d, 16)
                sp.dma_start(ob1, bcast_row(ins["ob1"], 256)).then_inc(ld_d, 16)

            @block.tensor
            def _(pe):
                pe.wait_ge(c_wr, 1)
                for i in range(NT):
                    for k in range(KT):
                        tok = slice(i * 128, (i + 1) * 128)
                        last = mm3(PS[:, 7, i * 8:(i + 1) * 8], (hTh[:, k, tok], hTl[:, k, tok]), (wrh[:, k, :], wrl[:, k, :]),
                                   k == 0, k == 1)
                last.then_inc(c_z, 1)

                def up(u):
                    e, c = cunits[u]
                    for m in range(KT):
                        v = 2 * u + m
                        if c == 0:
                            pe.wait_ge(c_wlo, e + 1)
                        if v >= 2:
                            pe.wait_ge(c_hid, v - 1)
                        for j in range(2):
                            for k in range(KT):
                                cols, tok = slice(m * 128, (m + 1) * 128), slice(c * 512, (c + 1) * 512)
                                last = mm3(PS[:, 2 * (v % 2) + j, :], (cw(c_wh, e)[j][:, k, cols], cw(c_wl, e)[j][:, k, cols]),
                                           (hTh[:, k, tok], hTl[:, k, tok]), k == 0, k == 1)
                            last.then_inc(c_g, 1)

                def down(u):
                    e, c = cunits[u]
                    pe.wait_ge(c_low, 2 * u + 2)
                    if u == 1:
                        pe.wait_ge(c_zread, 1)
                    if u >= 2:
                        pe.wait_ge(c_add, 4 * (u - 1))
                    for i in range(4):
                        for k in range(KT):
                            tok = slice(i * 128, (i + 1) * 128)
                            last = mm3(PS[:, 4 + 2 * (u % 2) + i // 2, (i % 2) * 256:(i % 2) * 256 + 256],
                                       (hidh[:, u % 2, k, tok], hidl[:, u % 2, k, tok]),
                                       (cw(c_wh, e)[2][:, k, :], cw(c_wl, e)[2][:, k, :]), k == 0, k == 1)
                        last.then_inc(c_dn, 1)

                up(0)
                for u in range(1, len(cunits)):
                    up(u)
                    down(u - 1)
                down(len(cunits) - 1)

            @block.scalar
            def _(act):
                def split(e):
                    act.wait_ge(ld_exp[e % 3], 16 * (e // 3 + 1))
                    if e >= 2:
                        act.wait_ge(c_dn, 4 * 2 * (e - 1))
                    nc.scalar.copy(c_wh[:, e % 2, :], c_raw[:, e % 3, :]).then_inc(c_whi, 1)

                def high(v):
                    act.wait_ge(c_hid, v + 1)
                    u = v // 2
                    if u >= 2:
                        act.wait_ge(c_dn, 4 * (u - 1))
                    nc.scalar.copy(hidh[:, u % 2, v % 2, :], hidf[:, v % 2, :]).then_inc(c_high, 1)

                split(0)
                split(1)
                act.wait_ge(c_temp, 1)
                act.wait_ge(c_z, 1)
                nc.scalar.activation(RT[:, 0, :], PS[:, 7, 0:64], ACT.Exp, scale=small[:, 210:211]).then_inc(c_zread, 1)
                act.wait_ge(c_dist, 1)
                nc.scalar.activation(RT[:, 2, :], RT[:, 1, :], ACT.Exp, scale=-10.0)
                nc.scalar.activation(RT[:, 3, :], RT[:, 1, :], ACT.Exp, scale=-1.0 / 0.3).then_inc(c_w, 1)
                for u in range(len(cunits)):
                    for m in range(KT):
                        v = 2 * u + m
                        act.wait_ge(c_g, 2 * v + 1)
                        if v >= 2:
                            act.wait_ge(c_hid, v - 1)
                        nc.scalar.activation(sgc[:, v % 2, :], PS[:, 2 * (v % 2), :], ACT.Silu).then_inc(c_silu, 1)
                        if v >= 1:
                            high(v - 1)
                    e, c = cunits[u]
                    if c == 0 and 1 <= e < E0 - 1:
                        split(e + 1)
                high(2 * NC - 1)

            @block.vector
            def _(dve):
                L = lambda inst: link(dve, "v", s_vec, inst)
                r = lambda j: RT[:, j, :]
                r3 = lambda j: RT[:, j, :].rearrange("p (i e) -> p i e", e=E0)
                dve.wait_ge(ld_moe, 16 * N_MOE)
                L(nc.vector.tensor_copy(wrh, wr))
                nc.vector.tensor_tensor(wrl, wr, wrh.bitcast(F32), ALU.subtract).then_inc(c_wr, 1)
                L(nc.vector.reciprocal(inv_t, temp))
                nc.vector.tensor_scalar(small[:, 210:211], inv_t, -1.0, None, ALU.mult).then_inc(c_temp, 1)
                dve.wait_ge(c_zread, 1)
                L(nc.vector.tensor_scalar(r(4), r(0), 1.0, None, ALU.add))
                L(nc.vector.reciprocal(r(5), r(4)))
                L(nc.vector.tensor_scalar(r(6), r(5), CENTER, None, ALU.subtract))
                nc.vector.scalar_tensor_tensor(r(1), r(6), -1.0, r(6), ALU.mult, ALU.max).then_inc(c_dist, 1)
                L(nc.vector.tensor_scalar(r(7), r(5), LOWER, None, ALU.is_ge))
                L(nc.vector.scalar_tensor_tensor(r(8), r(5), 0.5, r(7), ALU.is_le, ALU.mult))
                dve.wait_ge(c_w, 1)
                L(nc.vector.tensor_tensor(r(9), r(2), r(8), ALU.mult))
                w8 = small[:, 576:584]
                L(nc.vector.tensor_reduce(w8, r3(9), AX.X, ALU.add))
                no = small[:, 584:592]
                L(nc.vector.tensor_scalar(no, w8, 1e-8, None, ALU.is_lt))
                a4 = RT[:, 3, :].rearrange("p (i e o) -> p i e o", e=E0, o=1).to_broadcast([P, NT, E0, E0])
                b4 = RT[:, 3, :].rearrange("p (i o e) -> p i o e", e=E0, o=1).to_broadcast([P, NT, E0, E0])
                c4 = cmp8.rearrange("p (i e f) -> p i e f", e=E0, f=E0)
                d4 = cmp8b.rearrange("p (i e f) -> p i e f", e=E0, f=E0)
                L(nc.vector.tensor_tensor(c4, b4, a4, ALU.is_gt))
                L(nc.vector.tensor_tensor(d4, b4, a4, ALU.is_equal))
                for e in range(E0):
                    if e:
                        L(nc.vector.tensor_tensor(c4[:, :, e, 0:e], c4[:, :, e, 0:e], d4[:, :, e, 0:e], ALU.add))
                L(nc.vector.tensor_reduce(r(4), cmp8.rearrange("p (i f) -> p i f", f=E0), AX.X, ALU.add))
                L(nc.vector.scalar_tensor_tensor(r(6), r(4), 1.5, r(3), ALU.is_lt, ALU.mult))
                f8, fi = small[:, 592:600], small[:, 600:608]
                L(nc.vector.tensor_reduce(f8, r3(6), AX.X, ALU.add))
                L(nc.vector.tensor_scalar(f8, f8, 1e-8, None, ALU.max))
                L(nc.vector.reciprocal(fi, f8))
                wide = lambda a: a.rearrange("p (i o) -> p i o", o=1).to_broadcast([P, NT, E0])
                L(nc.vector.tensor_tensor(r3(6), r3(6), wide(fi), ALU.mult))
                L(nc.vector.tensor_tensor(r3(6), r3(6), wide(no), ALU.mult))
                L(nc.vector.tensor_scalar(no, no, -1.0, 1.0, ALU.mult, ALU.add))
                L(nc.vector.tensor_tensor(r3(9), r3(9), wide(no), ALU.mult))
                L(nc.vector.tensor_tensor(r(9), r(9), r(6), ALU.add))
                L(nc.vector.tensor_reduce(w8, r3(9), AX.X, ALU.add))
                L(nc.vector.tensor_scalar(w8, w8, 1e-8, None, ALU.max))
                L(nc.vector.reciprocal(fi, w8))
                L(nc.vector.tensor_tensor(r3(10), r3(9), wide(fi), ALU.mult))

                def product(v):
                    u, m = v // 2, v % 2
                    dve.wait_ge(c_silu, v + 1)
                    dve.wait_ge(c_g, 2 * v + 2)
                    if v >= 2:
                        dve.wait_ge(c_low, v - 1)
                    nc.vector.tensor_tensor(hidf[:, v % 2, :], PS[:, 2 * (v % 2) + 1, :], sgc[:, v % 2, :],
                                            ALU.mult).then_inc(c_hid, 1)

                def low(v):
                    u, m = v // 2, v % 2
                    dve.wait_ge(c_high, v + 1)
                    nc.vector.tensor_tensor(hidl[:, u % 2, m, :], hidf[:, v % 2, :], hidh[:, u % 2, m, :].bitcast(F32),
                                            ALU.subtract).then_inc(c_low, 1)

                def add(u):
                    e, c = cunits[u]
                    for i in range(4):
                        dve.wait_ge(c_dn, 4 * u + 2 * (i // 2) + 2)
                        ti = 4 * c + i
                        if u >= 2:
                            dve.wait_ge(c_add, 4 * (u - 2) + i + 1)
                        nc.vector.scalar_tensor_tensor(
                            x[:, ti, :], PS[:, 4 + 2 * (u % 2) + i // 2, (i % 2) * 256:(i % 2) * 256 + 256],
                            RT[:, 10, 8 * ti + e:8 * ti + e + 1], x[:, ti, :], ALU.mult, ALU.add).then_inc(c_add, 1)

                for v in range(2 * NC):
                    product(v)
                    if v >= 1:
                        low(v - 1)
                    if v % 2 == 1 and v >= 3:
                        add(v // 2 - 1)
                low(2 * NC - 1)
                add(NC - 1)
                dve.wait_ge(c_add, 4 * len(cunits))

        layer_norm("D", split=True)
        DS = at(0, "DS", 512).rearrange("p (a b) -> p a b", b=64)
        sel_raw = at(154, "sel_raw", 2048)
        sel = at(146, "sel", 2048, F32R).rearrange("p (j m) -> p j m", j=16)
        KZ = [at(kb, f"KZ{j}", 8192, F32R).rearrange("p (v g t) -> p v g t", v=KVH, g=GRP) for j, kb in enumerate((2, 114))]

        def clear_keys(pool, buf, done):
            nc.gpsimd.memset(buf.bitcast(F32), 0.0).then_inc(z_clear, 1)
            for g in range(GRP):
                pool.wait_ge(z_clear, done + 1 + g)
                nc.gpsimd.memset(buf[32 * g:32 * g + 32, :, g, :].bitcast(F32), 1.0).then_inc(z_clear, 1)
            pool.wait_ge(z_clear, done + 1 + GRP)

        def load_keys(sp, b, half):
            v = slice(4 * half, 4 * half + 4)
            for g in range(GRP):
                for j, part in enumerate((0, 0, 1)):
                    r0 = 32 * g + HD2 * j
                    sp.dma_start(KZ[b % 2][r0:r0 + HD2, v, g, :].bitcast(F32),
                                 ctx_parts[part].rearrange("(v d) t -> d v t", d=HD2)[:, v, b * 256:(b + 1) * 256]).then_inc(ld_keys[half], 16)

        dwh = v3(at(99, "d_wh", 2048, F32R), 2, 1024)
        dwl = v3(at(107, "d_wl", 2048, F32R), 2, 1024)
        owh = v3(at(115, "d_owh", 768, F32R), 3, 256)
        owl = v3(at(118, "d_owl", 768, F32R), 3, 256)
        tok_qkv = v4(at(121, "d_tok", 3072), 2, 4, 384)
        sq = v3(at(133, "d_sq", 1024), 4, 256)
        qT1, kT1, gate1, st1, zf = (v3(at(34 + 4 * j, f"d_act{j}", 1024), 2, 512) for j in range(5))
        zh = v3(at(137, "d_zh", 1024, F32R), 2, 512)
        zl = v3(at(141, "d_zl", 1024, F32R), 2, 512)
        ssum = DS[:, 2, 0:8]
        nrm = DS[:, 3, 0:8]
        floor = DS[:, 4, 16:24]
        inv = DS[:, 4, 8:16]
        scale_k = DS[:, 4, 0:4]
        beta_v = DS[:, 0:2, :].rearrange("p a b -> p (a b)")
        bwh = sb("bwh", [P, KT, NH1], F32R)[:, :, :]
        bwl = sb("bwl", [P, KT, NH1], F32R)[:, :, :]
        d_z, d_zp, d_t, d_tk, d_tq, d_g = (sem(f"d_{n}") for n in ("z", "zp", "t", "tk", "tq", "g"))
        d_qev, d_kev, d_gev, d_tev, d_sq, d_ss, d_nks, d_qs, d_kr = (
            sem(f"d_{n}") for n in ("qev", "kev", "gev", "tev", "sq", "ss", "nks", "qs", "kr"))
        d_s, d_sev, d_o, d_z1, d_zh, d_zl, d_acc, d_xadd, d_b1, d_b2 = (
            sem(f"d_{n}") for n in ("s", "sev", "o", "z1", "zh", "zl", "acc", "xadd", "b1", "b2"))
        d_x0, d_bw, d_whi, d_wlo = sem("d_x0"), sem("d_bw"), sem("d_whi"), sem("d_wlo")
        with nc.Block() as block:
            dunits = [(n, c) for n in range(NH1) for c in range(2)]
            ND = len(dunits)

            TILE, KEYS, QUERIES, SCORES, GATE, OUTS = (0, 1, 3, 5), 2, 4, 6, 7, 8

            def bank(s, turn):
                return PS[:, (9 * s + turn) % 4, :]

            @block.gpsimd
            def _(pool):
                clear_keys(pool, KZ[0], 0)

                def low(n):
                    pool.wait_ge(d_whi, 2 * n + 1)
                    nc.gpsimd.tensor_tensor(dwl[:, n % 2, :], d_raw[:, n % 3, 0:1024], dwh[:, n % 2, :].bitcast(F32),
                                            ALU.subtract).then_inc(d_wlo, 1)
                    pool.wait_ge(d_whi, 2 * n + 2)
                    nc.gpsimd.tensor_tensor(owl[:, n % 3, :], d_raw[:, n % 3, 1024:1280], owh[:, n % 3, :].bitcast(F32),
                                            ALU.subtract).then_inc(d_wlo, 1)

                low(0)
                low(1)
                for u in range(ND):
                    n, c = dunits[u]
                    if u >= 1:
                        pool.wait_ge(d_ss, u)
                    for i in range(4):
                        pool.wait_ge(d_tev, 4 * u + i + 1)
                        qk = tok_qkv[:, u % 2, i, 0:256]
                        nc.gpsimd.tensor_tensor(sq[:, i, :], qk, qk, ALU.mult).then_inc(d_sq, 1)
                    if c == 0 and 1 <= n < NH1 - 1:
                        low(n + 1)
                    if u == ND - 4:
                        pool.wait_ge(e_ld, 16)
                        nc.gpsimd.tensor_copy(sel.rearrange("p j m -> p (j m)"), sel_raw).then_inc(e_sel, 1)

            @block.sync
            def _(sp):
                for n in range(3, NH1):
                    sp.wait_ge(d_whi, 2 * (n - 2))
                    sp.wait_ge(d_wlo, 2 * (n - 2))
                    sp.dma_start(d_raw[:, n % 3, :], ins["w1"][:, n, :]).then_inc(ld_head[n % 3], 16)
                    if n == 3:
                        sp.wait_ge(z_clear, 5)
                        sp.wait_ge(ctx_stored, 32)
                        for half in range(2):
                            load_keys(sp, 0, half)
                        sp.dma_start(sel_raw, ins["sel"]).then_inc(e_ld, 16)

            @block.tensor
            def _(pe):
                pe.wait_ge(d_bw, 1)
                for i in range(NT):
                    for k in range(KT):
                        tok = slice(i * 128, (i + 1) * 128)
                        last = mm3(PS[:, 7, i * 16:(i + 1) * 16], (hTh[:, k, tok], hTl[:, k, tok]), (bwh[:, k, :], bwl[:, k, :]),
                                   k == 0, k == 1)
                last.then_inc(d_z, 1)

                def tile(s, i):
                    n, c = dunits[s]
                    tok = slice((4 * c + i) * 128, (4 * c + i + 1) * 128)
                    out = bank(s, TILE[i])[:, 0:384]
                    for k in range(KT):
                        w = [part[:, n % 2, 0:768].rearrange("p (j k d) -> p j k d", j=3, k=KT)[:, :, k, :] for part in (dwh, dwl)]
                        last = mm3(v3(out, 3, 128), (hTh[:, k, tok], hTl[:, k, tok]), w, k == 0, k == 1)
                    last.then_inc(d_t, 1)

                def gate(s):
                    n, c = dunits[s]
                    tok = slice(c * 512, (c + 1) * 512)
                    for k in range(KT):
                        o = 768 + k * 128
                        last = mm3(bank(s, GATE), (dwh[:, n % 2, o:o + 128], dwl[:, n % 2, o:o + 128]),
                                   (hTh[:, k, tok], hTl[:, k, tok]), k == 0, k == 1)
                    last.then_inc(d_g, 1)

                def turned(s, turn, j, done):
                    for i in range(4):
                        last = nc.tensor.transpose(bank(s, turn)[:, i * 128:(i + 1) * 128],
                                                   tok_qkv[:, (s - 1) % 2, i, j * 128:(j + 1) * 128], ident)
                    last.then_inc(done, 1)

                def out_proj(u):
                    n, c = dunits[u]
                    pe.wait_ge(d_zl, u + 1)
                    if u == 0:
                        pe.wait_ge(d_zp, 1)
                    for i in range(4):
                        t = slice(i * 128, (i + 1) * 128)
                        last = mm3(PS[:, 4 + 2 * c + i // 2, (i % 2) * 256:(i % 2) * 256 + 256], (zh[:, u % 2, t], zl[:, u % 2, t]),
                                   (owh[:, n % 3, :], owl[:, n % 3, :]), n == 0 and i % 2 == 0, n == NH1 - 1, skip_group_check=True)
                    last.then_inc(d_acc, 1)

                for s in range(ND + 2):
                    if s < ND:
                        pe.wait_ge(d_wlo, 2 * dunits[s][0] + 2)
                        if s >= 1:
                            pe.wait_ge(d_tev, 4 * s)
                        tile(s, 0)
                        if s >= 2:
                            pe.wait_ge(d_sev, 4 * (s - 1))
                        tile(s, 1)
                    if 1 <= s <= ND:
                        pe.wait_ge(d_tev, 4 * s)
                        pe.wait_ge(d_gev, s)
                        turned(s, KEYS, 1, d_tk)
                    if s >= 2:
                        out_proj(s - 2)
                    if s < ND:
                        if s >= 2:
                            pe.wait_ge(d_z1, s - 1)
                        tile(s, 2)
                    if 1 <= s <= ND:
                        pe.wait_ge(d_qs, s)
                        if s < ND:
                            pe.wait_ge(d_tev, 4 * s + 1)
                        turned(s, QUERIES, 0, d_tq)
                    if s < ND:
                        pe.wait_ge(d_tev, 4 * s + 2)
                        tile(s, 3)
                    if 1 <= s <= ND:
                        pe.wait_ge(d_kev, s)
                        pe.wait_ge(d_qev, s)
                        for i in range(4):
                            t = slice(i * 128, (i + 1) * 128)
                            last = nc.tensor.matmul(bank(s, SCORES)[:, t], kT1[:, (s - 1) % 2, t], qT1[:, (s - 1) % 2, t],
                                                    start=True, stop=True)
                        last.then_inc(d_s, 1)
                    if s < ND:
                        pe.wait_ge(d_tev, 4 * s + 3)
                        gate(s)
                    if 1 <= s <= ND:
                        for i in range(4):
                            t = slice(i * 128, (i + 1) * 128)
                            pe.wait_ge(d_sev, 4 * (s - 1) + i + 1)
                            last = nc.tensor.matmul(bank(s, OUTS)[:, t], tok_qkv[:, (s - 1) % 2, i, 256:384], st1[:, (s - 1) % 2, t],
                                                    start=True, stop=True)
                        last.then_inc(d_o, 1)

            @block.scalar
            def _(act):
                def split(n):
                    act.wait_ge(ld_head[n % 3], 16 * (n // 3 + 1))
                    if n >= 2:
                        act.wait_ge(d_g, 2 * (n - 1))
                    nc.scalar.copy(dwh[:, n % 2, :], d_raw[:, n % 3, 0:1024]).then_inc(d_whi, 1)
                    if n >= 3:
                        act.wait_ge(d_acc, 2 * (n - 2))
                    nc.scalar.copy(owh[:, n % 3, :], d_raw[:, n % 3, 1024:1280]).then_inc(d_whi, 1)

                def zhigh(u):
                    act.wait_ge(d_z1, u + 1)
                    if u >= 2:
                        act.wait_ge(d_acc, u - 1)
                    nc.scalar.copy(zh[:, u % 2, :], zf[:, u % 2, :]).then_inc(d_zh, 1)

                def root(u):
                    act.wait_ge(d_ss, u + 1)
                    if u >= 1:
                        act.wait_ge(d_kr, u)
                    nc.scalar.activation(nrm, ssum, ACT.Sqrt).then_inc(d_nks, 1)

                split(0)
                split(1)
                act.wait_ge(d_b1, 1)
                nc.scalar.activation(DS[:, 5:7, :], DS[:, 5:7, :], ACT.Exp, scale=-1.0).then_inc(s_act, 1)
                chain["a"] += 1
                act.wait_ge(s_act, chain["a"])
                nc.scalar.activation(DS[:, 5:7, :], DS[:, 5:7, :], ACT.Ln, bias=1.0).then_inc(d_b2, 1)
                for s in range(ND + 2):
                    if s >= 2:
                        zhigh(s - 2)
                    if 1 <= s <= ND:
                        root(s - 1)
                        act.wait_ge(d_tk, s)
                        if s >= 3:
                            act.wait_ge(d_s, s - 2)
                        nc.scalar.copy(kT1[:, (s - 1) % 2, :], bank(s, KEYS)).then_inc(d_kev, 1)
                    if s < ND and dunits[s][1] == 0 and 1 <= dunits[s][0] < NH1 - 1:
                        split(dunits[s][0] + 1)
                    if 1 <= s <= ND:
                        act.wait_ge(d_tq, s)
                        nc.scalar.copy(qT1[:, (s - 1) % 2, :], bank(s, QUERIES)).then_inc(d_qev, 1)
                    if s < ND:
                        act.wait_ge(d_g, s + 1)
                        if s >= 2:
                            act.wait_ge(d_z1, s - 1)
                        nc.scalar.activation(gate1[:, s % 2, :], bank(s, GATE), ACT.Silu).then_inc(d_gev, 1)

            @block.vector
            def _(dve):
                L = lambda inst: link(dve, "v", s_vec, inst)

                dve.wait_ge(ld_d, 16 * N_D)
                L(nc.vector.tensor_copy(bwh, bw1))
                nc.vector.tensor_tensor(bwl, bw1, bwh.bitcast(F32), ALU.subtract).then_inc(d_bw, 1)
                zb = beta_v.rearrange("p (i n) -> p i n", n=NH1)
                tmp = DS[:, 5:7, :].rearrange("p a b -> p (a b)").rearrange("p (i n) -> p i n", n=NH1)
                dve.wait_ge(d_z, 1)
                nc.vector.tensor_tensor(zb, PS[:, 7, 0:128].rearrange("p (i n) -> p i n", n=NH1),
                                        bb1.rearrange("p (o n) -> p o n", o=1).to_broadcast([P, NT, NH1]), ALU.add).then_inc(d_zp, 1)
                dve.wait_ge(d_zp, 1)
                nc.vector.scalar_tensor_tensor(tmp, zb, -1.0, zb, ALU.mult, ALU.max).then_inc(d_b1, 1)
                dve.wait_ge(d_b1, 1)
                L(nc.vector.tensor_scalar(zb, zb, 0.0, None, ALU.max))
                dve.wait_ge(d_b2, 1)
                L(nc.vector.tensor_tensor(zb, zb, tmp, ALU.add))

                def biased(u, i):
                    n, c = dunits[u]
                    dve.wait_ge(d_t, 4 * u + i + 1)
                    if i == 0 and u >= 2:
                        dve.wait_ge(d_o, u - 1)
                    nc.vector.tensor_tensor(tok_qkv[:, u % 2, i, :], bank(u, TILE[i])[:, 0:384], qkvb[:, n, :],
                                            ALU.add).then_inc(d_tev, 1)

                def summed(u):
                    dve.wait_ge(d_sq, 4 * (u + 1))
                    nc.vector.tensor_reduce(ssum, sq.rearrange("p i (j d) -> p (i j) d", d=HD1), AX.X, ALU.add).then_inc(d_ss, 1)

                def inverses(u):
                    n, c = dunits[u]
                    dve.wait_ge(d_nks, u + 1)
                    L(nc.vector.tensor_scalar(floor, nrm, 1e-12 * float(HD1) ** 0.5, None, ALU.max))
                    L(nc.vector.reciprocal(inv, floor))
                    if u >= 1:
                        dve.wait_ge(d_sev, 4 * u)
                    nc.vector.tensor_tensor(scale_k, inv.rearrange("p (i j) -> p i j", j=2)[:, :, 1], zb[:, 4 * c:4 * c + 4, n],
                                            ALU.mult).then_inc(d_kr, 1)
                    for i in range(4):
                        q = tok_qkv[:, u % 2, i, 0:128]
                        inst = nc.vector.tensor_scalar(q, q, inv[:, 2 * i:2 * i + 1], None, ALU.mult)
                    inst.then_inc(d_qs, 1)

                def masked(u):
                    dve.wait_ge(d_s, u + 1)
                    dve.wait_ge(d_kr, u + 1)
                    if u >= 2:
                        dve.wait_ge(d_o, u - 1)
                    for i in range(4):
                        t = slice(i * 128, (i + 1) * 128)
                        nc.vector.scalar_tensor_tensor(st1[:, u % 2, t], bank(u + 1, SCORES)[:, t], scale_k[:, i:i + 1], mask_chunk[:, t],
                                                       ALU.mult, ALU.mult).then_inc(d_sev, 1)

                def gated(u):
                    dve.wait_ge(d_o, u + 1)
                    dve.wait_ge(d_gev, u + 1)
                    if u >= 2:
                        dve.wait_ge(d_zl, u - 1)
                    nc.vector.tensor_tensor(zf[:, u % 2, :], bank(u + 1, OUTS), gate1[:, u % 2, :], ALU.mult).then_inc(d_z1, 1)

                def zlow(u):
                    dve.wait_ge(d_zh, u + 1)
                    if u >= 2:
                        dve.wait_ge(d_acc, u - 1)
                    nc.vector.tensor_tensor(zl[:, u % 2, :], zf[:, u % 2, :], zh[:, u % 2, :].bitcast(F32), ALU.subtract).then_inc(d_zl, 1)

                for s in range(ND + 2):
                    if s >= 2:
                        gated(s - 2)
                    if s < ND:
                        biased(s, 0)
                    if s >= 2:
                        zlow(s - 2)
                    if s < ND:
                        biased(s, 1)
                    if 1 <= s <= ND:
                        inverses(s - 1)
                    if s < ND:
                        biased(s, 2)
                        biased(s, 3)
                    if 1 <= s <= ND:
                        masked(s - 1)
                    if s < ND:
                        summed(s)
                    if s == 0:
                        nc.vector.tensor_tensor(x[:], x[:], ob1.rearrange("p (o f) -> p o f", o=1).to_broadcast([P, NT, H]), ALU.add).then_inc(d_x0, 1)
                dve.wait_ge(d_acc, ND)
                dve.wait_ge(d_x0, 1)
                for j in range(4):
                    nc.vector.tensor_tensor(x[:, 2 * j:2 * j + 2, :], x[:, 2 * j:2 * j + 2, :], v3(PS[:, 4 + j, :], 2, 256),
                                            ALU.add).then_inc(d_xadd, 1)
                dve.wait_ge(d_xadd, 4)

        f_codes = at(90, "f_codes", 6144, I32).rearrange("p (j w) -> p j w", j=8)
        f_scale = at(2, "f_scale", 6144).rearrange("p (j w) -> p j w", j=8)
        QT1 = at(34, "QT1", 2048, F32R).rearrange("p (v t) -> p v t", v=KVH)
        QT2 = at(42, "QT2", 2048, F32R).rearrange("p (v t) -> p v t", v=KVH)
        mT = at(50, "mT", 256, F32R)
        VS = at(52, "VS", 2048).rearrange("p (i v c) -> p i v c", i=NT, v=KVH)
        OS = v3(at(60, "OS", 512), 2, 256)
        mx = v3(at(62, "mx", 128), 2, 64)
        rden = v3(at(63, "rden", 64), 2, 32)
        on = at(64, "on", 512)
        PT = v4(at(66, "PT", 6144), 3, GRP, 512)
        SCALE2 = 1.0 / float(np.sqrt(HD2))

        def values_and_maxima(block):
            @block.gpsimd
            def _(pool):
                nc.gpsimd.memset(VS, 0.0).then_inc(e_vs, 1)
                nc.gpsimd.memset(mT.bitcast(F32), 0.0).then_inc(e_vs, 1)
                pool.wait_ge(e_vs, 2)
                nc.gpsimd.memset(VS[:, :, :, HD2:HD2 + 1], 1.0).then_inc(e_vs, 1)
                nc.gpsimd.tensor_copy(VS[:, :, :, 0:HD2], ctx_s[:].rearrange("p i (v d) -> p i v d", d=HD2)).then_inc(e_vs, 1)

        layer_norm("E", split=True, beside=values_and_maxima)
        e_t, e_tr, e_s, e_sr, e_nm, e_mt, e_pv, e_os, e_tp, e_on = (
            sem(f"e_{n}") for n in ("t", "tr", "s", "sr", "nm", "mt", "pv", "os", "tp", "on"))
        e_oread, e_x = sem("e_oread"), sem("e_x")
        with nc.Block() as block:
            NE = B * KVH
            turns_of = [4]
            for b in range(B):
                turns_of.append(turns_of[-1] + 1 + 4 + (4 if b + 1 < B else 0) + 4 * KVH)

            def turn_mt(b):
                return turns_of[b]

            def turn_q2(b, j):
                return turns_of[b] + 1 + j

            def turn_q1(b, j):
                return j if b == 0 else turns_of[b - 1] + 5 + j

            def turn_st(b, kv, g):
                return turns_of[b + 1] - 4 * KVH + 4 * kv + g

            def t_bank(k):
                return PS[:, 3 + k % 3, :]

            @block.gpsimd
            def _(pool):
                clear_keys(pool, KZ[1], 1 + GRP)

            @block.sync
            def _(sp):
                for b in range(1, B):
                    for half in range(2):
                        if b == 1:
                            sp.wait_ge(z_clear, 10)
                        else:
                            sp.wait_ge(e_t, turn_st(b - 2, 4 * half + 3, GRP - 1) + 1)
                        sp.wait_ge(ld_keys[half], 16 * 12 * b)
                        load_keys(sp, b, half)
                        if b == 1 and half == 1:
                            sp.dma_start(f_codes, ins["codes"]).then_inc(ld_f, 16)
                sp.wait_ge(e_t, turn_st(B - 2, KVH - 1, GRP - 1) + 1)
                for blk in range(8):
                    sp.dma_start(f_scale[16 * blk:16 * blk + 16, :, :],
                                 ins["scales"][blk:blk + 1, :].to_broadcast([16, 6144]).rearrange("p (j w) -> p j w", j=8)).then_inc(ld_f, 16)

            @block.tensor
            def _(pe):
                def take(k):
                    if k >= 3:
                        pe.wait_ge(e_tr, k - 2)
                    return t_bank(k)

                def stack1(b):
                    tok = slice(b * 256, (b + 1) * 256)
                    for j in range(4):
                        bank = take(turn_q1(b, j))
                        for kv in (2 * j, 2 * j + 1):
                            o = bank[:, (kv % 2) * 256:(kv % 2) * 256 + 256]
                            nc.tensor.matmul(o, sel[:, kv % 4, :], hTh[:, kv // 4, tok], start=True, stop=False)
                            last = nc.tensor.matmul(o, sel[:, 4 + kv % 4, :], hTl[:, kv // 4, tok], start=False, stop=True)
                        last.then_inc(e_t, 1)

                def stack2(b):
                    tok = slice(b * 256, (b + 1) * 256)
                    pe.wait_ge(e_tr, turn_mt(b) + 1)
                    for j in range(4):
                        bank = take(turn_q2(b, j))
                        for kv in (2 * j, 2 * j + 1):
                            o = bank[:, (kv % 2) * 256:(kv % 2) * 256 + 256]
                            nc.tensor.matmul(o, sel[:, kv % 4, :], hTh[:, kv // 4, tok], start=True, stop=False)
                            nc.tensor.matmul(o, sel[:, 4 + kv % 4, :], hTl[:, kv // 4, tok], start=False, stop=False)
                            last = nc.tensor.matmul(o, sel[:, 8 + kv, :], mT, start=False, stop=True)
                        last.then_inc(e_t, 1)

                def scores(b, kv, part):
                    if kv == 0 and part == 0:
                        pe.wait_ge(e_tr, turn_q1(b, 3) + 1)
                    if part == 0 and kv % 4 == 0:
                        pe.wait_ge(ld_keys[kv // 4], 16 * 12 * (b + 1))
                    k = (b * KVH + kv) * 4 + part
                    if k >= 3:
                        pe.wait_ge(e_sr, k - 2)
                    tt, pair = part // 2, part % 2
                    nc.tensor.matmul(PS[:, k % 3, :], QT1[:, kv, tt * 128:(tt + 1) * 128],
                                     KZ[b % 2][:, kv, 2 * pair:2 * pair + 2, :].rearrange("p g t -> p (g t)"),
                                     start=True, stop=True).then_inc(e_s, 1)

                def maxima(b):
                    pe.wait_ge(e_sr, (b + 1) * KVH * GRP)
                    bank = take(turn_mt(b))
                    for tt in range(2):
                        last = nc.tensor.transpose(bank[0:32, tt * 128:(tt + 1) * 128], mx[:, b % 2, tt * 32:(tt + 1) * 32], ident)
                    last.then_inc(e_t, 1)

                def scores_t(b, kv, g):
                    if kv == 0 and g == 0:
                        pe.wait_ge(e_tr, turn_q2(b, 3) + 1)
                    bank = take(turn_st(b, kv, g))
                    for st in range(2):
                        last = nc.tensor.matmul(bank[:, st * 256:(st + 1) * 256], KZ[b % 2][:, kv, g, st * 128:(st + 1) * 128],
                                                QT2[:, kv, :], start=True, stop=True)
                    last.then_inc(e_t, 1)

                def mix(m):
                    b, kv = m // KVH, m % KVH
                    for g in range(GRP):
                        pe.wait_ge(e_tr, turn_st(b, kv, g) + 1)
                        if m >= 1 and g == 0:
                            pe.wait_ge(e_os, m)
                        for st in range(2):
                            last = nc.tensor.matmul(PS[32 * g:32 * g + 32, 6, 0:256], VS[:, 2 * b + st, kv, :],
                                                    PT[:, m % 3, g, st * 256:(st + 1) * 256], start=st == 0, stop=st == 1,
                                                    tile_position=(0, 32 * g))
                        if g == GRP - 1:
                            last.then_inc(e_pv, 1)

                def turn(m):
                    pe.wait_ge(e_os, m + 1)
                    if m % 2 == 0 and m:
                        pe.wait_ge(e_oread, m // 2)
                    for tt in range(2):
                        o = (m % 2) * 256 + tt * 128
                        last = nc.tensor.transpose(PS[:, 7, o:o + 128], OS[:, m % 2, tt * 128:(tt + 1) * 128], ident)
                    last.then_inc(e_tp, 1)

                pe.wait_ge(e_sel, 1)
                pe.wait_ge(e_vs, 4)
                stack1(0)
                for kv in range(KVH):
                    for g in range(GRP):
                        scores(0, kv, g)
                for b in range(B):
                    maxima(b)
                    if b:
                        mix(b * KVH - 2)
                        turn(b * KVH - 3)
                    stack2(b)
                    if b:
                        mix(b * KVH - 1)
                        turn(b * KVH - 2)
                    if b + 1 < B:
                        stack1(b + 1)
                    for kv in range(KVH):
                        m = b * KVH + kv
                        for g in range(GRP):
                            scores_t(b, kv, g)
                            if b + 1 < B:
                                scores(b + 1, kv, g)
                        if kv >= 2:
                            mix(m - 2)
                        if kv >= 3 or (b and kv == 2):
                            turn(m - 3)
                mix(NE - 2)
                turn(NE - 3)
                mix(NE - 1)
                turn(NE - 2)
                turn(NE - 1)

            @block.scalar
            def _(act):
                def stacked(dst, k, j):
                    act.wait_ge(e_t, k + 1)
                    nc.scalar.copy(dst[:, 2 * j:2 * j + 2, :], v3(t_bank(k), 2, 256)).then_inc(e_tr, 1)

                def outputs(m):
                    act.wait_ge(e_pv, m + 1)
                    if m >= 2:
                        act.wait_ge(e_tp, m - 1)
                    nc.scalar.copy(OS[:, m % 2, :], PS[:, 6, 0:256]).then_inc(e_os, 1)

                for j in range(4):
                    stacked(QT1, turn_q1(0, j), j)
                for b in range(B):
                    act.wait_ge(e_t, turn_mt(b) + 1)
                    nc.scalar.activation(mT[0:32, :], t_bank(turn_mt(b))[0:32, 0:256], ACT.Copy, scale=-1.0).then_inc(e_tr, 1)
                    if b:
                        outputs(b * KVH - 3)
                        outputs(b * KVH - 2)
                    for j in range(4):
                        stacked(QT2, turn_q2(b, j), j)
                    if b:
                        outputs(b * KVH - 1)
                    if b + 1 < B:
                        for j in range(4):
                            stacked(QT1, turn_q1(b + 1, j), j)
                    for kv in range(KVH):
                        m = b * KVH + kv
                        if kv >= 3:
                            outputs(m - 3)
                        if m >= 3:
                            act.wait_ge(e_pv, m - 2)
                        for g in range(GRP):
                            k = turn_st(b, kv, g)
                            act.wait_ge(e_t, k + 1)
                            nc.scalar.activation(PT[:, m % 3, g, :], t_bank(k), ACT.Exp, scale=SCALE2).then_inc(e_tr, 1)
                outputs(NE - 3)
                outputs(NE - 2)
                outputs(NE - 1)

            @block.vector
            def _(dve):
                L = lambda inst: link(dve, "v", s_vec, inst)

                def maxima(b, kv):
                    for part in range(4):
                        k = (b * KVH + kv) * 4 + part
                        dve.wait_ge(e_s, k + 1)
                        if kv == 0 and part == 0 and b >= 2:
                            dve.wait_ge(e_t, turn_mt(b - 2) + 1)
                        h0 = 32 * (part // 2) + GRP * kv + 2 * (part % 2)
                        h = mx[:, b % 2, h0:h0 + 2]
                        nc.vector.tensor_reduce(h, v3(PS[:, k % 3, :], 2, 256), AX.X, ALU.max).then_inc(e_sr, 1)

                def finish(j):
                    m = 2 * j
                    b, kv = m // KVH, m % KVH
                    dve.wait_ge(e_tp, m + 2)
                    o = PS[:, 7, :].rearrange("p (a t g c) -> p a t g c", a=2, t=2, g=GRP)
                    for a in range(2):
                        r = rden[:, a, 0:8].rearrange("p (t g o) -> p t g o", t=2, o=1)
                        L(nc.vector.reciprocal(r, o[:, a, :, :, HD2:HD2 + 1]))
                        n4 = on[:, a * 64:(a + 1) * 64].rearrange("p (t g d) -> p t g d", t=2, g=GRP)
                        inst = nc.vector.tensor_tensor(n4, o[:, a, :, :, 0:HD2], r.to_broadcast([P, 2, GRP, HD2]), ALU.mult)
                        if a == 1:
                            inst.then_inc(e_oread, 1)
                            dve.wait_ge(e_oread, j + 1)
                        else:
                            L(inst)
                    for a in range(2):
                        c0 = 32 * (kv + a)
                        xs = x[:, 2 * b:2 * b + 2, c0:c0 + 32]
                        nc.vector.tensor_tensor(xs, xs, v3(on[:, a * 64:(a + 1) * 64], 2, 32), ALU.add).then_inc(e_x, 1)
                    dve.wait_ge(e_x, 2 * j + 2)

                for kv in range(KVH):
                    maxima(0, kv)
                for b in range(B):
                    if b:
                        finish(b * KVH // 2 - 2)
                    for kv in range(KVH):
                        m = b * KVH + kv
                        if b + 1 < B:
                            maxima(b + 1, kv)
                        if kv == 4 or kv == 6 or (b and kv == 2):
                            finish((m - 4) // 2)
                finish(NE // 2 - 2)
                finish(NE // 2 - 1)

        layer_norm("F", parity=True, split=True)
        NW = 2 * 768
        code = at(114, "f_code", 768, I16)
        sign = at(117, "f_sign", 768, I16)
        lin = at(120, "f_lin", 768, BF16)
        val = v3(at(123, "f_val", 1536, BF16), 2, NW)
        wf = at(129, "f_wf", 1536)
        fwh = v3(at(135, "f_wh", 3072, F32R), 2, NW)
        fwl = v3(at(33, "f_wl", 3072, F32R), 2, NW)
        gel = v3(at(45, "f_gel", 1024), 2, 512)
        hf = v3(at(49, "f_hf", 1024), 2, 512)
        hh = v3(at(53, "f_hh", 1536, F32R), 3, 512)
        hl = v3(at(59, "f_hl", 1536, F32R), 3, 512)
        NSTEP = NB // 2
        f_val, f_wf, f_wh, f_wl = (sem(f"f_{n}") for n in ("val", "wf", "wh", "wl"))
        f_g, f_gel, f_hid, f_hh, f_hl, f_dn, f_add, f_out = (sem(f"f_{n}") for n in ("g", "gel", "hid", "hh", "hl", "dn", "add", "out"))
        with nc.Block() as block:
            funits = [(n, c) for n in range(NB) for c in range(2)]
            NF = len(funits)

            @block.gpsimd
            def _(pool):
                for j in range(NSTEP):
                    pool.wait_ge(f_val, j + 1)
                    if j >= 1:
                        pool.wait_ge(f_wh, j)
                        pool.wait_ge(f_wl, j)
                    nc.gpsimd.tensor_tensor(wf.rearrange("p (y w) -> p y w", y=2), val[:, j % 2, :].rearrange("p (y w) -> p y w", y=2),
                                            f_scale[:, j:j + 1, :].to_broadcast([P, 2, 768]), ALU.mult).then_inc(f_wf, 1)
                    pool.wait_ge(f_wh, j + 1)
                    nc.gpsimd.tensor_tensor(fwl[:, j % 2, :], wf, fwh[:, j % 2, :].bitcast(F32), ALU.subtract).then_inc(f_wl, 1)

            @block.tensor
            def _(pe):
                def w(part, n, which, k):
                    o = k * 768 + which * 256 + (n % 2) * 128
                    return part[:, (n // 2) % 2, o:o + 128]

                def up(u):
                    n, c = funits[u]
                    pe.wait_ge(f_wl, n // 2 + 1)
                    if u >= 2:
                        pe.wait_ge(f_hid, u - 1)
                    tok = slice(c * 512, (c + 1) * 512)
                    for j in range(2):
                        for k in range(KT):
                            last = mm3(PS[:, 2 * (u % 2) + j, :], (w(fwh, n, j, k), w(fwl, n, j, k)), (hTh[:, k, tok], hTl[:, k, tok]),
                                       k == 0, k == 1)
                        last.then_inc(f_g, 1)

                def down(u):
                    n, c = funits[u]
                    pe.wait_ge(f_hl, u + 1)
                    o = (n % 2) * 768 + 512
                    for i in range(4):
                        t = slice(i * 128, (i + 1) * 128)
                        last = mm3(PS[:, 4 + 2 * c + i // 2, (i % 2) * 256:(i % 2) * 256 + 256], (hh[:, u % 3, t], hl[:, u % 3, t]),
                                   (fwh[:, (n // 2) % 2, o:o + 256], fwl[:, (n // 2) % 2, o:o + 256]),
                                   n == 0 and i % 2 == 0, n == NB - 1, skip_group_check=True)
                    last.then_inc(f_dn, 1)

                for u in range(NF + 2):
                    if u < NF:
                        up(u)
                    if u >= 2:
                        down(u - 2)

            @block.scalar
            def _(act):
                def split(j):
                    act.wait_ge(f_wf, j + 1)
                    if j >= 2:
                        act.wait_ge(f_dn, 4 * (j - 1))
                    nc.scalar.copy(fwh[:, j % 2, :], wf).then_inc(f_wh, 1)

                def high(u):
                    act.wait_ge(f_hid, u + 1)
                    if u >= 3:
                        act.wait_ge(f_dn, u - 2)
                    nc.scalar.copy(hh[:, u % 3, :], hf[:, u % 2, :]).then_inc(f_hh, 1)

                split(0)
                split(1)
                for u in range(NF):
                    act.wait_ge(f_g, 2 * u + 1)
                    if u >= 2:
                        act.wait_ge(f_hid, u - 1)
                    nc.scalar.activation(gel[:, u % 2, :], PS[:, 2 * (u % 2), :], ACT.Gelu_apprx_tanh).then_inc(f_gel, 1)
                    if u >= 1:
                        high(u - 1)
                    if u % 4 == 1 and 1 <= u // 4 < NSTEP - 1:
                        split(u // 4 + 1)
                high(NF - 1)

            @block.vector
            def _(dve):
                L = lambda inst: link(dve, "v", s_vec, inst)
                dve.wait_ge(ld_f, 16 * 9)

                def dequant(j):
                    src = f_codes[:, j, :].bitcast(I16)[:, 0::2]
                    if j >= 2:
                        dve.wait_ge(f_wf, j - 1)
                    for parity in range(2):
                        sl = slice(768 * parity, 768 * parity + 768)
                        L(nc.vector.tensor_scalar(code[:, sl], src, 6 - 4 * parity, 0x1C0, ALU.logical_shift_left, ALU.bitwise_and))
                        L(nc.vector.tensor_scalar(sign[:, sl], src, 12 - 4 * parity, -32768, ALU.logical_shift_left, ALU.bitwise_and))
                    v = val[:, j % 2, :]
                    L(nc.vector.tensor_scalar(code, code, 0x3E00, None, ALU.bitwise_or))
                    L(nc.vector.tensor_scalar(lin, code.bitcast(BF16), 8.0, -1.0, ALU.mult, ALU.add))
                    L(nc.vector.tensor_scalar(v, code.bitcast(BF16), 4.0, None, ALU.mult))
                    L(nc.vector.tensor_tensor(v, lin, v, ALU.min))
                    nc.vector.tensor_tensor(v.bitcast(I16), v.bitcast(I16), sign, ALU.bitwise_or).then_inc(f_val, 1)
                    dve.wait_ge(f_val, j + 1)

                def product(u):
                    dve.wait_ge(f_gel, u + 1)
                    dve.wait_ge(f_g, 2 * u + 2)
                    if u >= 2:
                        dve.wait_ge(f_hl, u - 1)
                    nc.vector.tensor_tensor(hf[:, u % 2, :], PS[:, 2 * (u % 2) + 1, :], gel[:, u % 2, :], ALU.mult).then_inc(f_hid, 1)

                def low(u):
                    dve.wait_ge(f_hh, u + 1)
                    if u >= 3:
                        dve.wait_ge(f_dn, u - 2)
                    nc.vector.tensor_tensor(hl[:, u % 3, :], hf[:, u % 2, :], hh[:, u % 3, :].bitcast(F32), ALU.subtract).then_inc(f_hl, 1)

                dequant(0)
                dequant(1)
                for u in range(NF):
                    product(u)
                    if u >= 1:
                        low(u - 1)
                    if u % 4 == 0 and u // 4 + 2 < NSTEP:
                        dequant(u // 4 + 2)
                low(NF - 1)
                for c in range(2):
                    dve.wait_ge(f_dn, NF - 1 + c)
                    for j in (2 * c, 2 * c + 1):
                        nc.vector.tensor_tensor(x[:, 2 * j:2 * j + 2, :], x[:, 2 * j:2 * j + 2, :], v3(PS[:, 4 + j, :], 2, 256),
                                                ALU.add).then_inc(f_add, 1)

            @block.sync
            def _(sp):
                for c in range(2):
                    sp.wait_ge(f_add, 2 * c + 2)
                    sp.dma_start(out[:, 4 * c:4 * c + 4, :], x[:, 4 * c:4 * c + 4, :]).then_inc(f_out, 16)
                sp.wait_ge(f_out, 32)


def shape_constants():
    i = np.arange(P)
    causal = (i[:, None] <= i[None, :]).astype(np.float32)
    same = (i[:, None] // CHUNK == i[None, :] // CHUNK).astype(np.float32)
    mask_ret = np.concatenate([causal, np.ones((P, P), np.float32), causal], 1)
    consts = np.concatenate([np.eye(P, dtype=np.float32), np.ones((P, P), np.float32), mask_ret] + [causal * same] * 4, 1)
    half = HD0 // 2
    xscale = (np.arange(0, HD0, 2, dtype=np.float32) + np.float32(0.4 * HD0)) / np.float32(1.4 * HD0)
    pos = np.arange(S, dtype=np.float32)
    scale = xscale[None, :].astype(np.float64) ** (pos[:, None] / 64).astype(np.float64)
    inv_freq = (1.0 / 10000.0 ** (np.arange(half) / half)).astype(np.float32)
    angle = (pos[:, None] * inv_freq[None, :]).astype(np.float64)
    gammas = (1.0 - np.exp(np.linspace(np.log(1.0 / 32), np.log(1.0 / 64), NH0))).astype(np.float32).astype(np.float64)
    tab = np.zeros((2, P, 2, 2, 2, NH0, half))
    for n in range(NH0):
        grow = gammas[n] ** pos.astype(np.float64)[:, None]
        for j, size in enumerate((scale * grow, 1.0 / (scale * grow))):
            for eo, sign in enumerate((-1.0, 1.0)):
                tab[:, :, 0, j, eo, n, :] = (np.cos(angle) * size).reshape(2, P, half)
                tab[:, :, 1, j, eo, n, :] = (sign * np.sin(angle) * size).reshape(2, P, half)
    tab = tab.transpose(1, 0, 2, 3, 4, 5, 6).reshape(P, 2, 1024)
    sel = np.zeros((P, 16, P), np.float32)
    for q in range(4):
        for g in range(GRP):
            for d in range(HD2):
                row = 32 * q + HD2 * g + d
                sel[row, q, 32 * g + d] = sel[row, q, 32 * g + 16 + d] = 1.0
                sel[row, 4 + q, 32 * g + 8 + d] = 1.0
    for kv in range(KVH):
        for g in range(GRP):
            sel[GRP * kv + g, 8 + kv, 32 * g + 24] = 1.0
    return consts, tab.astype(np.float32), sel.reshape(P, 16 * P)


def kernel(**inputs):
    import concourse.bacc as _bacc
    from concourse.bass_utils import run_bass_kernel_spmd as _run

    a = {k: np.asarray(v) for k, v in inputs.items()}
    kp = lambda w: w.reshape(KT, P, -1).transpose(1, 0, 2)
    heads = lambda w: w.transpose(1, 0, 2)
    even_odd = lambda w: [heads(w)[:, :, j::2].reshape(H, P) for j in range(2)]
    consts, rot_tab, sel = shape_constants()
    ctx = a["ctx_512"]
    codes = lambda p: p.T.reshape(P, 8, P, 2).transpose(0, 1, 3, 2).reshape(P, 8, 256)
    scl = lambda s: s.T.reshape(8, 8, P, 2).transpose(0, 1, 3, 2).reshape(8, 8, 256)
    experts = lambda w: w.reshape(E0, KT, P, 256).transpose(2, 0, 1, 3).reshape(P, E0, 512)
    by_head = lambda w: w.T.reshape(KT, P, NH1, P).transpose(1, 2, 0, 3).reshape(P, NH1, 256)
    arrays = {
        "x": a["x"].reshape(NT, P, H).transpose(1, 0, 2),
        "consts": consts, "rot_tab": rot_tab, "sel": sel,
        "wqkvg": kp(np.concatenate(even_odd(a["L0_attn_W_Q"]) + even_odd(a["L0_attn_W_K"])
                                   + [heads(a["L0_attn_W_V"]).reshape(H, 256), a["L0_attn_W_G"]], 1)),
        "wo0": kp(a["L0_attn_W_O"]),
        "gn_w": a["L0_attn_gn_weight"], "gn_b": a["L0_attn_gn_bias"],
        "ctxT": ctx.reshape(T, CD).T, "ctx_s": ctx.reshape(NT, P, CD).transpose(1, 0, 2),
        "wkT": a["L0_xattn_W_k"].T, "bk": a["L0_xattn_b_k"], "xg": a["L0_xattn_ln_gamma"], "xb": a["L0_xattn_ln_beta"],
        "wr": kp(a["L0_ffn_Wr"]), "temp": a["L0_ffn_temperature"],
        "wexp": np.stack([experts(a[f"L0_ffn_{n}"]) for n in ("Wg", "Wu", "Wd")], 2).reshape(P, E0, 1536),
        "w1": np.concatenate([by_head(a[f"L1_attn_{n}_w"]) for n in ("q", "k", "v", "og")]
                             + [a["L1_attn_o_w"].T.reshape(NB, P, H).transpose(1, 0, 2)], 2),
        "qkvb": np.stack([a[f"L1_attn_{n}_b"].reshape(NH1, P) for n in "qkv"], 1).reshape(-1),
        "bw1": kp(a["L1_attn_b_w"].T), "bb1": a["L1_attn_b_b"], "ob1": a["L1_attn_o_b"],
        "codes": np.stack([codes(a["L1_ffn_gate_W_packed"]), codes(a["L1_ffn_up_W_packed"]),
                           a["L1_ffn_down_W_packed"].T.reshape(8, P, H).transpose(1, 0, 2)], 2).reshape(P, 8, 768),
        "scales": np.stack([scl(a["L1_ffn_gate_scales"]), scl(a["L1_ffn_up_scales"]),
                            a["L1_ffn_down_scales"].T.reshape(8, 8, H).transpose(1, 0, 2)], 2).reshape(8, 8 * 768),
    }
    nc = _bacc.Bacc("TRN2", target_bir_lowering=False, num_devices=1)
    args, feed = {}, {}
    for name, arr in arrays.items():
        arr = np.ascontiguousarray(arr)
        feed[f"in_{name}"] = arr
        args[name] = nc.dram_tensor(f"in_{name}", arr.shape, mybir.dt.from_np(arr.dtype), kind="ExternalInput").ap()
    out = nc.dram_tensor("out_x", (P, NT, H), F32, kind="ExternalOutput").ap()
    build_decoder(nc, args, out)
    r = _run(nc, [feed], core_ids=[0])
    return r.results[0]["out_x"].transpose(1, 0, 2).reshape(B, S, H)
```

```python
from contextlib import ExitStack

import numpy as np

import concourse.bass as bass
from concourse import mybir

ALU = mybir.AluOpType
ACT = mybir.ActivationFunctionType
AX = mybir.AxisListType
F32 = mybir.dt.float32
F32R = mybir.dt.float32r
BF16 = mybir.dt.bfloat16
I16 = mybir.dt.int16
I32 = mybir.dt.int32

P = 128
B, S, H = 4, 256, 256
T = B * S
NT = T // P
KT = H // P
HALF = T // 2
NH0, HD0 = 16, 16
E0 = 8
NH1, HD1 = 16, 128
CHUNK = 64
KVH, GRP, HD2 = 8, 4, 8
CD = 64
MLP = 2048
NB = MLP // P
LN_EPS = 1e-5

KB = 256


def build_decoder(nc, ins, out):
    with ExitStack() as ctx:
        def sb(name, shape, dt=F32):
            return ctx.enter_context(nc.sbuf_tensor(name, shape, dt))

        sem_names = set()

        def sem(name):
            assert name not in sem_names
            sem_names.add(name)
            return ctx.enter_context(nc.semaphore(name))

        PS = ctx.enter_context(nc.psum_tensor("PS", [P, 8, 512], F32))
        x = sb("x", [P, NT, H])
        hTh = sb("hTh", [P, KT, T], F32R)
        hTl = sb("hTl", [P, KT, T], F32R)
        consts = sb("consts", [P, 1152])
        ident = consts[:, 0:128]
        ones = consts[:, 128:256]
        mask_ret = consts[:, 256:640]
        mask_chunk = consts[:, 640:1152]
        eps_t = sb("eps_t", [P, 2])
        small = sb("small", [P, 640])

        SLAB_KB = 167
        slab = sb("slab", [P, SLAB_KB * KB])
        slab_at = nc.lookup_mloc("slab").addr

        def at(kb, name, words, dt=F32):
            assert kb * KB + words <= SLAB_KB * KB
            n = words * 4 // (2 if dt in (I16, BF16) else 4)
            return nc.alloc_sbuf_tensor_at(name, [P, n], dt, offset=slab_at + kb * 1024)[:, :]

        def v3(ap, a, b):
            return ap.rearrange("p (a b) -> p a b", a=a, b=b)

        def v4(ap, a, b, c):
            return ap.rearrange("p (a b c) -> p a b c", a=a, b=b, c=c)

        PASSES = ((0, 0), (0, 1), (1, 0))

        def mm3(out, stat, mov, start, stop, **kw):
            for j, (a, b) in enumerate(PASSES):
                last = nc.tensor.matmul(out, stat[a], mov[b], start=start and j == 0, stop=stop and j == 2, **kw)
            return last

        def narrow(banks, wh, wl, n):
            for c in range(2):
                tok = slice(c * 512, (c + 1) * 512)
                for k in range(KT):
                    last = mm3(PS[0:n, banks + c, :], (wh[:, k, :], wl[:, k, :]), (hTh[:, k, tok], hTl[:, k, tok]), k == 0, k == 1)
            return last

        def rows_turned(bank, rows, n):
            for i in range(NT):
                last = nc.tensor.transpose(PS[:, bank, i * n:(i + 1) * n], rows[:, i * 128:(i + 1) * 128], ident[0:n, 0:n])
            return last

        R2 = at(32, "R2", 88 * KB)
        hT = v3(at(120, "hT", 2048), KT, T)
        SC = at(128, "SC", 2048)
        a_w = v3(at(0, "a_w", 2048), KT, 1024)
        a_wh_t = v3(at(8, "a_wh_t", 2048, F32R), KT, 1024)
        a_wl_t = v3(at(16, "a_wl_t", 2048, F32R), KT, 1024)
        rot_tab = v3(at(24, "rot_tab", 2048), 2, 1024)
        gn_w, gn_b = at(112, "gn_w", 256), at(113, "gn_b", 256)
        wo0 = v3(at(114, "a_wo", 512), KT, 256)
        woh = v3(at(116, "a_woh", 512, F32R), KT, 256)
        wol = v3(at(118, "a_wol", 512, F32R), KT, 256)

        s_vec = sem("s_vec")
        s_act = sem("s_act")
        s_pool = sem("s_pool")
        chain = {"v": 0, "a": 0, "p": 0}

        def link(eng, key, s, inst):
            chain[key] += 1
            inst.then_inc(s, 1)
            eng.wait_ge(s, chain[key])

        ld_x, ld_c, ld_a, ld_w = sem("ld_x"), sem("ld_c"), sem("ld_a"), sem("ld_w")
        a_whi, a_wl, a_wo = sem("a_whi"), sem("a_wl"), sem("a_wo")
        ld_b, ld_moe = sem("ld_b"), sem("ld_moe")
        ld_d, ld_f, ld_scale, eps_set = sem("ld_d"), sem("ld_f"), sem("ld_scale"), sem("eps_set")
        ld_keys = [sem("ld_keys0"), sem("ld_keys1")]
        e_ld, e_sel, e_vs = sem("e_ld"), sem("e_sel"), sem("e_vs")
        z_clear = sem("z_clear")
        ctx_h = at(154, "ctx_h", 1024, F32R)[0:64, :]
        ctx_l = at(158, "ctx_l", 1024, F32R)[0:64, :]
        ctx_parts = nc.dram_tensor("ctx_parts", (2, CD, T), F32, kind="Internal").ap()
        ctx_split, ctx_stored = sem("ctx_split"), sem("ctx_stored")
        ctxT = SC[0:64, 0:1024]
        wkT = small[0:64, 0:64]
        bk_col = small[0:64, 64:65]
        bk_row = small[:, 128:192]
        xg_row = sb("xg_row", [P, 512])
        wr = small[:, 192:208].rearrange("p (k e) -> p k e", k=KT)
        temp = small[:, 208:209]
        bw1 = small[:, 256:288].rearrange("p (k e) -> p k e", k=KT)
        bb1 = small[:, 288:304]
        ob1 = small[:, 304:560]
        ctx_s = sb("ctx_s", [P, NT, CD])
        mv = sb("mv", [P, NT, 2])
        stats = sb("stats", [P, NT, 6])
        rstd = sb("rstd", [P, NT])
        rin = sb("rin", [P, NT])
        xn = sb("xn", [P, 5, 256])

        c_raw = v3(at(136, "c_raw", 3 * 1536), 3, 1536)
        ld_exp = [sem(f"ld_exp{j}") for j in range(3)]

        def bcast_row(a, n):
            return a.rearrange("(o n) -> o n", o=1).to_broadcast([P, n])

        N_A, N_B, N_MOE, N_D = 4, 7, 2, 4

        with nc.Block() as block:
            @block.sync
            def _(sp):
                sp.dma_start(x[:], ins["x"]).then_inc(ld_x, 16)
                sp.dma_start(consts[:], ins["consts"]).then_inc(ld_c, 16)
                for k in range(KT):
                    sp.dma_start(a_w[:, k, :], ins["wqkvg"][:, k, :]).then_inc(ld_w, 16)
                sp.dma_start(rot_tab, ins["rot_tab"]).then_inc(ld_a, 16)
                sp.dma_start(wo0, ins["wo0"]).then_inc(ld_a, 16)
                sp.dma_start(gn_w, bcast_row(ins["gn_w"], 256)).then_inc(ld_a, 16)
                sp.dma_start(gn_b, bcast_row(ins["gn_b"], 256)).then_inc(ld_a, 16)
                sp.dma_start(ctxT, ins["ctxT"]).then_inc(ld_b, 16)
                sp.dma_start(wkT, ins["wkT"]).then_inc(ld_b, 16)
                sp.dma_start(bk_col, ins["bk"].rearrange("(n o) -> n o", o=1)).then_inc(ld_b, 16)
                sp.dma_start(bk_row, bcast_row(ins["bk"], 64)).then_inc(ld_b, 16)
                sp.dma_start(xg_row[:, 0:256], bcast_row(ins["xg"], 256)).then_inc(ld_b, 16)
                sp.dma_start(xg_row[:, 256:512], bcast_row(ins["xb"], 256)).then_inc(ld_b, 16)
                sp.dma_start(ctx_s[:], ins["ctx_s"]).then_inc(ld_b, 16)
                sp.dma_start(wr, ins["wr"]).then_inc(ld_moe, 16)
                sp.dma_start(temp, bcast_row(ins["temp"], 1)).then_inc(ld_moe, 16)

            @block.vector
            def _(dve):
                nc.vector.memset(eps_t[:, 0:1], LN_EPS)
                nc.vector.memset(eps_t[:, 1:2], 1e-6).then_inc(eps_set, 1)

        ln_var, ln_sd, ln_rstd, ln_vector, ln_pool, ln_turned, ln_out, ln_low = (
            sem(f"ln_{n}") for n in ("var", "sd", "rstd", "vector", "pool", "turned", "out", "low"))
        table_out = sb("table_out", [P, 1])
        ln_round = [0, 0]

        def layer_norm(ph, parity=False, split=False, before=None, beside=None, scalar_beside=None,
                       tensor_before=None, vector_after=None):
            n0 = ln_round[0]
            n0_low = ln_round[1]
            ln_round[0] += 1
            ln_round[1] += split
            tr0, ev0, low0 = n0 * NT, n0 * NT // 2, n0_low * NT // 2
            dst = hTh if split else hT
            by_pool = (3, 7)
            slot = lambda i: i % 4 if i < 7 else 4
            by_vector = tuple(i for i in range(NT) if i not in by_pool)
            with nc.Block() as block:
                @block.vector
                def _(dve):
                    if ph == "A":
                        dve.wait_ge(ld_x, 16)
                    for i in range(NT):
                        nc.vector.bn_stats(stats[:, i, :], x[:, i, :]).then_inc(s_vec, 1)
                        chain["v"] += 1
                    dve.wait_ge(s_vec, chain["v"])
                    for i in range(NT):
                        last = nc.vector.bn_aggr(mv[:, i, :], stats[:, i, :])
                    last.then_inc(ln_var, 1)
                    dve.wait_ge(ln_sd, n0 + 1)
                    nc.vector.reciprocal(rstd[:], rin[:]).then_inc(ln_rstd, 1)
                    dve.wait_ge(ln_rstd, n0 + 1)

                    def low(j):
                        t = slice(j * 256, (j + 1) * 256)
                        dve.wait_ge(ln_out, ev0 + j + 1)
                        nc.vector.tensor_tensor(hTl[:, :, t], v3(PS[:, j, :], KT, 256), hTh[:, :, t].bitcast(F32),
                                                ALU.subtract).then_inc(ln_low, 1)

                    for i in by_vector:
                        if i >= 4:
                            dve.wait_ge(ln_turned, tr0 + i - 3)
                        nc.vector.tensor_scalar(xn[:, slot(i), :], x[:, i, :], mv[:, i, 0:1], rstd[:, i:i + 1],
                                                ALU.subtract, ALU.mult).then_inc(ln_vector, 1)
                    if split:
                        for j in range(NT // 2):
                            low(j)
                        dve.wait_ge(ln_low, low0 + NT // 2)
                    if vector_after:
                        vector_after(dve)

                @block.gpsimd
                def _(pool):
                    if before:
                        before(pool)
                    pool.wait_ge(ln_rstd, n0 + 1)
                    for i in by_pool:
                        nc.gpsimd.tensor_scalar(xn[:, slot(i), :], x[:, i, :], mv[:, i, 0:1], rstd[:, i:i + 1],
                                                ALU.subtract, ALU.mult).then_inc(ln_pool, 1)
                    if beside:
                        beside(pool)
                    if ph == "A":
                        for k in range(KT):
                            pool.wait_ge(a_whi, k + 1)
                            nc.gpsimd.tensor_tensor(a_wl_t[:, k, :], a_w[:, k, :], a_wh_t[:, k, :].bitcast(F32),
                                                    ALU.subtract).then_inc(a_wl, 1)

                @block.scalar
                def _(act):
                    if ph == "A":
                        act.wait_ge(eps_set, 1)
                    nc.scalar.activation(table_out[:], eps_t[:, 0:1], ACT.Sqrt).then_inc(s_act, 1)
                    chain["a"] += 1
                    act.wait_ge(s_act, chain["a"])
                    act.wait_ge(ln_var, n0 + 1)
                    nc.scalar.activation(rin[:], mv[:, :, 1], ACT.Sqrt, bias=eps_t[:, 0:1]).then_inc(ln_sd, 1)
                    if scalar_beside:
                        scalar_beside(act)
                    if ph == "A":
                        act.wait_ge(ld_w, 16 * KT)
                        for k in range(KT):
                            nc.scalar.copy(a_wh_t[:, k, :], a_w[:, k, :]).then_inc(a_whi, 1)
                    for j in range(NT // 2):
                        act.wait_ge(ln_turned, tr0 + 2 * j + 2)
                        nc.scalar.copy(dst[:, :, j * 256:(j + 1) * 256], v3(PS[:, j, :], KT, 256)).then_inc(ln_out, 1)
                    act.wait_ge(ln_out, ev0 + NT // 2)

                @block.tensor
                def _(pe):
                    if ph == "A":
                        pe.wait_ge(ld_c, 16)
                    if tensor_before:
                        tensor_before(pe)
                    for i in range(NT):
                        if i in by_pool:
                            pe.wait_ge(ln_pool, n0 * len(by_pool) + by_pool.index(i) + 1)
                        else:
                            pe.wait_ge(ln_vector, n0 * len(by_vector) + by_vector.index(i) + 1)
                        for k in range(KT):
                            src = xn[:, slot(i), k::2] if parity else xn[:, slot(i), k * 128:(k + 1) * 128]
                            o = k * 256 + (i % 2) * 128
                            last = nc.tensor.transpose(PS[:, i // 2, o:o + 128], src, ident)
                        last.then_inc(ln_turned, 1)

        layer_norm("A", split=True)
        QT = v3(at(32, "a_QT", 8192, F32R), 8, T)
        KTs = v3(at(64, "a_KT", 8192, F32R), 8, T)
        v0 = v4(at(96, "a_v", 4096), NT, NH0, 32)
        sgate = v3(at(154, "a_gate", 2048), NT, 256)
        Qs = v3(at(120, "a_Qs", 2048, F32R), 2, 1024)
        Ks = v3(at(136, "a_Ks", 2048, F32R), 2, 1024)
        rot = v3(at(144, "a_rotated", 1024), 2, 512)
        by_cos = at(148, "a_cos", 512)
        by_sin = at(150, "a_sin", 512)
        identr = at(152, "a_identr", 128, F32R)
        a_qk, a_vg, a_vgev, a_prod, a_rot, a_hi, a_low, a_pad, a_tn, a_qtev, a_ktev = (
            sem(f"a_{n}") for n in ("qk", "vg", "vgev", "prod", "rot", "hi", "low", "pad", "tn", "qtev", "ktev"))
        a_s, a_sev, a_pv, a_ytev, a_yt, a_yread, a_yn = (sem(f"a_{n}") for n in ("s", "sev", "pv", "ytev", "yt", "yread", "yn"))
        a_var, a_sd, a_z, a_zt, a_zth, a_ztl, a_o, a_xadd = (sem(f"a_{n}") for n in ("var", "sd", "z", "zt", "zth", "ztl", "o", "xadd"))
        with nc.Block() as block:
            @block.gpsimd
            def _(pool):
                for stack in (Qs, Ks):
                    pad = stack.bitcast(F32).rearrange("p s (n c) -> p (s n) c", c=64)[:, :, 48:64]
                    nc.gpsimd.memset(pad, 0.0).then_inc(a_pad, 1)
                nc.gpsimd.memset(v0[:, :, :, HD0:32], 0.0).then_inc(a_pad, 1)
                pool.wait_ge(ld_a, 16 * N_A)
                nc.gpsimd.tensor_copy(woh.rearrange("p k n -> p (k n)"), wo0.rearrange("p k n -> p (k n)")).then_inc(a_wo, 1)
                pool.wait_ge(a_wo, 1)
                nc.gpsimd.tensor_tensor(wol.rearrange("p k n -> p (k n)"), wo0.rearrange("p k n -> p (k n)"),
                                        woh.bitcast(F32).rearrange("p k n -> p (k n)"), ALU.subtract).then_inc(a_wo, 1)

            @block.tensor
            def _(pe):
                pe.wait_ge(a_wl, KT)

                def project(i):
                    tok = slice(i * 128, (i + 1) * 128)
                    for j, done in enumerate((a_qk, a_vg)):
                        if i >= 2:
                            if j == 0:
                                pe.wait_ge(a_prod, 3 * (i - 1))
                            else:
                                pe.wait_ge(a_vgev, 2 * (i - 1))
                        col = slice(j * 512, (j + 1) * 512)
                        for k in range(KT):
                            last = mm3(PS[:, 2 * j + i % 2, :], (hTh[:, k, tok], hTl[:, k, tok]),
                                       (a_wh_t[:, k, col], a_wl_t[:, k, col]), k == 0, k == 1)
                        last.then_inc(done, 1)

                def turn(i):
                    for j, (stack, ev) in enumerate(((Qs, a_qtev), (Ks, a_ktev))):
                        pe.wait_ge(a_low, 2 * i + j + 1)
                        for half in range(2):
                            if i >= 1:
                                pe.wait_ge(ev, 2 * (i - 1) + half + 1)
                            for g in range(4):
                                o = (4 * half + g) * 128
                                last = nc.tensor.matmul(PS[:, 4 + 2 * j + half, g * 128:(g + 1) * 128], stack[:, i % 2, o:o + 128],
                                                        identr, start=True, stop=True)
                            last.then_inc(a_tn, 1)

                for i in range(NT + 1):
                    if i < NT:
                        project(i)
                    if i == 1:
                        pe.wait_ge(a_pad, 4)
                    if i >= 1:
                        turn(i - 1)

            @block.scalar
            def _(act):
                for i in range(NT + 1):
                    if i < NT:
                        r = lambda j: rot[:, i % 2, j * 256:(j + 1) * 256].rearrange("p (n o d) -> p n o d", o=1, d=HD0).to_broadcast([P, NH0, 2, HD0])
                        st = lambda stack: stack[:, i % 2, :].rearrange("p (n c d) -> p n c d", c=4, d=HD0)
                        for j, dst in enumerate((st(Qs)[:, :, 0:3:2, :], st(Ks)[:, :, 0:2, :])):
                            act.wait_ge(a_rot, 2 * i + j + 1)
                            if i >= 2:
                                act.wait_ge(a_tn, 4 * (i - 1))
                            nc.scalar.copy(dst, r(j)).then_inc(a_hi, 1)
                    if i >= 1:
                        for half in range(2):
                            act.wait_ge(a_tn, 4 * (i - 1) + half + 1)
                            nc.scalar.copy(QT[:, 4 * half:4 * half + 4, (i - 1) * 128:i * 128], v3(PS[:, 4 + half, :], 4, 128)).then_inc(a_qtev, 1)
                    if i < NT:
                        act.wait_ge(a_vg, i + 1)
                        nc.scalar.copy(v0[:, i, :, 0:HD0], v3(PS[:, 2 + i % 2, 0:256], NH0, HD0)).then_inc(a_vgev, 1)
                        nc.scalar.activation(sgate[:, i, :], PS[:, 2 + i % 2, 256:512], ACT.Silu).then_inc(a_vgev, 1)
                act.wait_ge(a_vgev, 2 * NT)
                act.wait_ge(a_qtev, 2 * NT)

            @block.vector
            def _(dve):
                nc.vector.tensor_copy(identr, ident).then_inc(a_pad, 1)
                dve.wait_ge(ld_a, 16 * N_A)
                for i in range(NT + 1):
                    if i < NT:
                        qk = v4(PS[:, i % 2, :], 2, 2, 128)
                        sins = v4(rot_tab[:, i % 2, 512:1024], 2, 2, 128)
                        prod = v4(by_sin, 2, 2, 128)
                        dve.wait_ge(a_qk, i + 1)
                        if i >= 1:
                            dve.wait_ge(a_rot, 2 * i)
                        nc.vector.tensor_tensor(by_cos, PS[:, i % 2, :], rot_tab[:, i % 2, 0:512], ALU.mult).then_inc(a_prod, 1)
                        for eo in range(2):
                            nc.vector.tensor_tensor(prod[:, :, eo, :], qk[:, :, 1 - eo, :], sins[:, :, eo, :], ALU.mult).then_inc(a_prod, 1)
                        dve.wait_ge(a_prod, 3 * (i + 1))
                        for j in range(2):
                            c = slice(j * 256, (j + 1) * 256)
                            src = lambda ap: ap[:, c].rearrange("p (e n f) -> p e n f", e=2, n=NH0)
                            nc.vector.tensor_tensor(rot[:, i % 2, c].rearrange("p (n e f) -> p e n f", e=2, n=NH0), src(by_cos), src(by_sin),
                                                    ALU.add).then_inc(a_rot, 1)
                    if i >= 1:
                        for half in range(2):
                            dve.wait_ge(a_tn, 4 * (i - 1) + half + 3)
                            nc.vector.tensor_copy(KTs[:, 4 * half:4 * half + 4, (i - 1) * 128:i * 128], v3(PS[:, 6 + half, :], 4, 128)).then_inc(a_ktev, 1)
                    if i < NT:
                        for j, (stack, low) in enumerate(((Qs, 1), (Ks, 2))):
                            st = stack[:, i % 2, :].rearrange("p (n c d) -> p n c d", c=4, d=HD0)
                            dve.wait_ge(a_hi, 2 * i + j + 1)
                            nc.vector.tensor_tensor(st[:, :, low, :], rot[:, i % 2, j * 256:(j + 1) * 256].rearrange("p (n d) -> p n d", d=HD0),
                                                    st[:, :, 0, :].bitcast(F32), ALU.subtract).then_inc(a_low, 1)
                dve.wait_ge(a_ktev, 2 * NT)

        sT = v3(at(0, "a_sT", 8 * 384), 8, 384)
        yc, ysq = at(12, "a_yc", 512), at(14, "a_ysq", 512)
        z0 = v3(at(16, "a_z0", 512), 2, 256)
        zTh = v3(at(18, "a_zTh", 512, F32R), KT, 256)
        zTl = v3(at(20, "a_zTl", 512, F32R), KT, 256)
        ysmall = at(22, "a_ysmall", 160)
        ysum, ymean, yvar, ysd, yrs = (ysmall[:, 32 * j:32 * j + 32] for j in range(5))
        YT = v3(at(24, "a_YT", 1024), 4, 256)
        KP = v4(at(136, "a_KP", 4096, F32R), 2, 8, 256)
        a_zero, a_even, a_odd = sem("a_zero"), sem("a_even"), sem("a_odd")

        def keys_apart(eng, copy, parity, b, g, done):
            rows = slice(64 * parity, 64 * parity + 64)
            if b >= 1:
                eng.wait_ge(a_s, NH0 * (b - 1) + 2 * g + 2)
            copy(KP[rows, parity, g, :], KTs[rows, g, b * 256:(b + 1) * 256]).then_inc(done, 1)
        with nc.Block() as block:
            n3 = lambda ap: ap.rearrange("p (n d) -> p n d", d=HD0)
            NQ = B * NH0 // 4
            STEPS = range(4 * (B - 1) + 11)
            batch_at = lambda q, first: (q - first) // 4 if q >= first and (q - first) % 4 == 0 and (q - first) // 4 < B else None

            both = lambda ap: ap.rearrange("p (o f) -> p o f", o=1).to_broadcast([P, 2, 256])

            def affine(eng, tensor_tensor, b, key, own):
                eng.wait_ge(a_yn, b + 1)
                link(eng, key, own, tensor_tensor(v3(yc, 2, 256), v3(yc, 2, 256), both(gn_w), ALU.mult))
                link(eng, key, own, tensor_tensor(v3(yc, 2, 256), v3(yc, 2, 256), both(gn_b), ALU.add))
                if b >= 1:
                    eng.wait_ge(a_zt, b)
                tensor_tensor(z0, v3(yc, 2, 256), sgate[:, 2 * b:2 * b + 2, :], ALU.mult).then_inc(a_z, 1)
                eng.wait_ge(a_z, b + 1)

            @block.gpsimd
            def _(pool):
                for g in range(8):
                    keys_apart(pool, nc.gpsimd.tensor_copy, 1, 0, g, a_odd)
                for q in STEPS:
                    if 1 <= q <= NQ - 4:
                        for g in (2 * ((q - 1) % 4), 2 * ((q - 1) % 4) + 1):
                            keys_apart(pool, nc.gpsimd.tensor_copy, 1, (q - 1) // 4 + 1, g, a_odd)
                    if batch_at(q, 6) is not None and batch_at(q, 6) < B - 1:
                        pool.wait_ge(a_odd, 8 + 2 * min(q, NQ - 4))
                        affine(pool, nc.gpsimd.tensor_tensor, batch_at(q, 6), "p", s_pool)

            @block.tensor
            def _(pe):
                def scores(m):
                    b, n = m // NH0, m % NH0
                    g = n // 2
                    if m < 2:
                        pe.wait_ge(a_zero, m + 1)
                    pe.wait_ge(a_odd if n % 2 else a_even, 8 * b + g + 1)
                    if m >= 3:
                        pe.wait_ge(a_sev, m - 2)
                    keys = KP[:, n % 2, g, :]
                    nc.tensor.matmul(PS[:, m % 3, 0:256], keys[:, 0:128], QT[:, g, b * 256:b * 256 + 256], start=True, stop=True)
                    nc.tensor.matmul(PS[:, m % 3, 256:384], keys[:, 128:256], QT[:, g, b * 256 + 128:b * 256 + 256],
                                     start=True, stop=True).then_inc(a_s, 1)

                def mix(q):
                    b = q // 4
                    pe.wait_ge(a_sev, 4 * q + 4)
                    if q >= 1:
                        pe.wait_ge(a_ytev, q)
                    for r in range(4):
                        n, rows = (4 * q + r) % NH0, slice(32 * r, 32 * r + 32)
                        s = sT[:, (4 * q + r) % 8, :]
                        nc.tensor.matmul(PS[rows, 3, 0:256], v0[:, 2 * b, n, :], s[:, 0:256], start=True, stop=False,
                                         tile_position=(0, 32 * r))
                        last = nc.tensor.matmul(PS[rows, 3, 128:256], v0[:, 2 * b + 1, n, :], s[:, 256:384], start=False, stop=True,
                                                tile_position=(0, 32 * r))
                    last.then_inc(a_pv, 1)

                def outputs(b):
                    pe.wait_ge(a_ytev, 4 * b + 4)
                    if b >= 1:
                        pe.wait_ge(a_yread, b)
                    for i in range(2):
                        for g in range(4):
                            last = nc.tensor.transpose(PS[:, 4 + i, g * 128:(g + 1) * 128], YT[:, g, i * 128:(i + 1) * 128], ident)
                    last.then_inc(a_yt, 1)

                def turn(b):
                    pe.wait_ge(a_z, b + 1)
                    if b >= 1:
                        pe.wait_ge(a_ztl, b)
                    for i in range(2):
                        for k in range(KT):
                            last = nc.tensor.transpose(PS[:, 6, k * 256 + i * 128:k * 256 + i * 128 + 128],
                                                       z0[:, i, k * 128:(k + 1) * 128], ident)
                    last.then_inc(a_zt, 1)

                def project(b):
                    pe.wait_ge(a_ztl, b + 1)
                    if b == 0:
                        pe.wait_ge(a_wo, 2)
                    else:
                        pe.wait_ge(a_xadd, b)
                    for i in range(2):
                        t = slice(i * 128, (i + 1) * 128)
                        for k in range(KT):
                            last = mm3(PS[:, 7, i * 256:(i + 1) * 256], (zTh[:, k, t], zTl[:, k, t]), (woh[:, k, :], wol[:, k, :]),
                                       k == 0, k == 1)
                    last.then_inc(a_o, 1)

                for q in STEPS:
                    if q < NQ:
                        for r in range(4):
                            scores(4 * q + r)
                    if 1 <= q <= NQ:
                        mix(q - 1)
                    for first, stage in ((5, outputs), (9, turn), (10, project)):
                        if batch_at(q, first) is not None:
                            stage(batch_at(q, first))

            @block.scalar
            def _(act):
                def moved(q):
                    act.wait_ge(a_pv, q + 1)
                    if q >= 4:
                        act.wait_ge(a_yt, q // 4)
                    nc.scalar.copy(YT[:, q % 4, :], PS[:, 3, 0:256]).then_inc(a_ytev, 1)

                def root(b):
                    act.wait_ge(a_var, b + 1)
                    nc.scalar.activation(ysd, yvar, ACT.Sqrt, bias=eps_t[:, 0:1], scale=1.0 / HD0).then_inc(a_sd, 1)

                def high(b):
                    act.wait_ge(a_zt, b + 1)
                    if b >= 1:
                        act.wait_ge(a_o, b)
                    nc.scalar.copy(zTh, v3(PS[:, 6, :], KT, 256)).then_inc(a_zth, 1)

                for g in range(8):
                    keys_apart(act, nc.scalar.copy, 0, 0, g, a_even)
                for q in STEPS:
                    if 1 <= q <= NQ:
                        moved(q - 1)
                    if 1 <= q <= NQ - 4:
                        for g in (2 * ((q - 1) % 4), 2 * ((q - 1) % 4) + 1):
                            keys_apart(act, nc.scalar.copy, 0, (q - 1) // 4 + 1, g, a_even)
                    for first, stage in ((6, root), (9, high)):
                        if batch_at(q, first) is not None:
                            stage(batch_at(q, first))

            @block.vector
            def _(dve):
                for parity in range(2):
                    rows = slice(64 * (1 - parity), 64 * (1 - parity) + 64)
                    nc.vector.memset(KP[rows, parity, :, :].bitcast(F32), 0.0).then_inc(a_zero, 1)
                wide = lambda ap: ap.rearrange("p (n o) -> p n o", o=1).to_broadcast([P, 32, HD0])
                y = PS[:, 4:6, :].rearrange("p i (n c) -> p (i n) c", c=32)[:, :, 0:HD0]

                def mask(m):
                    dve.wait_ge(a_s, m + 1)
                    if m >= 8:
                        dve.wait_ge(a_pv, m // 4 - 1)
                    nc.vector.tensor_tensor(sT[:, m % 8, :], PS[:, m % 3, 0:384], mask_ret, ALU.mult).then_inc(a_sev, 1)

                def means(b):
                    dve.wait_ge(a_yt, b + 1)
                    link(dve, "v", s_vec, nc.vector.tensor_reduce(ysum, y, AX.X, ALU.add))
                    link(dve, "v", s_vec, nc.vector.tensor_scalar(ymean, ysum, 1.0 / HD0, None, ALU.mult))

                def centre(b):
                    if b >= 1:
                        dve.wait_ge(a_z, b)
                    nc.vector.tensor_tensor(n3(yc), y, wide(ymean), ALU.subtract).then_inc(a_yread, 1)

                def variances(b):
                    dve.wait_ge(a_yread, b + 1)
                    link(dve, "v", s_vec, nc.vector.tensor_tensor(ysq, yc, yc, ALU.mult))
                    nc.vector.tensor_reduce(yvar, n3(ysq), AX.X, ALU.add).then_inc(a_var, 1)

                def normed(b):
                    dve.wait_ge(a_sd, b + 1)
                    link(dve, "v", s_vec, nc.vector.reciprocal(yrs, ysd))
                    nc.vector.tensor_tensor(n3(yc), n3(yc), wide(yrs), ALU.mult).then_inc(a_yn, 1)
                    if b == B - 1:
                        affine(dve, nc.vector.tensor_tensor, b, "v", s_vec)

                def low(b):
                    dve.wait_ge(a_zth, b + 1)
                    nc.vector.tensor_tensor(zTl, v3(PS[:, 6, :], KT, 256), zTh.bitcast(F32), ALU.subtract).then_inc(a_ztl, 1)

                def add(b):
                    dve.wait_ge(a_o, b + 1)
                    nc.vector.tensor_tensor(x[:, 2 * b:2 * b + 2, :], x[:, 2 * b:2 * b + 2, :], v3(PS[:, 7, :], 2, 256),
                                            ALU.add).then_inc(a_xadd, 1)

                for q in STEPS:
                    for r in range(4):
                        if q < NQ:
                            mask(4 * q + r)
                        for first, after, stage in ((5, 3, means), (6, 0, centre), (6, 1, variances), (10, 0, low), (10, 3, add),
                                                    (6, 3, normed)):
                            if r == after and batch_at(q, first) is not None:
                                stage(batch_at(q, first))
                dve.wait_ge(a_xadd, B)

        kvT = SC[0:64, 1024:2048]
        kvs = R2[:, 0:512].rearrange("p (i d) -> p i d", d=CD)
        oT = v3(R2[0:64, 4096:5120], 4, 256)
        sim = v4(R2[:, 1024:2048], 2, 2, 256)
        att = v4(R2[:, 2048:3072], 2, 2, 256)
        bstat = v3(R2[:, 3072:3072 + 48], NT, 6)
        bmv = v3(R2[:, 3120:3136], NT, 2)
        bsd, brs, bmx, bsum, bri = (R2[:, 3136 + 8 * j:3144 + 8 * j] for j in range(5))
        b_kv, b_kvev, b_o, b_oev, b_sim, b_var, b_sd, b_norm, b_affine, b_max, b_exp, b_read = (
            sem(f"b_{n}") for n in ("kv", "kvev", "o", "oev", "sim", "var", "sd", "norm", "affine", "max", "exp", "read"))

        def keys(pe):
            pe.wait_ge(ld_b, 16 * N_B)
            for c in range(2):
                nc.tensor.matmul(PS[0:64, 4 + c, :], wkT, ctxT[:, c * 512:(c + 1) * 512], start=True, stop=True).then_inc(b_kv, 1)
            for i in range(NT):
                last = nc.tensor.matmul(PS[:, 6, i * 64:(i + 1) * 64], ctxT[:, i * 128:(i + 1) * 128], wkT, start=True, stop=True)
            last.then_inc(b_kv, 1)

        def keys_by_feature(act):
            for c in range(2):
                act.wait_ge(b_kv, c + 1)
                nc.scalar.activation(kvT[:, c * 512:(c + 1) * 512], PS[0:64, 4 + c, :], ACT.Identity, bias=bk_col).then_inc(b_kvev, 1)

        def keys_by_token(dve):
            dve.wait_ge(b_kv, 3)
            nc.vector.tensor_tensor(kvs, PS[:, 6, :].rearrange("p (i d) -> p i d", d=CD),
                                    bk_row.rearrange("p (o d) -> p o d", o=1).to_broadcast([P, NT, CD]), ALU.add).then_inc(b_kvev, 1)

        layer_norm("B", tensor_before=keys, scalar_beside=keys_by_feature, vector_after=keys_by_token)
        with nc.Block() as block:
            def pair(ap, b):
                return ap[:, 2 * b:2 * b + 2]

            @block.gpsimd
            def _(pool):
                both = lambda ap: ap.rearrange("p (o f) -> p o f", o=1).to_broadcast([P, 2, 256])
                for b in range(B):
                    pool.wait_ge(b_norm, 2 * (b + 1))
                    s = sim[:, b % 2, :, :]
                    link(pool, "p", s_pool, nc.gpsimd.tensor_tensor(s, s, both(xg_row[:, 0:256]), ALU.mult))
                    nc.gpsimd.tensor_tensor(s, s, both(xg_row[:, 256:512]), ALU.add).then_inc(b_affine, 1)
                nc.gpsimd.tensor_copy(ctx_h, ctxT).then_inc(ctx_split, 1)
                pool.wait_ge(ctx_split, 1)
                nc.gpsimd.tensor_tensor(ctx_l, ctxT, ctx_h.bitcast(F32), ALU.subtract).then_inc(ctx_split, 1)

            @block.sync
            def _(sp):
                for e in range(3):
                    sp.dma_start(c_raw[:, e, :], ins["wexp"][:, e, :]).then_inc(ld_exp[e], 16)
                sp.wait_ge(ctx_split, 2)
                sp.dma_start(ctx_parts[0], ctx_h.bitcast(F32)).then_inc(ctx_stored, 16)
                sp.dma_start(ctx_parts[1], ctx_l.bitcast(F32)).then_inc(ctx_stored, 16)

            @block.tensor
            def _(pe):
                def out(b):
                    for k in range(KT):
                        last = nc.tensor.matmul(PS[0:64, b, 0:256], kvs[:, 2 * b + k, :], hT[:, k, b * 256:(b + 1) * 256],
                                                start=k == 0, stop=k == 1)
                    last.then_inc(b_o, 1)

                def similar(b):
                    pe.wait_ge(b_oev, b + 1)
                    for i in range(2):
                        last = nc.tensor.matmul(PS[:, 4 + b, i * 256:(i + 1) * 256], oT[:, b, i * 128:(i + 1) * 128],
                                                kvT[:, b * 256:(b + 1) * 256], start=True, stop=True)
                    last.then_inc(b_sim, 1)

                pe.wait_ge(b_kvev, 3)
                out(0)
                for b in range(B):
                    if b + 1 < B:
                        out(b + 1)
                    similar(b)

            @block.scalar
            def _(act):
                def scaled_out(b):
                    act.wait_ge(b_o, b + 1)
                    nc.scalar.activation(oT[:, b, :], PS[0:64, b, 0:256], ACT.Copy, scale=1.0 / 16.0).then_inc(b_oev, 1)

                def root(b):
                    act.wait_ge(b_var, b + 1)
                    nc.scalar.activation(pair(bsd, b), pair(bmv, b)[:, :, 1], ACT.Sqrt, bias=eps_t[:, 1:2]).then_inc(b_sd, 1)

                def exponentials(b):
                    act.wait_ge(b_max, b + 1)
                    if b >= 2:
                        act.wait_ge(b_read, 2 * (b - 1))
                    for t in range(2):
                        i = 2 * b + t
                        nc.scalar.activation(att[:, b % 2, t, :], sim[:, b % 2, t, :], ACT.Exp, bias=bmx[:, i:i + 1],
                                             accum_out=bsum[:, i:i + 1]).then_inc(b_exp, 1)

                scaled_out(0)
                scaled_out(1)
                root(0)
                scaled_out(2)
                root(1)
                scaled_out(3)
                exponentials(0)
                root(2)
                exponentials(1)
                root(3)
                exponentials(2)
                exponentials(3)

            @block.vector
            def _(dve):
                L = lambda inst: link(dve, "v", s_vec, inst)

                def variances(b):
                    dve.wait_ge(b_sim, b + 1)
                    for t in range(2):
                        nc.vector.bn_stats(bstat[:, 2 * b + t, :], PS[:, 4 + b, t * 256:(t + 1) * 256]).then_inc(s_vec, 1)
                        chain["v"] += 1
                    dve.wait_ge(s_vec, chain["v"])
                    for t in range(2):
                        last = nc.vector.bn_aggr(bmv[:, 2 * b + t, :], bstat[:, 2 * b + t, :])
                    last.then_inc(b_var, 1)

                def normed(b):
                    dve.wait_ge(b_sd, b + 1)
                    L(nc.vector.reciprocal(pair(brs, b), pair(bsd, b)))
                    if b >= 2:
                        dve.wait_ge(b_exp, 2 * (b - 1))
                    for t in range(2):
                        i = 2 * b + t
                        nc.vector.tensor_scalar(sim[:, b % 2, t, :], PS[:, 4 + b, t * 256:(t + 1) * 256], bmv[:, i, 0:1], brs[:, i:i + 1],
                                                ALU.subtract, ALU.mult).then_inc(b_norm, 1)

                def peaks(b):
                    dve.wait_ge(b_affine, b + 1)
                    L(nc.vector.tensor_reduce(pair(rin, b), sim[:, b % 2, :, :], AX.X, ALU.max))
                    nc.vector.tensor_scalar(pair(bmx, b), pair(rin, b), -1.0, None, ALU.mult).then_inc(b_max, 1)

                def finish(b):
                    dve.wait_ge(b_exp, 2 * (b + 1))
                    L(nc.vector.reciprocal(pair(bri, b), pair(bsum, b)))
                    for t in range(2):
                        i = 2 * b + t
                        nc.vector.scalar_tensor_tensor(x[:, i, :], att[:, b % 2, t, :], bri[:, i:i + 1], x[:, i, :],
                                                       ALU.mult, ALU.add).then_inc(b_read, 1)

                for b in range(B + 2):
                    if b < B:
                        variances(b)
                        normed(b)
                    if 1 <= b <= B:
                        peaks(b - 1)
                    if b >= 2:
                        finish(b - 2)
                dve.wait_ge(b_read, NT)

        layer_norm("C", split=True)
        c_wh = v3(at(0, "c_wh", 2 * 1536, F32R), 2, 1536)
        c_wl = v3(at(12, "c_wl", 2 * 1536, F32R), 2, 1536)
        CR = at(24, "CR", 2048)
        RT = v3(CR[:, 0:768], 12, 64)
        cmp8 = CR[:, 768:1280]
        cmp8b = CR[:, 1280:1792]
        hidf = v3(at(32, "c_hidf", 1024), 2, 512)
        hidh = v4(at(36, "c_hidh", 2048, F32R), 2, KT, 512)
        hidl = v4(at(44, "c_hidl", 2048, F32R), 2, KT, 512)
        sgc = v3(at(52, "c_sg", 1024), 2, 512)
        inv_t = small[:, 209:210]
        z_rows = at(56, "c_zrows", 1024)[0:E0, :]
        c_z, c_dist, c_w = (sem(f"c_{n}") for n in ("z", "dist", "w"))
        c_g, c_silu, c_hid, c_high, c_low, c_dn, c_add, c_temp = (
            sem(f"c_{n}") for n in ("g", "silu", "hid", "high", "low", "dn", "add", "temp"))
        c_zread, c_whi, c_wlo = sem("c_zread"), sem("c_whi"), sem("c_wlo")

        def cw(part, e):
            return [v3(part[:, e % 2, j * 512:(j + 1) * 512], KT, 256) for j in range(3)]

        c_wr = sem("c_wr")
        wrh = sb("wrh", [P, KT, E0], F32R)[:, :, :]
        wrl = sb("wrl", [P, KT, E0], F32R)[:, :, :]
        d_raw = v3(at(60, "d_raw", 3 * 1280), 3, 1280)
        qkvb = at(75, "qkvb", 6144).rearrange("p (n w) -> p n w", n=NH1)
        ld_head = [sem(f"ld_head{j}") for j in range(3)]
        CENTER = float(np.float32(1.0 / np.e))
        LOWER = float(np.float32(0.5 - np.log(4.0 / 3.0)))
        with nc.Block() as block:
            cunits = [(e, c) for e in range(E0) for c in range(2)]
            NC = len(cunits)

            @block.gpsimd
            def _(pool):
                for e in range(E0):
                    pool.wait_ge(c_whi, e + 1)
                    nc.gpsimd.tensor_tensor(c_wl[:, e % 2, :], c_raw[:, e % 3, :], c_wh[:, e % 2, :].bitcast(F32),
                                            ALU.subtract).then_inc(c_wlo, 1)

            @block.sync
            def _(sp):
                for e in range(3, E0):
                    sp.wait_ge(c_whi, e - 2)
                    sp.wait_ge(c_wlo, e - 2)
                    sp.dma_start(c_raw[:, e % 3, :], ins["wexp"][:, e, :]).then_inc(ld_exp[e % 3], 16)
                for n in range(3):
                    sp.dma_start(d_raw[:, n, :], ins["w1"][:, n, :]).then_inc(ld_head[n], 16)
                sp.dma_start(qkvb.rearrange("p n w -> p (n w)"), bcast_row(ins["qkvb"], 6144)).then_inc(ld_d, 16)
                sp.dma_start(bw1, ins["bw1"]).then_inc(ld_d, 16)
                sp.dma_start(bb1, bcast_row(ins["bb1"], 16)).then_inc(ld_d, 16)
                sp.dma_start(ob1, bcast_row(ins["ob1"], 256)).then_inc(ld_d, 16)

            @block.tensor
            def _(pe):
                pe.wait_ge(c_wr, 1)
                narrow(4, wrh, wrl, E0).then_inc(c_z, 1)
                pe.wait_ge(c_zread, 1)
                rows_turned(7, z_rows, E0).then_inc(c_z, 1)

                def up(u):
                    e, c = cunits[u]
                    for m in range(KT):
                        v = 2 * u + m
                        if c == 0:
                            pe.wait_ge(c_wlo, e + 1)
                        if v >= 2:
                            pe.wait_ge(c_hid, v - 1)
                        for j in range(2):
                            for k in range(KT):
                                cols, tok = slice(m * 128, (m + 1) * 128), slice(c * 512, (c + 1) * 512)
                                last = mm3(PS[:, 2 * (v % 2) + j, :], (cw(c_wh, e)[j][:, k, cols], cw(c_wl, e)[j][:, k, cols]),
                                           (hTh[:, k, tok], hTl[:, k, tok]), k == 0, k == 1)
                            last.then_inc(c_g, 1)

                def down(u):
                    e, c = cunits[u]
                    pe.wait_ge(c_low, 2 * u + 2)
                    if u == 1:
                        pe.wait_ge(c_zread, 2)
                    if u >= 2:
                        pe.wait_ge(c_add, 4 * (u - 1))
                    for i in range(4):
                        for k in range(KT):
                            tok = slice(i * 128, (i + 1) * 128)
                            last = mm3(PS[:, 4 + 2 * (u % 2) + i // 2, (i % 2) * 256:(i % 2) * 256 + 256],
                                       (hidh[:, u % 2, k, tok], hidl[:, u % 2, k, tok]),
                                       (cw(c_wh, e)[2][:, k, :], cw(c_wl, e)[2][:, k, :]), k == 0, k == 1)
                        last.then_inc(c_dn, 1)

                up(0)
                for u in range(1, len(cunits)):
                    up(u)
                    down(u - 1)
                down(len(cunits) - 1)

            @block.scalar
            def _(act):
                def split(e):
                    act.wait_ge(ld_exp[e % 3], 16 * (e // 3 + 1))
                    if e >= 2:
                        act.wait_ge(c_dn, 4 * 2 * (e - 1))
                    nc.scalar.copy(c_wh[:, e % 2, :], c_raw[:, e % 3, :]).then_inc(c_whi, 1)

                def high(v):
                    act.wait_ge(c_hid, v + 1)
                    u = v // 2
                    if u >= 2:
                        act.wait_ge(c_dn, 4 * (u - 1))
                    nc.scalar.copy(hidh[:, u % 2, v % 2, :], hidf[:, v % 2, :]).then_inc(c_high, 1)

                split(0)
                act.wait_ge(c_z, 1)
                nc.scalar.copy(z_rows, PS[0:E0, 4:6, :].rearrange("p b t -> p (b t)")).then_inc(c_zread, 1)
                split(1)
                act.wait_ge(c_temp, 1)
                act.wait_ge(c_z, 2)
                nc.scalar.activation(RT[:, 0, :], PS[:, 7, 0:64], ACT.Exp, scale=small[:, 210:211]).then_inc(c_zread, 1)
                act.wait_ge(c_dist, 1)
                nc.scalar.activation(RT[:, 2, :], RT[:, 1, :], ACT.Exp, scale=-10.0)
                nc.scalar.activation(RT[:, 3, :], RT[:, 1, :], ACT.Exp, scale=-1.0 / 0.3).then_inc(c_w, 1)
                for u in range(len(cunits)):
                    for m in range(KT):
                        v = 2 * u + m
                        act.wait_ge(c_g, 2 * v + 1)
                        if v >= 2:
                            act.wait_ge(c_hid, v - 1)
                        nc.scalar.activation(sgc[:, v % 2, :], PS[:, 2 * (v % 2), :], ACT.Silu).then_inc(c_silu, 1)
                        if v >= 1:
                            high(v - 1)
                    e, c = cunits[u]
                    if c == 0 and 1 <= e < E0 - 1:
                        split(e + 1)
                high(2 * NC - 1)

            @block.vector
            def _(dve):
                L = lambda inst: link(dve, "v", s_vec, inst)
                r = lambda j: RT[:, j, :]
                r3 = lambda j: RT[:, j, :].rearrange("p (i e) -> p i e", e=E0)
                dve.wait_ge(ld_moe, 16 * N_MOE)
                L(nc.vector.tensor_copy(wrh, wr))
                nc.vector.tensor_tensor(wrl, wr, wrh.bitcast(F32), ALU.subtract).then_inc(c_wr, 1)
                L(nc.vector.reciprocal(inv_t, temp))
                nc.vector.tensor_scalar(small[:, 210:211], inv_t, -1.0, None, ALU.mult).then_inc(c_temp, 1)
                dve.wait_ge(c_zread, 2)
                L(nc.vector.tensor_scalar(r(4), r(0), 1.0, None, ALU.add))
                L(nc.vector.reciprocal(r(5), r(4)))
                L(nc.vector.tensor_scalar(r(6), r(5), CENTER, None, ALU.subtract))
                nc.vector.scalar_tensor_tensor(r(1), r(6), -1.0, r(6), ALU.mult, ALU.max).then_inc(c_dist, 1)
                L(nc.vector.tensor_scalar(r(7), r(5), LOWER, None, ALU.is_ge))
                L(nc.vector.scalar_tensor_tensor(r(8), r(5), 0.5, r(7), ALU.is_le, ALU.mult))
                dve.wait_ge(c_w, 1)
                L(nc.vector.tensor_tensor(r(9), r(2), r(8), ALU.mult))
                w8 = small[:, 576:584]
                L(nc.vector.tensor_reduce(w8, r3(9), AX.X, ALU.add))
                no = small[:, 584:592]
                L(nc.vector.tensor_scalar(no, w8, 1e-8, None, ALU.is_lt))
                a4 = RT[:, 3, :].rearrange("p (i e o) -> p i e o", e=E0, o=1).to_broadcast([P, NT, E0, E0])
                b4 = RT[:, 3, :].rearrange("p (i o e) -> p i o e", e=E0, o=1).to_broadcast([P, NT, E0, E0])
                c4 = cmp8.rearrange("p (i e f) -> p i e f", e=E0, f=E0)
                d4 = cmp8b.rearrange("p (i e f) -> p i e f", e=E0, f=E0)
                L(nc.vector.tensor_tensor(c4, b4, a4, ALU.is_gt))
                L(nc.vector.tensor_tensor(d4, b4, a4, ALU.is_equal))
                for e in range(E0):
                    if e:
                        L(nc.vector.tensor_tensor(c4[:, :, e, 0:e], c4[:, :, e, 0:e], d4[:, :, e, 0:e], ALU.add))
                L(nc.vector.tensor_reduce(r(4), cmp8.rearrange("p (i f) -> p i f", f=E0), AX.X, ALU.add))
                L(nc.vector.scalar_tensor_tensor(r(6), r(4), 1.5, r(3), ALU.is_lt, ALU.mult))
                f8, fi = small[:, 592:600], small[:, 600:608]
                L(nc.vector.tensor_reduce(f8, r3(6), AX.X, ALU.add))
                L(nc.vector.tensor_scalar(f8, f8, 1e-8, None, ALU.max))
                L(nc.vector.reciprocal(fi, f8))
                wide = lambda a: a.rearrange("p (i o) -> p i o", o=1).to_broadcast([P, NT, E0])
                L(nc.vector.tensor_tensor(r3(6), r3(6), wide(fi), ALU.mult))
                L(nc.vector.tensor_tensor(r3(6), r3(6), wide(no), ALU.mult))
                L(nc.vector.tensor_scalar(no, no, -1.0, 1.0, ALU.mult, ALU.add))
                L(nc.vector.tensor_tensor(r3(9), r3(9), wide(no), ALU.mult))
                L(nc.vector.tensor_tensor(r(9), r(9), r(6), ALU.add))
                L(nc.vector.tensor_reduce(w8, r3(9), AX.X, ALU.add))
                L(nc.vector.tensor_scalar(w8, w8, 1e-8, None, ALU.max))
                L(nc.vector.reciprocal(fi, w8))
                L(nc.vector.tensor_tensor(r3(10), r3(9), wide(fi), ALU.mult))

                def product(v):
                    u, m = v // 2, v % 2
                    dve.wait_ge(c_silu, v + 1)
                    dve.wait_ge(c_g, 2 * v + 2)
                    if v >= 2:
                        dve.wait_ge(c_low, v - 1)
                    nc.vector.tensor_tensor(hidf[:, v % 2, :], PS[:, 2 * (v % 2) + 1, :], sgc[:, v % 2, :],
                                            ALU.mult).then_inc(c_hid, 1)

                def low(v):
                    u, m = v // 2, v % 2
                    dve.wait_ge(c_high, v + 1)
                    nc.vector.tensor_tensor(hidl[:, u % 2, m, :], hidf[:, v % 2, :], hidh[:, u % 2, m, :].bitcast(F32),
                                            ALU.subtract).then_inc(c_low, 1)

                def add(u):
                    e, c = cunits[u]
                    for i in range(4):
                        dve.wait_ge(c_dn, 4 * u + 2 * (i // 2) + 2)
                        ti = 4 * c + i
                        if u >= 2:
                            dve.wait_ge(c_add, 4 * (u - 2) + i + 1)
                        nc.vector.scalar_tensor_tensor(
                            x[:, ti, :], PS[:, 4 + 2 * (u % 2) + i // 2, (i % 2) * 256:(i % 2) * 256 + 256],
                            RT[:, 10, 8 * ti + e:8 * ti + e + 1], x[:, ti, :], ALU.mult, ALU.add).then_inc(c_add, 1)

                for v in range(2 * NC):
                    product(v)
                    if v >= 1:
                        low(v - 1)
                    if v % 2 == 1 and v >= 3:
                        add(v // 2 - 1)
                low(2 * NC - 1)
                add(NC - 1)
                dve.wait_ge(c_add, 4 * len(cunits))

        layer_norm("D", split=True)
        DS = at(0, "DS", 512).rearrange("p (a b) -> p a b", b=64)
        sel_raw = at(154, "sel_raw", 2048)
        sel = at(146, "sel", 2048, F32R).rearrange("p (j m) -> p j m", j=16)
        KZ = [at(kb, f"KZ{j}", 8192, F32R).rearrange("p (v g t) -> p v g t", v=KVH, g=GRP) for j, kb in enumerate((2, 114))]

        def clear_keys(pool, buf, done):
            nc.gpsimd.memset(buf.bitcast(F32), 0.0).then_inc(z_clear, 1)
            for g in range(GRP):
                pool.wait_ge(z_clear, done + 1 + g)
                nc.gpsimd.memset(buf[32 * g:32 * g + 32, :, g, :].bitcast(F32), 1.0).then_inc(z_clear, 1)
            pool.wait_ge(z_clear, done + 1 + GRP)

        def load_keys(sp, b, half):
            v = slice(4 * half, 4 * half + 4)
            for g in range(GRP):
                for j, part in enumerate((0, 0, 1)):
                    r0 = 32 * g + HD2 * j
                    sp.dma_start(KZ[b % 2][r0:r0 + HD2, v, g, :].bitcast(F32),
                                 ctx_parts[part].rearrange("(v d) t -> d v t", d=HD2)[:, v, b * 256:(b + 1) * 256]).then_inc(ld_keys[half], 16)

        dwh = v3(at(99, "d_wh", 2048, F32R), 2, 1024)
        dwl = v3(at(107, "d_wl", 2048, F32R), 2, 1024)
        owh = v3(at(115, "d_owh", 768, F32R), 3, 256)
        owl = v3(at(118, "d_owl", 768, F32R), 3, 256)
        tok_qkv = v4(at(121, "d_tok", 3072), 2, 4, 384)
        sq = v3(at(133, "d_sq", 1024), 4, 256)
        qT1, kT1, gate1, st1, zf = (v3(at(34 + 4 * j, f"d_act{j}", 1024), 2, 512) for j in range(5))
        zh = v3(at(137, "d_zh", 1024, F32R), 2, 512)
        zl = v3(at(141, "d_zl", 1024, F32R), 2, 512)
        ssum = DS[:, 2, 0:8]
        nrm = DS[:, 3, 0:8]
        floor = DS[:, 4, 16:24]
        inv = DS[:, 4, 8:16]
        scale_k = DS[:, 4, 0:4]
        beta_v = DS[:, 0:2, :].rearrange("p a b -> p (a b)")
        zb_rows = at(54, "d_zrows", 1024)[0:NH1, :]
        bwh = sb("bwh", [P, KT, NH1], F32R)[:, :, :]
        bwl = sb("bwl", [P, KT, NH1], F32R)[:, :, :]
        d_z, d_zp, d_t, d_tk, d_tq, d_g = (sem(f"d_{n}") for n in ("z", "zp", "t", "tk", "tq", "g"))
        d_qev, d_kev, d_gev, d_tev, d_sq, d_ss, d_nks, d_qs, d_kr = (
            sem(f"d_{n}") for n in ("qev", "kev", "gev", "tev", "sq", "ss", "nks", "qs", "kr"))
        d_s, d_sev, d_o, d_z1, d_zh, d_zl, d_acc, d_xadd, d_b1, d_b2 = (
            sem(f"d_{n}") for n in ("s", "sev", "o", "z1", "zh", "zl", "acc", "xadd", "b1", "b2"))
        d_x0, d_bw, d_whi, d_wlo, d_zrows = (sem(f"d_{n}") for n in ("x0", "bw", "whi", "wlo", "zrows"))
        with nc.Block() as block:
            dunits = [(n, c) for n in range(NH1) for c in range(2)]
            ND = len(dunits)

            TILE, KEYS, QUERIES, SCORES, GATE, OUTS = (0, 1, 3, 5), 2, 4, 6, 7, 8

            def bank(s, turn):
                return PS[:, (9 * s + turn) % 4, :]

            @block.gpsimd
            def _(pool):
                def low(n):
                    pool.wait_ge(d_whi, 2 * n + 1)
                    nc.gpsimd.tensor_tensor(dwl[:, n % 2, :], d_raw[:, n % 3, 0:1024], dwh[:, n % 2, :].bitcast(F32),
                                            ALU.subtract).then_inc(d_wlo, 1)
                    pool.wait_ge(d_whi, 2 * n + 2)
                    nc.gpsimd.tensor_tensor(owl[:, n % 3, :], d_raw[:, n % 3, 1024:1280], owh[:, n % 3, :].bitcast(F32),
                                            ALU.subtract).then_inc(d_wlo, 1)

                low(0)
                low(1)
                for u in range(ND):
                    if u == 2:
                        clear_keys(pool, KZ[0], 0)
                    n, c = dunits[u]
                    if u >= 1:
                        pool.wait_ge(d_ss, u)
                    for i in range(4):
                        pool.wait_ge(d_tev, 4 * u + i + 1)
                        qk = tok_qkv[:, u % 2, i, 0:256]
                        nc.gpsimd.tensor_tensor(sq[:, i, :], qk, qk, ALU.mult).then_inc(d_sq, 1)
                    if c == 0 and 1 <= n < NH1 - 1:
                        low(n + 1)
                    if u == ND - 4:
                        pool.wait_ge(e_ld, 16)
                        nc.gpsimd.tensor_copy(sel.rearrange("p j m -> p (j m)"), sel_raw).then_inc(e_sel, 1)

            @block.sync
            def _(sp):
                for n in range(3, NH1):
                    sp.wait_ge(d_whi, 2 * (n - 2))
                    sp.wait_ge(d_wlo, 2 * (n - 2))
                    sp.dma_start(d_raw[:, n % 3, :], ins["w1"][:, n, :]).then_inc(ld_head[n % 3], 16)
                    if n == 3:
                        sp.wait_ge(z_clear, 5)
                        sp.wait_ge(ctx_stored, 32)
                        for half in range(2):
                            load_keys(sp, 0, half)
                        sp.dma_start(sel_raw, ins["sel"]).then_inc(e_ld, 16)

            @block.tensor
            def _(pe):
                pe.wait_ge(d_bw, 1)
                narrow(4, bwh, bwl, NH1).then_inc(d_z, 1)

                def tile(s, i):
                    n, c = dunits[s]
                    tok = slice((4 * c + i) * 128, (4 * c + i + 1) * 128)
                    out = bank(s, TILE[i])[:, 0:384]
                    for k in range(KT):
                        w = [part[:, n % 2, 0:768].rearrange("p (j k d) -> p j k d", j=3, k=KT)[:, :, k, :] for part in (dwh, dwl)]
                        last = mm3(v3(out, 3, 128), (hTh[:, k, tok], hTl[:, k, tok]), w, k == 0, k == 1)
                    last.then_inc(d_t, 1)

                def gate(s):
                    n, c = dunits[s]
                    tok = slice(c * 512, (c + 1) * 512)
                    for k in range(KT):
                        o = 768 + k * 128
                        last = mm3(bank(s, GATE), (dwh[:, n % 2, o:o + 128], dwl[:, n % 2, o:o + 128]),
                                   (hTh[:, k, tok], hTl[:, k, tok]), k == 0, k == 1)
                    last.then_inc(d_g, 1)

                def turned(s, turn, j, done):
                    for i in range(4):
                        last = nc.tensor.transpose(bank(s, turn)[:, i * 128:(i + 1) * 128],
                                                   tok_qkv[:, (s - 1) % 2, i, j * 128:(j + 1) * 128], ident)
                    last.then_inc(done, 1)

                def out_proj(u):
                    n, c = dunits[u]
                    pe.wait_ge(d_zl, u + 1)
                    if u == 0:
                        pe.wait_ge(d_zp, 1)
                    for i in range(4):
                        t = slice(i * 128, (i + 1) * 128)
                        last = mm3(PS[:, 4 + 2 * c + i // 2, (i % 2) * 256:(i % 2) * 256 + 256], (zh[:, u % 2, t], zl[:, u % 2, t]),
                                   (owh[:, n % 3, :], owl[:, n % 3, :]), n == 0 and i % 2 == 0, n == NH1 - 1, skip_group_check=True)
                    last.then_inc(d_acc, 1)

                for s in range(ND + 2):
                    if s < ND:
                        pe.wait_ge(d_wlo, 2 * dunits[s][0] + 2)
                        if s >= 1:
                            pe.wait_ge(d_tev, 4 * s)
                        tile(s, 0)
                        if s >= 2:
                            pe.wait_ge(d_sev, 4 * (s - 1))
                        tile(s, 1)
                    if s == 0:
                        pe.wait_ge(d_zrows, 1)
                        rows_turned(7, zb_rows, NH1).then_inc(d_z, 1)
                    if 1 <= s <= ND:
                        pe.wait_ge(d_tev, 4 * s)
                        pe.wait_ge(d_gev, s)
                        turned(s, KEYS, 1, d_tk)
                    if s >= 2:
                        out_proj(s - 2)
                    if s < ND:
                        if s >= 2:
                            pe.wait_ge(d_z1, s - 1)
                        tile(s, 2)
                    if 1 <= s <= ND:
                        pe.wait_ge(d_qs, s)
                        if s < ND:
                            pe.wait_ge(d_tev, 4 * s + 1)
                        turned(s, QUERIES, 0, d_tq)
                    if s < ND:
                        pe.wait_ge(d_tev, 4 * s + 2)
                        tile(s, 3)
                    if 1 <= s <= ND:
                        pe.wait_ge(d_kev, s)
                        pe.wait_ge(d_qev, s)
                        for i in range(4):
                            t = slice(i * 128, (i + 1) * 128)
                            last = nc.tensor.matmul(bank(s, SCORES)[:, t], kT1[:, (s - 1) % 2, t], qT1[:, (s - 1) % 2, t],
                                                    start=True, stop=True)
                        last.then_inc(d_s, 1)
                    if s < ND:
                        pe.wait_ge(d_tev, 4 * s + 3)
                        gate(s)
                    if 1 <= s <= ND:
                        for i in range(4):
                            t = slice(i * 128, (i + 1) * 128)
                            pe.wait_ge(d_sev, 4 * (s - 1) + i + 1)
                            last = nc.tensor.matmul(bank(s, OUTS)[:, t], tok_qkv[:, (s - 1) % 2, i, 256:384], st1[:, (s - 1) % 2, t],
                                                    start=True, stop=True)
                        last.then_inc(d_o, 1)

            @block.scalar
            def _(act):
                def split(n):
                    act.wait_ge(ld_head[n % 3], 16 * (n // 3 + 1))
                    if n >= 2:
                        act.wait_ge(d_g, 2 * (n - 1))
                    nc.scalar.copy(dwh[:, n % 2, :], d_raw[:, n % 3, 0:1024]).then_inc(d_whi, 1)
                    if n >= 3:
                        act.wait_ge(d_acc, 2 * (n - 2))
                    nc.scalar.copy(owh[:, n % 3, :], d_raw[:, n % 3, 1024:1280]).then_inc(d_whi, 1)

                def zhigh(u):
                    act.wait_ge(d_z1, u + 1)
                    if u >= 2:
                        act.wait_ge(d_acc, u - 1)
                    nc.scalar.copy(zh[:, u % 2, :], zf[:, u % 2, :]).then_inc(d_zh, 1)

                def root(u):
                    act.wait_ge(d_ss, u + 1)
                    if u >= 1:
                        act.wait_ge(d_kr, u)
                    nc.scalar.activation(nrm, ssum, ACT.Sqrt).then_inc(d_nks, 1)

                split(0)
                act.wait_ge(d_z, 1)
                nc.scalar.copy(zb_rows, PS[0:NH1, 4:6, :].rearrange("p b t -> p (b t)")).then_inc(d_zrows, 1)
                split(1)
                act.wait_ge(d_b1, 1)
                nc.scalar.activation(DS[:, 5:7, :], DS[:, 5:7, :], ACT.Exp, scale=-1.0).then_inc(s_act, 1)
                chain["a"] += 1
                act.wait_ge(s_act, chain["a"])
                nc.scalar.activation(DS[:, 5:7, :], DS[:, 5:7, :], ACT.Ln, bias=1.0).then_inc(d_b2, 1)
                for s in range(ND + 2):
                    if s >= 2:
                        zhigh(s - 2)
                    if 1 <= s <= ND:
                        root(s - 1)
                        act.wait_ge(d_tk, s)
                        if s >= 3:
                            act.wait_ge(d_s, s - 2)
                        nc.scalar.copy(kT1[:, (s - 1) % 2, :], bank(s, KEYS)).then_inc(d_kev, 1)
                    if s < ND and dunits[s][1] == 0 and 1 <= dunits[s][0] < NH1 - 1:
                        split(dunits[s][0] + 1)
                    if 1 <= s <= ND:
                        act.wait_ge(d_tq, s)
                        nc.scalar.copy(qT1[:, (s - 1) % 2, :], bank(s, QUERIES)).then_inc(d_qev, 1)
                    if s < ND:
                        act.wait_ge(d_g, s + 1)
                        if s >= 2:
                            act.wait_ge(d_z1, s - 1)
                        nc.scalar.activation(gate1[:, s % 2, :], bank(s, GATE), ACT.Silu).then_inc(d_gev, 1)

            @block.vector
            def _(dve):
                L = lambda inst: link(dve, "v", s_vec, inst)

                dve.wait_ge(ld_d, 16 * N_D)
                L(nc.vector.tensor_copy(bwh, bw1))
                nc.vector.tensor_tensor(bwl, bw1, bwh.bitcast(F32), ALU.subtract).then_inc(d_bw, 1)
                zb = beta_v.rearrange("p (i n) -> p i n", n=NH1)
                tmp = DS[:, 5:7, :].rearrange("p a b -> p (a b)").rearrange("p (i n) -> p i n", n=NH1)
                def beta_first():
                    dve.wait_ge(d_z, 2)
                    nc.vector.tensor_tensor(zb, PS[:, 7, 0:128].rearrange("p (i n) -> p i n", n=NH1),
                                            bb1.rearrange("p (o n) -> p o n", o=1).to_broadcast([P, NT, NH1]), ALU.add).then_inc(d_zp, 1)
                    dve.wait_ge(d_zp, 1)
                    nc.vector.scalar_tensor_tensor(tmp, zb, -1.0, zb, ALU.mult, ALU.max).then_inc(d_b1, 1)
                    dve.wait_ge(d_b1, 1)
                    L(nc.vector.tensor_scalar(zb, zb, 0.0, None, ALU.max))

                def beta_last():
                    dve.wait_ge(d_b2, 1)
                    L(nc.vector.tensor_tensor(zb, zb, tmp, ALU.add))

                def biased(u, i):
                    n, c = dunits[u]
                    dve.wait_ge(d_t, 4 * u + i + 1)
                    if i == 0 and u >= 2:
                        dve.wait_ge(d_o, u - 1)
                    nc.vector.tensor_tensor(tok_qkv[:, u % 2, i, :], bank(u, TILE[i])[:, 0:384], qkvb[:, n, :],
                                            ALU.add).then_inc(d_tev, 1)

                def summed(u):
                    dve.wait_ge(d_sq, 4 * (u + 1))
                    nc.vector.tensor_reduce(ssum, sq.rearrange("p i (j d) -> p (i j) d", d=HD1), AX.X, ALU.add).then_inc(d_ss, 1)

                def inverses(u):
                    n, c = dunits[u]
                    dve.wait_ge(d_nks, u + 1)
                    L(nc.vector.tensor_scalar(floor, nrm, 1e-12 * float(HD1) ** 0.5, None, ALU.max))
                    L(nc.vector.reciprocal(inv, floor))
                    if u >= 1:
                        dve.wait_ge(d_sev, 4 * u)
                    nc.vector.tensor_tensor(scale_k, inv.rearrange("p (i j) -> p i j", j=2)[:, :, 1], zb[:, 4 * c:4 * c + 4, n],
                                            ALU.mult).then_inc(d_kr, 1)
                    for i in range(4):
                        q = tok_qkv[:, u % 2, i, 0:128]
                        inst = nc.vector.tensor_scalar(q, q, inv[:, 2 * i:2 * i + 1], None, ALU.mult)
                    inst.then_inc(d_qs, 1)

                def masked(u):
                    dve.wait_ge(d_s, u + 1)
                    dve.wait_ge(d_kr, u + 1)
                    if u >= 2:
                        dve.wait_ge(d_o, u - 1)
                    for i in range(4):
                        t = slice(i * 128, (i + 1) * 128)
                        nc.vector.scalar_tensor_tensor(st1[:, u % 2, t], bank(u + 1, SCORES)[:, t], scale_k[:, i:i + 1], mask_chunk[:, t],
                                                       ALU.mult, ALU.mult).then_inc(d_sev, 1)

                def gated(u):
                    dve.wait_ge(d_o, u + 1)
                    dve.wait_ge(d_gev, u + 1)
                    if u >= 2:
                        dve.wait_ge(d_zl, u - 1)
                    nc.vector.tensor_tensor(zf[:, u % 2, :], bank(u + 1, OUTS), gate1[:, u % 2, :], ALU.mult).then_inc(d_z1, 1)

                def zlow(u):
                    dve.wait_ge(d_zh, u + 1)
                    if u >= 2:
                        dve.wait_ge(d_acc, u - 1)
                    nc.vector.tensor_tensor(zl[:, u % 2, :], zf[:, u % 2, :], zh[:, u % 2, :].bitcast(F32), ALU.subtract).then_inc(d_zl, 1)

                for s in range(ND + 2):
                    if s >= 2:
                        gated(s - 2)
                    if s < ND:
                        biased(s, 0)
                    if s >= 2:
                        zlow(s - 2)
                    if s < ND:
                        biased(s, 1)
                    if s == 0:
                        beta_first()
                    if 1 <= s <= ND:
                        inverses(s - 1)
                    if s < ND:
                        biased(s, 2)
                        biased(s, 3)
                    if s == 0:
                        beta_last()
                    if 1 <= s <= ND:
                        masked(s - 1)
                    if s < ND:
                        summed(s)
                    if s == 0:
                        nc.vector.tensor_tensor(x[:], x[:], ob1.rearrange("p (o f) -> p o f", o=1).to_broadcast([P, NT, H]), ALU.add).then_inc(d_x0, 1)
                dve.wait_ge(d_acc, ND)
                dve.wait_ge(d_x0, 1)
                for j in range(4):
                    nc.vector.tensor_tensor(x[:, 2 * j:2 * j + 2, :], x[:, 2 * j:2 * j + 2, :], v3(PS[:, 4 + j, :], 2, 256),
                                            ALU.add).then_inc(d_xadd, 1)
                dve.wait_ge(d_xadd, 4)

        f_codes = at(90, "f_codes", 6144, I32).rearrange("p (j w) -> p j w", j=8)
        f_scale = at(2, "f_scale", 6144).rearrange("p (j w) -> p j w", j=8)
        QT1 = at(34, "QT1", 2048, F32R).rearrange("p (v t) -> p v t", v=KVH)
        QT2 = at(42, "QT2", 2048, F32R).rearrange("p (v t) -> p v t", v=KVH)
        mT = at(50, "mT", 256, F32R)
        VS = at(52, "VS", 2048).rearrange("p (i v c) -> p i v c", i=NT, v=KVH)
        OS = v3(at(60, "OS", 512), 2, 256)
        mx = v3(at(62, "mx", 128), 2, 64)
        rden = v3(at(63, "rden", 64), 2, 32)
        on = at(64, "on", 512)
        PT = v4(at(66, "PT", 6144), 3, GRP, 512)
        SCALE2 = 1.0 / float(np.sqrt(HD2))

        NW = 2 * 768
        code = at(154, "f_code", 768, I16)
        sign = at(157, "f_sign", 768, I16)
        lin = at(160, "f_lin", 768, BF16)
        val = v3(at(26, "f_val", 1536, BF16), 2, NW)
        wf = at(129, "f_wf", 1536)
        fwh = v3(at(135, "f_wh", 3072, F32R), 2, NW)
        fwl = v3(at(33, "f_wl", 3072, F32R), 2, NW)
        gel = v3(at(45, "f_gel", 1024), 2, 512)
        hf = v3(at(49, "f_hf", 1024), 2, 512)
        hh = v3(at(53, "f_hh", 1536, F32R), 3, 512)
        hl = v3(at(59, "f_hl", 1536, F32R), 3, 512)
        NSTEP = NB // 2
        f_val, f_wf, f_wh, f_wl = (sem(f"f_{n}") for n in ("val", "wf", "wh", "wl"))
        def dequant(dve, j):
            src = f_codes[:, j, :].bitcast(I16)[:, 0::2]
            L = lambda inst: link(dve, "v", s_vec, inst)
            if j >= 2:
                dve.wait_ge(f_wf, j - 1)
            for parity in range(2):
                sl = slice(768 * parity, 768 * parity + 768)
                L(nc.vector.tensor_scalar(code[:, sl], src, 6 - 4 * parity, 0x1C0, ALU.logical_shift_left, ALU.bitwise_and))
                L(nc.vector.tensor_scalar(sign[:, sl], src, 12 - 4 * parity, -32768, ALU.logical_shift_left, ALU.bitwise_and))
            v = val[:, j % 2, :]
            L(nc.vector.tensor_scalar(code, code, 0x3E00, None, ALU.bitwise_or))
            L(nc.vector.tensor_scalar(lin, code.bitcast(BF16), 8.0, -1.0, ALU.mult, ALU.add))
            L(nc.vector.tensor_scalar(v, code.bitcast(BF16), 4.0, None, ALU.mult))
            L(nc.vector.tensor_tensor(v, lin, v, ALU.min))
            nc.vector.tensor_tensor(v.bitcast(I16), v.bitcast(I16), sign, ALU.bitwise_or).then_inc(f_val, 1)
            dve.wait_ge(f_val, j + 1)

        def scaled(pool, j):
            nc.gpsimd.tensor_tensor(wf.rearrange("p (y w) -> p y w", y=2), val[:, j % 2, :].rearrange("p (y w) -> p y w", y=2),
                                    f_scale[:, j:j + 1, :].to_broadcast([P, 2, 768]), ALU.mult).then_inc(f_wf, 1)

        def weights_low(pool, j):
            pool.wait_ge(f_wh, j + 1)
            nc.gpsimd.tensor_tensor(fwl[:, j % 2, :], wf, fwh[:, j % 2, :].bitcast(F32), ALU.subtract).then_inc(f_wl, 1)

        def values_and_maxima(pool):
            nc.gpsimd.memset(VS, 0.0).then_inc(e_vs, 1)
            nc.gpsimd.memset(mT.bitcast(F32), 0.0).then_inc(e_vs, 1)
            pool.wait_ge(e_vs, 2)
            nc.gpsimd.memset(VS[:, :, :, HD2:HD2 + 1], 1.0).then_inc(e_vs, 1)
            nc.gpsimd.tensor_copy(VS[:, :, :, 0:HD2], ctx_s[:].rearrange("p i (v d) -> p i v d", d=HD2)).then_inc(e_vs, 1)

        layer_norm("E", split=True, beside=values_and_maxima)
        e_t, e_tr, e_s, e_sr, e_nm, e_mt, e_pv, e_os, e_tp, e_on = (
            sem(f"e_{n}") for n in ("t", "tr", "s", "sr", "nm", "mt", "pv", "os", "tp", "on"))
        e_oread, e_x = sem("e_oread"), sem("e_x")
        with nc.Block() as block:
            NE = B * KVH
            turns_of = [4]
            for b in range(B):
                turns_of.append(turns_of[-1] + 1 + 4 + (4 if b + 1 < B else 0) + 4 * KVH)

            def turn_q1(b, j):
                return j if b == 0 else turns_of[b - 1] + j

            def turn_mt(b):
                return turns_of[b] + (4 if b + 1 < B else 0)

            def turn_q2(b, j):
                return turn_mt(b) + 1 + j

            def turn_st(b, kv, g):
                return turns_of[b + 1] - 4 * KVH + 4 * kv + g

            def t_bank(k):
                return PS[:, 3 + k % 3, :]

            @block.gpsimd
            def _(pool):
                clear_keys(pool, KZ[1], 1 + GRP)

            @block.sync
            def _(sp):
                for b in range(1, B):
                    for half in range(2):
                        if b == 1:
                            sp.wait_ge(z_clear, 10)
                        else:
                            sp.wait_ge(e_t, turn_st(b - 2, 4 * half + 3, GRP - 1) + 1)
                        sp.wait_ge(ld_keys[half], 16 * 12 * b)
                        load_keys(sp, b, half)
                        if b == 1 and half == 1:
                            sp.dma_start(f_codes, ins["codes"]).then_inc(ld_f, 16)
                sp.wait_ge(e_t, turn_st(B - 2, KVH - 1, GRP - 1) + 1)
                for blk in range(8):
                    sp.dma_start(f_scale[16 * blk:16 * blk + 16, :, :],
                                 ins["scales"][blk:blk + 1, :].to_broadcast([16, 6144]).rearrange("p (j w) -> p j w", j=8)).then_inc(ld_scale, 16)

            @block.tensor
            def _(pe):
                def take(k):
                    if k >= 3:
                        pe.wait_ge(e_tr, k - 2)
                    return t_bank(k)

                def stack1(b):
                    tok = slice(b * 256, (b + 1) * 256)
                    for j in range(4):
                        bank = take(turn_q1(b, j))
                        for kv in (2 * j, 2 * j + 1):
                            o = bank[:, (kv % 2) * 256:(kv % 2) * 256 + 256]
                            nc.tensor.matmul(o, sel[:, kv % 4, :], hTh[:, kv // 4, tok], start=True, stop=False)
                            last = nc.tensor.matmul(o, sel[:, 4 + kv % 4, :], hTl[:, kv // 4, tok], start=False, stop=True)
                        last.then_inc(e_t, 1)

                def stack2(b):
                    tok = slice(b * 256, (b + 1) * 256)
                    pe.wait_ge(e_tr, turn_mt(b) + 1)
                    for j in range(4):
                        bank = take(turn_q2(b, j))
                        for kv in (2 * j, 2 * j + 1):
                            o = bank[:, (kv % 2) * 256:(kv % 2) * 256 + 256]
                            nc.tensor.matmul(o, sel[:, kv % 4, :], hTh[:, kv // 4, tok], start=True, stop=False)
                            nc.tensor.matmul(o, sel[:, 4 + kv % 4, :], hTl[:, kv // 4, tok], start=False, stop=False)
                            last = nc.tensor.matmul(o, sel[:, 8 + kv, :], mT, start=False, stop=True)
                        last.then_inc(e_t, 1)

                def scores(b, kv, part):
                    if kv == 0 and part == 0:
                        pe.wait_ge(e_tr, turn_q1(b, 3) + 1)
                    if part == 0 and kv % 4 == 0:
                        pe.wait_ge(ld_keys[kv // 4], 16 * 12 * (b + 1))
                    k = (b * KVH + kv) * 4 + part
                    if k >= 3:
                        pe.wait_ge(e_sr, k - 2)
                    tt, pair = part // 2, part % 2
                    nc.tensor.matmul(PS[:, k % 3, :], QT1[:, kv, tt * 128:(tt + 1) * 128],
                                     KZ[b % 2][:, kv, 2 * pair:2 * pair + 2, :].rearrange("p g t -> p (g t)"),
                                     start=True, stop=True).then_inc(e_s, 1)

                def maxima(b):
                    pe.wait_ge(e_sr, (b + 1) * KVH * GRP)
                    bank = take(turn_mt(b))
                    for tt in range(2):
                        last = nc.tensor.transpose(bank[0:32, tt * 128:(tt + 1) * 128], mx[:, b % 2, tt * 32:(tt + 1) * 32], ident)
                    last.then_inc(e_t, 1)

                def scores_t(b, kv, g):
                    if kv == 0 and g == 0:
                        pe.wait_ge(e_tr, turn_q2(b, 3) + 1)
                    bank = take(turn_st(b, kv, g))
                    for st in range(2):
                        last = nc.tensor.matmul(bank[:, st * 256:(st + 1) * 256], KZ[b % 2][:, kv, g, st * 128:(st + 1) * 128],
                                                QT2[:, kv, :], start=True, stop=True)
                    last.then_inc(e_t, 1)

                def mix(m):
                    b, kv = m // KVH, m % KVH
                    for g in range(GRP):
                        pe.wait_ge(e_tr, turn_st(b, kv, g) + 1)
                        if m >= 1 and g == 0:
                            pe.wait_ge(e_os, m)
                        for st in range(2):
                            last = nc.tensor.matmul(PS[32 * g:32 * g + 32, 6, 0:256], VS[:, 2 * b + st, kv, :],
                                                    PT[:, m % 3, g, st * 256:(st + 1) * 256], start=st == 0, stop=st == 1,
                                                    tile_position=(0, 32 * g))
                        if g == GRP - 1:
                            last.then_inc(e_pv, 1)

                def turn(m):
                    pe.wait_ge(e_os, m + 1)
                    if m % 2 == 0 and m:
                        pe.wait_ge(e_oread, m // 2)
                    for tt in range(2):
                        o = (m % 2) * 256 + tt * 128
                        last = nc.tensor.transpose(PS[:, 7, o:o + 128], OS[:, m % 2, tt * 128:(tt + 1) * 128], ident)
                    last.then_inc(e_tp, 1)

                pe.wait_ge(e_sel, 1)
                pe.wait_ge(e_vs, 4)
                stack1(0)
                for kv in range(KVH):
                    for g in range(GRP):
                        scores(0, kv, g)
                for b in range(B):
                    if b + 1 < B:
                        stack1(b + 1)
                    maxima(b)
                    if b:
                        mix(b * KVH - 2)
                        turn(b * KVH - 3)
                    stack2(b)
                    if b:
                        mix(b * KVH - 1)
                        turn(b * KVH - 2)
                    for kv in range(KVH):
                        m = b * KVH + kv
                        for g in range(GRP):
                            scores_t(b, kv, g)
                            if b + 1 < B:
                                scores(b + 1, kv, g)
                        if kv >= 2:
                            mix(m - 2)
                        if kv >= 3 or (b and kv == 2):
                            turn(m - 3)
                mix(NE - 2)
                turn(NE - 3)
                mix(NE - 1)
                turn(NE - 2)
                turn(NE - 1)

            @block.scalar
            def _(act):
                def stacked(dst, k, j):
                    act.wait_ge(e_t, k + 1)
                    nc.scalar.copy(dst[:, 2 * j:2 * j + 2, :], v3(t_bank(k), 2, 256)).then_inc(e_tr, 1)

                def outputs(m):
                    act.wait_ge(e_pv, m + 1)
                    if m >= 2:
                        act.wait_ge(e_tp, m - 1)
                    nc.scalar.copy(OS[:, m % 2, :], PS[:, 6, 0:256]).then_inc(e_os, 1)

                for j in range(4):
                    stacked(QT1, turn_q1(0, j), j)
                for b in range(B):
                    if b + 1 < B:
                        for j in range(4):
                            stacked(QT1, turn_q1(b + 1, j), j)
                    act.wait_ge(e_t, turn_mt(b) + 1)
                    nc.scalar.activation(mT[0:32, :], t_bank(turn_mt(b))[0:32, 0:256], ACT.Copy, scale=-1.0).then_inc(e_tr, 1)
                    if b:
                        outputs(b * KVH - 3)
                        outputs(b * KVH - 2)
                    for j in range(4):
                        stacked(QT2, turn_q2(b, j), j)
                    if b:
                        outputs(b * KVH - 1)
                    for kv in range(KVH):
                        m = b * KVH + kv
                        if kv >= 3:
                            outputs(m - 3)
                        if m >= 3:
                            act.wait_ge(e_pv, m - 2)
                        for g in range(GRP):
                            k = turn_st(b, kv, g)
                            act.wait_ge(e_t, k + 1)
                            nc.scalar.activation(PT[:, m % 3, g, :], t_bank(k), ACT.Exp, scale=SCALE2).then_inc(e_tr, 1)
                outputs(NE - 3)
                outputs(NE - 2)
                outputs(NE - 1)

            @block.vector
            def _(dve):
                L = lambda inst: link(dve, "v", s_vec, inst)

                def maxima(b, kv, parts=range(4)):
                    for part in parts:
                        k = (b * KVH + kv) * 4 + part
                        dve.wait_ge(e_s, k + 1)
                        if kv == 0 and part == 0 and b >= 2:
                            dve.wait_ge(e_t, turn_mt(b - 2) + 1)
                        h0 = 32 * (part // 2) + GRP * kv + 2 * (part % 2)
                        h = mx[:, b % 2, h0:h0 + 2]
                        nc.vector.tensor_reduce(h, v3(PS[:, k % 3, :], 2, 256), AX.X, ALU.max).then_inc(e_sr, 1)

                def finish(j):
                    m = 2 * j
                    b, kv = m // KVH, m % KVH
                    dve.wait_ge(e_tp, m + 2)
                    o = PS[:, 7, :].rearrange("p (a t g c) -> p a t g c", a=2, t=2, g=GRP)
                    for a in range(2):
                        r = rden[:, a, 0:8].rearrange("p (t g o) -> p t g o", t=2, o=1)
                        L(nc.vector.reciprocal(r, o[:, a, :, :, HD2:HD2 + 1]))
                        n4 = on[:, a * 64:(a + 1) * 64].rearrange("p (t g d) -> p t g d", t=2, g=GRP)
                        inst = nc.vector.tensor_tensor(n4, o[:, a, :, :, 0:HD2], r.to_broadcast([P, 2, GRP, HD2]), ALU.mult)
                        if a == 1:
                            inst.then_inc(e_oread, 1)
                            dve.wait_ge(e_oread, j + 1)
                        else:
                            L(inst)
                    for a in range(2):
                        c0 = 32 * (kv + a)
                        xs = x[:, 2 * b:2 * b + 2, c0:c0 + 32]
                        nc.vector.tensor_tensor(xs, xs, v3(on[:, a * 64:(a + 1) * 64], 2, 32), ALU.add).then_inc(e_x, 1)
                    dve.wait_ge(e_x, 2 * j + 2)

                for kv in range(KVH):
                    maxima(0, kv)
                for b in range(B):
                    if b:
                        finish(b * KVH // 2 - 2)
                    if b == B - 1:
                        dve.wait_ge(ld_f, 16)
                        dve.wait_ge(e_t, turn_st(B - 2, KVH - 1, GRP - 1) + 1)
                        dequant(dve, 0)
                    for kv in range(KVH):
                        m = b * KVH + kv
                        if b + 1 < B:
                            maxima(b + 1, kv, (0, 1))
                        if kv == 5 or kv == 7 or (b and kv == 3):
                            finish((m - 5) // 2)
                        if b + 1 < B:
                            maxima(b + 1, kv, (2, 3))
                finish(NE // 2 - 2)
                finish(NE // 2 - 1)


        def first_scaled(pool):
            pool.wait_ge(f_val, 1)
            pool.wait_ge(ld_scale, 16 * 8)
            scaled(pool, 0)

        def first_high(act):
            act.wait_ge(f_wf, 1)
            nc.scalar.copy(fwh[:, 0, :], wf).then_inc(f_wh, 1)

        layer_norm("F", parity=True, split=True, before=first_scaled, beside=lambda pool: weights_low(pool, 0), scalar_beside=first_high)
        f_g, f_gel, f_hid, f_hh, f_hl, f_dn, f_add, f_out = (sem(f"f_{n}") for n in ("g", "gel", "hid", "hh", "hl", "dn", "add", "out"))
        with nc.Block() as block:
            funits = [(n, c) for n in range(NB) for c in range(2)]
            NF = len(funits)

            @block.gpsimd
            def _(pool):
                for j in range(1, NSTEP):
                    pool.wait_ge(f_val, j + 1)
                    pool.wait_ge(f_wh, j)
                    pool.wait_ge(f_wl, j)
                    scaled(pool, j)
                    weights_low(pool, j)

            @block.tensor
            def _(pe):
                def w(part, n, which, k):
                    o = k * 768 + which * 256 + (n % 2) * 128
                    return part[:, (n // 2) % 2, o:o + 128]

                def up(u):
                    n, c = funits[u]
                    pe.wait_ge(f_wl, n // 2 + 1)
                    if u >= 2:
                        pe.wait_ge(f_hid, u - 1)
                    tok = slice(c * 512, (c + 1) * 512)
                    for j in range(2):
                        for k in range(KT):
                            last = mm3(PS[:, 2 * (u % 2) + j, :], (w(fwh, n, j, k), w(fwl, n, j, k)), (hTh[:, k, tok], hTl[:, k, tok]),
                                       k == 0, k == 1)
                        last.then_inc(f_g, 1)

                def down(u):
                    n, c = funits[u]
                    pe.wait_ge(f_hl, u + 1)
                    o = (n % 2) * 768 + 512
                    for i in range(4):
                        t = slice(i * 128, (i + 1) * 128)
                        last = mm3(PS[:, 4 + 2 * c + i // 2, (i % 2) * 256:(i % 2) * 256 + 256], (hh[:, u % 3, t], hl[:, u % 3, t]),
                                   (fwh[:, (n // 2) % 2, o:o + 256], fwl[:, (n // 2) % 2, o:o + 256]),
                                   n == 0 and i % 2 == 0, n == NB - 1, skip_group_check=True)
                    last.then_inc(f_dn, 1)

                for u in range(NF + 2):
                    if u < NF:
                        up(u)
                    if u >= 2:
                        down(u - 2)

            @block.scalar
            def _(act):
                def split(j):
                    act.wait_ge(f_wf, j + 1)
                    if j >= 2:
                        act.wait_ge(f_dn, 4 * (j - 1))
                    nc.scalar.copy(fwh[:, j % 2, :], wf).then_inc(f_wh, 1)

                def high(u):
                    act.wait_ge(f_hid, u + 1)
                    if u >= 3:
                        act.wait_ge(f_dn, u - 2)
                    nc.scalar.copy(hh[:, u % 3, :], hf[:, u % 2, :]).then_inc(f_hh, 1)

                split(1)
                for u in range(NF):
                    act.wait_ge(f_g, 2 * u + 1)
                    if u >= 2:
                        act.wait_ge(f_hid, u - 1)
                    nc.scalar.activation(gel[:, u % 2, :], PS[:, 2 * (u % 2), :], ACT.Gelu_apprx_tanh).then_inc(f_gel, 1)
                    if u >= 1:
                        high(u - 1)
                    if u % 4 == 1 and 1 <= u // 4 < NSTEP - 1:
                        split(u // 4 + 1)
                high(NF - 1)

            @block.vector
            def _(dve):
                def product(u):
                    dve.wait_ge(f_gel, u + 1)
                    dve.wait_ge(f_g, 2 * u + 2)
                    if u >= 2:
                        dve.wait_ge(f_hl, u - 1)
                    nc.vector.tensor_tensor(hf[:, u % 2, :], PS[:, 2 * (u % 2) + 1, :], gel[:, u % 2, :], ALU.mult).then_inc(f_hid, 1)

                def low(u):
                    dve.wait_ge(f_hh, u + 1)
                    if u >= 3:
                        dve.wait_ge(f_dn, u - 2)
                    nc.vector.tensor_tensor(hl[:, u % 3, :], hf[:, u % 2, :], hh[:, u % 3, :].bitcast(F32), ALU.subtract).then_inc(f_hl, 1)

                dequant(dve, 1)
                for u in range(NF):
                    product(u)
                    if u >= 1:
                        low(u - 1)
                    if u % 4 == 0 and u // 4 + 2 < NSTEP:
                        dequant(dve, u // 4 + 2)
                low(NF - 1)
                for c in range(2):
                    dve.wait_ge(f_dn, NF - 1 + c)
                    for j in (2 * c, 2 * c + 1):
                        nc.vector.tensor_tensor(x[:, 2 * j:2 * j + 2, :], x[:, 2 * j:2 * j + 2, :], v3(PS[:, 4 + j, :], 2, 256),
                                                ALU.add).then_inc(f_add, 1)

            @block.sync
            def _(sp):
                for c in range(2):
                    sp.wait_ge(f_add, 2 * c + 2)
                    sp.dma_start(out[:, 4 * c:4 * c + 4, :], x[:, 4 * c:4 * c + 4, :]).then_inc(f_out, 16)
                sp.wait_ge(f_out, 32)


def shape_constants():
    i = np.arange(P)
    causal = (i[:, None] <= i[None, :]).astype(np.float32)
    same = (i[:, None] // CHUNK == i[None, :] // CHUNK).astype(np.float32)
    mask_ret = np.concatenate([causal, np.ones((P, P), np.float32), causal], 1)
    consts = np.concatenate([np.eye(P, dtype=np.float32), np.ones((P, P), np.float32), mask_ret] + [causal * same] * 4, 1)
    half = HD0 // 2
    xscale = (np.arange(0, HD0, 2, dtype=np.float32) + np.float32(0.4 * HD0)) / np.float32(1.4 * HD0)
    pos = np.arange(S, dtype=np.float32)
    scale = xscale[None, :].astype(np.float64) ** (pos[:, None] / 64).astype(np.float64)
    inv_freq = (1.0 / 10000.0 ** (np.arange(half) / half)).astype(np.float32)
    angle = (pos[:, None] * inv_freq[None, :]).astype(np.float64)
    gammas = (1.0 - np.exp(np.linspace(np.log(1.0 / 32), np.log(1.0 / 64), NH0))).astype(np.float32).astype(np.float64)
    tab = np.zeros((2, P, 2, 2, 2, NH0, half))
    for n in range(NH0):
        grow = gammas[n] ** pos.astype(np.float64)[:, None]
        for j, size in enumerate((scale * grow, 1.0 / (scale * grow))):
            for eo, sign in enumerate((-1.0, 1.0)):
                tab[:, :, 0, j, eo, n, :] = (np.cos(angle) * size).reshape(2, P, half)
                tab[:, :, 1, j, eo, n, :] = (sign * np.sin(angle) * size).reshape(2, P, half)
    tab = tab.transpose(1, 0, 2, 3, 4, 5, 6).reshape(P, 2, 1024)
    sel = np.zeros((P, 16, P), np.float32)
    for q in range(4):
        for g in range(GRP):
            for d in range(HD2):
                row = 32 * q + HD2 * g + d
                sel[row, q, 32 * g + d] = sel[row, q, 32 * g + 16 + d] = 1.0
                sel[row, 4 + q, 32 * g + 8 + d] = 1.0
    for kv in range(KVH):
        for g in range(GRP):
            sel[GRP * kv + g, 8 + kv, 32 * g + 24] = 1.0
    return consts, tab.astype(np.float32), sel.reshape(P, 16 * P)


def kernel(**inputs):
    import concourse.bacc as _bacc
    from concourse.bass_utils import run_bass_kernel_spmd as _run

    a = {k: np.asarray(v) for k, v in inputs.items()}
    kp = lambda w: w.reshape(KT, P, -1).transpose(1, 0, 2)
    heads = lambda w: w.transpose(1, 0, 2)
    even_odd = lambda w: [heads(w)[:, :, j::2].reshape(H, P) for j in range(2)]
    consts, rot_tab, sel = shape_constants()
    ctx = a["ctx_512"]
    codes = lambda p: p.T.reshape(P, 8, P, 2).transpose(0, 1, 3, 2).reshape(P, 8, 256)
    scl = lambda s: s.T.reshape(8, 8, P, 2).transpose(0, 1, 3, 2).reshape(8, 8, 256)
    experts = lambda w: w.reshape(E0, KT, P, 256).transpose(2, 0, 1, 3).reshape(P, E0, 512)
    by_head = lambda w: w.T.reshape(KT, P, NH1, P).transpose(1, 2, 0, 3).reshape(P, NH1, 256)
    arrays = {
        "x": a["x"].reshape(NT, P, H).transpose(1, 0, 2),
        "consts": consts, "rot_tab": rot_tab, "sel": sel,
        "wqkvg": kp(np.concatenate(even_odd(a["L0_attn_W_Q"]) + even_odd(a["L0_attn_W_K"])
                                   + [heads(a["L0_attn_W_V"]).reshape(H, 256), a["L0_attn_W_G"]], 1)),
        "wo0": kp(a["L0_attn_W_O"]),
        "gn_w": a["L0_attn_gn_weight"], "gn_b": a["L0_attn_gn_bias"],
        "ctxT": ctx.reshape(T, CD).T, "ctx_s": ctx.reshape(NT, P, CD).transpose(1, 0, 2),
        "wkT": a["L0_xattn_W_k"].T, "bk": a["L0_xattn_b_k"], "xg": a["L0_xattn_ln_gamma"], "xb": a["L0_xattn_ln_beta"],
        "wr": kp(a["L0_ffn_Wr"]), "temp": a["L0_ffn_temperature"],
        "wexp": np.stack([experts(a[f"L0_ffn_{n}"]) for n in ("Wg", "Wu", "Wd")], 2).reshape(P, E0, 1536),
        "w1": np.concatenate([by_head(a[f"L1_attn_{n}_w"]) for n in ("q", "k", "v", "og")]
                             + [a["L1_attn_o_w"].T.reshape(NB, P, H).transpose(1, 0, 2)], 2),
        "qkvb": np.stack([a[f"L1_attn_{n}_b"].reshape(NH1, P) for n in "qkv"], 1).reshape(-1),
        "bw1": kp(a["L1_attn_b_w"].T), "bb1": a["L1_attn_b_b"], "ob1": a["L1_attn_o_b"],
        "codes": np.stack([codes(a["L1_ffn_gate_W_packed"]), codes(a["L1_ffn_up_W_packed"]),
                           a["L1_ffn_down_W_packed"].T.reshape(8, P, H).transpose(1, 0, 2)], 2).reshape(P, 8, 768),
        "scales": np.stack([scl(a["L1_ffn_gate_scales"]), scl(a["L1_ffn_up_scales"]),
                            a["L1_ffn_down_scales"].T.reshape(8, 8, H).transpose(1, 0, 2)], 2).reshape(8, 8 * 768),
    }
    nc = _bacc.Bacc("TRN2", target_bir_lowering=False, num_devices=1)
    args, feed = {}, {}
    for name, arr in arrays.items():
        arr = np.ascontiguousarray(arr)
        feed[f"in_{name}"] = arr
        args[name] = nc.dram_tensor(f"in_{name}", arr.shape, mybir.dt.from_np(arr.dtype), kind="ExternalInput").ap()
    out = nc.dram_tensor("out_x", (P, NT, H), F32, kind="ExternalOutput").ap()
    build_decoder(nc, args, out)
    r = _run(nc, [feed], core_ids=[0])
    return r.results[0]["out_x"].transpose(1, 0, 2).reshape(B, S, H)
```
